# Optimizing a Trainium2 kernel written in Bass

```python
import numpy as np
import jax
import jax.numpy as jnp

def _softmax(x, axis=-1):
    return jax.nn.softmax(x, axis=axis)

def _gelu(x):
    return jax.nn.gelu(x, approximate=True)

def _silu(x):
    return jax.nn.silu(x)

def _sigmoid(x):
    return jax.nn.sigmoid(x)

def _layernorm(x, axis=-1, eps=1e-05):
    m = jnp.mean(x, axis=axis, keepdims=True)
    v = jnp.var(x, axis=axis, keepdims=True)
    return (x - m) / jnp.sqrt(v + eps)

def _scatter_add(tgt, idx, src, axis=0):
    return tgt.at[idx].add(src)

def _segment_sum(src, seg, n):
    return jax.ops.segment_sum(src, seg, n)
kernel_name = 'mk_gps_d2_gnn_r32_cb5450'

def setup_inputs(seed: int=0):
    np.random.seed(seed)
    _w = jnp.asarray

    def _rec_inputs():
        import jax
        import jax.numpy as jnp
        _gk = jax.random.key(seed)
        x = -5.39e-05 + 0.9998 * jax.random.normal(jax.random.fold_in(_gk, 1), (3125, 256), jnp.float32)
        _s = jax.random.randint(jax.random.fold_in(_gk, 2), (25000,), 0, 3125, jnp.int32)
        _d = jax.random.randint(jax.random.fold_in(_gk, 3), (25000,), 0, 3125, jnp.int32)
        _loop = jnp.arange(3125, dtype=jnp.int32)
        src = jnp.concatenate([_s, _d, _loop])
        dst = jnp.concatenate([_d, _s, _loop])
        _o = jnp.argsort(dst, stable=True)
        src = src[_o]
        dst = dst[_o]
        edge_attr_4 = 0.000126197 + 0.999763 * jax.random.normal(jax.random.fold_in(_gk, 12), (53125, 4), jnp.float32)
        edge_attr_8 = jax.random.uniform(jax.random.fold_in(_gk, 13), (53125, 8), jnp.float32, 0.0, 1)
        edge_weight = jax.random.uniform(jax.random.fold_in(_gk, 15), (53125,), jnp.float32, 0.0, 1)
        return (x, src, dst, edge_attr_4, edge_attr_8, edge_weight)
    x, src, dst, edge_attr_4, edge_attr_8, edge_weight = _rec_inputs()

    def _L0_gnn_setup():
        import jax, jax.numpy as jnp
        import numpy as np
        N_NODES = 3125
        N_EDGES = 100000
        N_FEAT = 256
        N_FILT = 256
        key = jax.random.key(seed)
        k1, k2, k3, k4, k5 = jax.random.split(key, 5)
        std = (2.0 / (N_FEAT + N_FILT)) ** 0.5
        filters = jax.random.normal(k1, (N_FEAT, N_FILT), dtype=jnp.float32) * std
        x = jax.random.normal(k2, (N_NODES, N_FEAT), dtype=jnp.float32)
        edge_row = jax.random.randint(k3, (N_EDGES,), 0, N_NODES, dtype=jnp.int32)
        edge_col = jax.random.randint(k4, (N_EDGES,), 0, N_NODES, dtype=jnp.int32)
        edge_weight = jax.random.uniform(k5, (N_EDGES,), dtype=jnp.float32)
        return {'x': x, 'filters': filters, 'edge_row': edge_row, 'edge_col': edge_col, 'edge_weight': edge_weight}
    _L0_gnn_all = _L0_gnn_setup()
    _L0_gnn_in = {k: v for k, v in _L0_gnn_all.items() if k in ('filters',)}
    del _L0_gnn_all

    def _L0_mix_setup():
        import jax, jax.numpy as jnp
        import numpy as np
        HEADS = 8
        EPS = 1e-05

        def _ln(t, w, b, headc):
            m = jnp.mean(t, axis=-1, keepdims=True)
            d = t - m
            std = jnp.sqrt(jnp.sum(d * d, axis=-1, keepdims=True) / (headc - 1))
            return w * (d / (std + EPS)) + b
        key = jax.random.key(seed)
        B, N, C = (32, 128, 256)
        headc = C // HEADS
        x = jax.random.normal(key, (B, N, C), dtype=jnp.float32)
        return {'x': x, 'kln_weight': jnp.ones((HEADS, 1, headc), dtype=jnp.float32), 'kln_bias': jnp.zeros((HEADS, 1, headc), dtype=jnp.float32), 'vln_weight': jnp.ones((HEADS, 1, headc), dtype=jnp.float32), 'vln_bias': jnp.zeros((HEADS, 1, headc), dtype=jnp.float32)}
    _L0_mix_all = _L0_mix_setup()
    _L0_mix_in = {k: v for k, v in _L0_mix_all.items() if k in ('kln_weight', 'kln_bias', 'vln_weight', 'vln_bias')}
    del _L0_mix_all

    def _L0_ffn_setup():
        import jax, jax.numpy as jnp
        import numpy as np
        DIM = 256
        H = 8
        D = 64
        G = 64
        INNER = H * D
        SCALE = D ** (-0.5)
        key = jax.random.key(seed)
        ks = jax.random.split(key, 12)
        B, N = (4, 512)
        x = jax.random.normal(ks[0], (B, N, DIM), dtype=jnp.float32)
        s = lambda fan_in: 1.0 / np.sqrt(fan_in)
        W_fx = jax.random.normal(ks[1], (DIM, INNER), dtype=jnp.float32) * s(DIM)
        b_fx = jnp.zeros((INNER,), dtype=jnp.float32)
        W_x = jax.random.normal(ks[2], (DIM, INNER), dtype=jnp.float32) * s(DIM)
        b_x = jnp.zeros((INNER,), dtype=jnp.float32)
        A = jax.random.normal(ks[3], (G, D), dtype=jnp.float32)
        Q, _ = jnp.linalg.qr(A.T)
        W_slice = Q[:, :G].astype(jnp.float32)
        b_slice = jnp.zeros((G,), dtype=jnp.float32)
        W_q = jax.random.normal(ks[4], (D, D), dtype=jnp.float32) * s(D)
        W_k = jax.random.normal(ks[5], (D, D), dtype=jnp.float32) * s(D)
        W_v = jax.random.normal(ks[6], (D, D), dtype=jnp.float32) * s(D)
        W_out = jax.random.normal(ks[7], (INNER, DIM), dtype=jnp.float32) * s(INNER)
        b_out = jnp.zeros((DIM,), dtype=jnp.float32)
        temperature = jnp.ones((1, H, 1, 1), dtype=jnp.float32) * 0.5
        return {'x': x, 'W_fx': W_fx, 'b_fx': b_fx, 'W_x': W_x, 'b_x': b_x, 'W_slice': W_slice, 'b_slice': b_slice, 'W_q': W_q, 'W_k': W_k, 'W_v': W_v, 'W_out': W_out, 'b_out': b_out, 'temperature': temperature}
    _L0_ffn_all = _L0_ffn_setup()
    _L0_ffn_in = {k: v for k, v in _L0_ffn_all.items() if k in ('W_fx', 'b_fx', 'W_x', 'b_x', 'W_slice', 'b_slice', 'W_q', 'W_k', 'W_v', 'W_out', 'b_out', 'temperature')}
    del _L0_ffn_all

    def _L1_gnn_setup():
        import jax, jax.numpy as jnp
        import numpy as np
        N_NODES = 625
        N_EDGES = 10000
        MUL = 64
        NUM_BASIS = 8
        INV_SQRT3 = 0.5773502691896258
        EPS = 1e-05
        key = jax.random.key(seed)
        k = jax.random.split(key, 16)
        return {'node_hiddens': jax.random.normal(k[0], (N_NODES, 4 * MUL), dtype=jnp.float32), 'edge_attr': jax.random.uniform(k[1], (N_EDGES, NUM_BASIS), dtype=jnp.float32), 'edge_sh': jax.random.normal(k[2], (N_EDGES, 4), dtype=jnp.float32), 'w1_s': jax.random.normal(k[3], (MUL, MUL), dtype=jnp.float32), 'w1_v': jax.random.normal(k[4], (MUL, MUL), dtype=jnp.float32), 'wsc_s': jax.random.normal(k[5], (MUL, MUL), dtype=jnp.float32), 'wsc_v': jax.random.normal(k[6], (MUL, MUL), dtype=jnp.float32), 'w2_s': jax.random.normal(k[7], (2 * MUL, MUL), dtype=jnp.float32), 'w2_v': jax.random.normal(k[8], (2 * MUL, MUL), dtype=jnp.float32), 'fc_w1': jax.random.normal(k[9], (NUM_BASIS, 64), dtype=jnp.float32), 'fc_w2': jax.random.normal(k[10], (64, 64), dtype=jnp.float32), 'fc_w3': jax.random.normal(k[11], (64, 4 * MUL), dtype=jnp.float32), 'g_s': jnp.ones((MUL,), dtype=jnp.float32), 'g_v': jnp.ones((MUL,), dtype=jnp.float32), 'edge_index': jax.random.randint(k[12], (2, N_EDGES), 0, N_NODES)}
    _L1_gnn_all = _L1_gnn_setup()
    _L1_gnn_in = {k: v for k, v in _L1_gnn_all.items() if k in ('w1_s', 'w1_v', 'wsc_s', 'wsc_v', 'w2_s', 'w2_v', 'fc_w1', 'fc_w2', 'fc_w3', 'g_s', 'g_v')}
    del _L1_gnn_all

    def _L1_mix_setup():
        import jax, jax.numpy as jnp
        import numpy as np
        A, Bc, Cc = (0.5, 1.0, 1.0)
        H = 8
        EPS = 1e-12

        def _normalize(t):
            n = jnp.linalg.norm(t, axis=-1, keepdims=True)
            return t / jnp.maximum(n, EPS)
        key = jax.random.key(seed)
        ks = jax.random.split(key, 5)
        B, N, C = (8, 64, 256)
        D = C // H
        x = jax.random.normal(ks[0], (B, N, C), dtype=jnp.float32)
        Wqkv = jax.random.normal(ks[1], (3 * H * D, C), dtype=jnp.float32) * 0.02
        bqkv = jnp.zeros((3 * H * D,), dtype=jnp.float32)
        Wproj = jax.random.normal(ks[2], (C, H * D), dtype=jnp.float32) * 0.02
        bproj = jnp.zeros((C,), dtype=jnp.float32)
        temperature = jnp.ones((1, H, 1, 1), dtype=jnp.float32)
        return {'x': x, 'Wqkv': Wqkv, 'bqkv': bqkv, 'Wproj': Wproj, 'bproj': bproj, 'temperature': temperature}
    _L1_mix_all = _L1_mix_setup()
    _L1_mix_in = {k: v for k, v in _L1_mix_all.items() if k in ('Wqkv', 'bqkv', 'Wproj', 'bproj', 'temperature')}
    del _L1_mix_all

    def _L1_ffn_setup():
        import jax, jax.numpy as jnp
        import numpy as np
        E = 8
        K = 2
        D = 256
        H = 512
        DOUT = 256
        EPS = 1e-05
        key = jax.random.key(seed)
        ks = jax.random.split(key, 9)
        s = 0.02
        return {'x': jax.random.normal(ks[0], (4, 256, D), jnp.float32), 'gamma': 1.0 + 0.05 * jax.random.normal(ks[1], (D,), jnp.float32), 'beta': 0.05 * jax.random.normal(ks[2], (D,), jnp.float32), 'Wr': 0.01 * jax.random.normal(ks[3], (D, E), jnp.float32), 'br': jnp.zeros((E,), jnp.float32), 'W1': s * jax.random.normal(ks[4], (E, D, H), jnp.float32), 'b1': s * jax.random.normal(ks[5], (E, H), jnp.float32), 'W2': s * jax.random.normal(ks[6], (E, H, DOUT), jnp.float32), 'b2': s * jax.random.normal(ks[7], (E, DOUT), jnp.float32)}
    _L1_ffn_all = _L1_ffn_setup()
    _L1_ffn_in = {k: v for k, v in _L1_ffn_all.items() if k in ('gamma', 'beta', 'Wr', 'br', 'W1', 'b1', 'W2', 'b2')}
    del _L1_ffn_all
    return {'x': x, 'src': src, 'dst': dst, 'edge_attr_4': edge_attr_4, 'edge_attr_8': edge_attr_8, 'edge_weight': edge_weight, 'L0_gnn_filters': _L0_gnn_in['filters'], 'L0_mix_kln_weight': _L0_mix_in['kln_weight'], 'L0_mix_kln_bias': _L0_mix_in['kln_bias'], 'L0_mix_vln_weight': _L0_mix_in['vln_weight'], 'L0_mix_vln_bias': _L0_mix_in['vln_bias'], 'L0_ffn_W_fx': _L0_ffn_in['W_fx'], 'L0_ffn_b_fx': _L0_ffn_in['b_fx'], 'L0_ffn_W_x': _L0_ffn_in['W_x'], 'L0_ffn_b_x': _L0_ffn_in['b_x'], 'L0_ffn_W_slice': _L0_ffn_in['W_slice'], 'L0_ffn_b_slice': _L0_ffn_in['b_slice'], 'L0_ffn_W_q': _L0_ffn_in['W_q'], 'L0_ffn_W_k': _L0_ffn_in['W_k'], 'L0_ffn_W_v': _L0_ffn_in['W_v'], 'L0_ffn_W_out': _L0_ffn_in['W_out'], 'L0_ffn_b_out': _L0_ffn_in['b_out'], 'L0_ffn_temperature': _L0_ffn_in['temperature'], 'L1_gnn_w1_s': _L1_gnn_in['w1_s'], 'L1_gnn_w1_v': _L1_gnn_in['w1_v'], 'L1_gnn_wsc_s': _L1_gnn_in['wsc_s'], 'L1_gnn_wsc_v': _L1_gnn_in['wsc_v'], 'L1_gnn_w2_s': _L1_gnn_in['w2_s'], 'L1_gnn_w2_v': _L1_gnn_in['w2_v'], 'L1_gnn_fc_w1': _L1_gnn_in['fc_w1'], 'L1_gnn_fc_w2': _L1_gnn_in['fc_w2'], 'L1_gnn_fc_w3': _L1_gnn_in['fc_w3'], 'L1_gnn_g_s': _L1_gnn_in['g_s'], 'L1_gnn_g_v': _L1_gnn_in['g_v'], 'L1_mix_Wqkv': _L1_mix_in['Wqkv'], 'L1_mix_bqkv': _L1_mix_in['bqkv'], 'L1_mix_Wproj': _L1_mix_in['Wproj'], 'L1_mix_bproj': _L1_mix_in['bproj'], 'L1_mix_temperature': _L1_mix_in['temperature'], 'L1_ffn_gamma': _L1_ffn_in['gamma'], 'L1_ffn_beta': _L1_ffn_in['beta'], 'L1_ffn_Wr': _L1_ffn_in['Wr'], 'L1_ffn_br': _L1_ffn_in['br'], 'L1_ffn_W1': _L1_ffn_in['W1'], 'L1_ffn_b1': _L1_ffn_in['b1'], 'L1_ffn_W2': _L1_ffn_in['W2'], 'L1_ffn_b2': _L1_ffn_in['b2']}

def reference(x, src, dst, edge_attr_4, edge_attr_8, edge_weight, L0_gnn_filters, L0_mix_kln_weight, L0_mix_kln_bias, L0_mix_vln_weight, L0_mix_vln_bias, L0_ffn_W_fx, L0_ffn_b_fx, L0_ffn_W_x, L0_ffn_b_x, L0_ffn_W_slice, L0_ffn_b_slice, L0_ffn_W_q, L0_ffn_W_k, L0_ffn_W_v, L0_ffn_W_out, L0_ffn_b_out, L0_ffn_temperature, L1_gnn_w1_s, L1_gnn_w1_v, L1_gnn_wsc_s, L1_gnn_wsc_v, L1_gnn_w2_s, L1_gnn_w2_v, L1_gnn_fc_w1, L1_gnn_fc_w2, L1_gnn_fc_w3, L1_gnn_g_s, L1_gnn_g_v, L1_mix_Wqkv, L1_mix_bqkv, L1_mix_Wproj, L1_mix_bproj, L1_mix_temperature, L1_ffn_gamma, L1_ffn_beta, L1_ffn_Wr, L1_ffn_br, L1_ffn_W1, L1_ffn_b1, L1_ffn_W2, L1_ffn_b2):
    import jax
    import jax.numpy as jnp

    def _L0_gnn_ref(x, filters, edge_row, edge_col, edge_weight):
        import jax, jax.numpy as jnp
        import numpy as np
        N_NODES = 3125
        N_EDGES = 100000
        N_FEAT = 256
        N_FILT = 256
        XF = jnp.matmul(x, filters)
        msgs = edge_weight[:, None] * XF[edge_col]
        out = jax.ops.segment_sum(msgs, edge_row, num_segments=N_NODES)
        return out

    def _L0_mix_ref(x, kln_weight, kln_bias, vln_weight, vln_bias):
        import jax, jax.numpy as jnp
        import numpy as np
        HEADS = 8
        EPS = 1e-05

        def _ln(t, w, b, headc):
            m = jnp.mean(t, axis=-1, keepdims=True)
            d = t - m
            std = jnp.sqrt(jnp.sum(d * d, axis=-1, keepdims=True) / (headc - 1))
            return w * (d / (std + EPS)) + b
        B, N, C = x.shape
        headc = C // HEADS
        qkv = x.reshape(B, N, HEADS, headc).transpose(0, 2, 1, 3)
        k = _ln(qkv, kln_weight, kln_bias, headc)
        v = _ln(qkv, vln_weight, vln_bias, headc)
        kv = jnp.einsum('bhnd,bhne->bhde', k, v) / N
        out = jnp.einsum('bhnd,bhde->bhne', qkv, kv)
        out = out.transpose(0, 2, 1, 3).reshape(B, N, C)
        return out + x

    def _L0_ffn_ref(x, W_fx, b_fx, W_x, b_x, W_slice, b_slice, W_q, W_k, W_v, W_out, b_out, temperature):
        import jax, jax.numpy as jnp
        import numpy as np
        DIM = 256
        H = 8
        D = 64
        G = 64
        INNER = H * D
        SCALE = D ** (-0.5)
        B, N, _ = x.shape
        fx_mid = (x @ W_fx + b_fx).reshape(B, N, H, D).transpose(0, 2, 1, 3)
        x_mid = (x @ W_x + b_x).reshape(B, N, H, D).transpose(0, 2, 1, 3)
        temp = jnp.clip(temperature, 0.1, 5.0)
        slice_weights = jax.nn.softmax((x_mid @ W_slice + b_slice) / temp, axis=-1)
        slice_norm = slice_weights.sum(axis=2)
        slice_token = jnp.einsum('bhnc,bhng->bhgc', fx_mid, slice_weights)
        slice_token = slice_token / (slice_norm[..., None] + 1e-05)
        q = slice_token @ W_q
        k = slice_token @ W_k
        v = slice_token @ W_v
        attn = jax.nn.softmax(jnp.einsum('bhgc,bhkc->bhgk', q, k) * SCALE, axis=-1)
        out_slice = jnp.einsum('bhgk,bhkc->bhgc', attn, v)
        out_x = jnp.einsum('bhgc,bhng->bhnc', out_slice, slice_weights)
        out_x = out_x.transpose(0, 2, 1, 3).reshape(B, N, INNER)
        return out_x @ W_out + b_out

    def _L1_gnn_ref(node_hiddens, edge_attr, edge_sh, w1_s, w1_v, wsc_s, wsc_v, w2_s, w2_v, fc_w1, fc_w2, fc_w3, g_s, g_v, edge_index):
        import jax, jax.numpy as jnp
        import numpy as np
        N_NODES = 625
        N_EDGES = 10000
        MUL = 64
        NUM_BASIS = 8
        INV_SQRT3 = 0.5773502691896258
        EPS = 1e-05
        N = node_hiddens.shape[0]
        xs = node_hiddens[:, :MUL]
        xv = node_hiddens[:, MUL:].reshape(N, MUL, 3)
        h = jax.nn.silu(edge_attr @ fc_w1 * (1.0 / np.sqrt(float(NUM_BASIS))))
        h = jax.nn.silu(h @ fc_w2 * (1.0 / np.sqrt(64.0)))
        w = h @ fc_w3 * (1.0 / np.sqrt(64.0))
        wA, wB, wC, wD = jnp.split(w, 4, axis=1)
        inv = 1.0 / np.sqrt(float(MUL))
        sc_s = xs @ wsc_s * inv
        sc_v = jnp.einsum('nud,uv->nvd', xv, wsc_v) * inv
        ys = xs @ w1_s * inv
        yv = jnp.einsum('nud,uv->nvd', xv, w1_v) * inv
        src = edge_index[0]
        dst = edge_index[1]
        es = ys[dst]
        ev = yv[dst]
        sh0 = edge_sh[:, :1]
        sh1 = edge_sh[:, 1:]
        m0a = wA * es * sh0
        m0b = wD * jnp.einsum('eud,ed->eu', ev, sh1) * INV_SQRT3
        m1a = wB[:, :, None] * es[:, :, None] * sh1[:, None, :]
        m1b = wC[:, :, None] * ev * sh0[:, :, None]
        mid_s = jnp.concatenate([m0a, m0b], axis=1)
        mid_v = jnp.concatenate([m1a, m1b], axis=1)
        ns = jax.ops.segment_sum(mid_s, src, num_segments=N)
        nv = jax.ops.segment_sum(mid_v, src, num_segments=N)
        deg = jax.ops.segment_sum(jnp.ones((src.shape[0],), node_hiddens.dtype), src, num_segments=N)
        dn = jax.lax.rsqrt(jnp.maximum(deg, 1.0))
        ns = ns * dn[:, None]
        nv = nv * dn[:, None, None]
        inv2 = 1.0 / np.sqrt(2.0 * MUL)
        os_ = ns @ w2_s * inv2 + sc_s
        ov = jnp.einsum('nud,uv->nvd', nv, w2_v) * inv2 + sc_v
        os_ = os_ * jax.lax.rsqrt(jnp.mean(os_ * os_, axis=1, keepdims=True) + EPS) * g_s
        rms_v = jax.lax.rsqrt(jnp.mean(ov * ov, axis=(1, 2))[:, None, None] + EPS)
        ov = ov * rms_v * g_v[None, :, None]
        return jnp.concatenate([os_, ov.reshape(N, 3 * MUL)], axis=1)

    def _L1_mix_ref(x, Wqkv, bqkv, Wproj, bproj, temperature):
        import jax, jax.numpy as jnp
        import numpy as np
        A, Bc, Cc = (0.5, 1.0, 1.0)
        H = 8
        EPS = 1e-12

        def _normalize(t):
            n = jnp.linalg.norm(t, axis=-1, keepdims=True)
            return t / jnp.maximum(n, EPS)
        B, N, C = x.shape
        D = C // H
        scale = float(D) ** 0.25
        qkv = (x @ Wqkv.T + bqkv).reshape(B, N, 3, H, D)
        qkv = jnp.transpose(qkv, (2, 0, 3, 1, 4))
        q, k, v = (qkv[0], qkv[1], qkv[2])
        q = q * scale
        v1 = jnp.concatenate([jnp.ones((B, H, N, 1), dtype=v.dtype), v], axis=-1)
        qn = _normalize(q) * (scale * temperature)
        kn = _normalize(k) * scale
        vN = v1 / N
        kv_mod = jnp.einsum('bhni,bhnj,bhne->bhije', kn, kn, vN)
        kv = jnp.einsum('bhnd,bhne->bhde', kn, vN)
        vsum = jnp.sum(vN, axis=-2)[:, :, None, :]
        y = A * jnp.einsum('bhni,bhnj,bhije->bhne', qn, qn, kv_mod) + scale ** 2 * Bc * jnp.einsum('bhnd,bhde->bhne', qn, kv) + scale ** 4 * Cc * vsum
        y_norm, y = (y[..., :1], y[..., 1:])
        y = y / y_norm
        out = jnp.transpose(y, (0, 2, 1, 3)).reshape(B, N, H * D)
        return out @ Wproj.T + bproj

    def _L1_ffn_ref(x, gamma, beta, Wr, br, W1, b1, W2, b2):
        import jax, jax.numpy as jnp
        import numpy as np
        E = 8
        K = 2
        D = 256
        H = 512
        DOUT = 256
        EPS = 1e-05
        mu = jnp.mean(x, axis=-1, keepdims=True)
        var = jnp.mean(jnp.square(x - mu), axis=-1, keepdims=True)
        xn = (x - mu) * jax.lax.rsqrt(var + EPS) * gamma + beta
        logits = jnp.einsum('bsd,de->bse', xn, Wr) + br
        top_vals, top_idx = jax.lax.top_k(logits, K)
        w = jax.nn.softmax(top_vals, axis=-1)
        w_full = jnp.einsum('bsk,bske->bse', w, jax.nn.one_hot(top_idx, E, dtype=w.dtype))
        y = jnp.zeros(x.shape[:-1] + (DOUT,), x.dtype)
        for e in range(E):
            h = jax.nn.gelu(jnp.einsum('bsd,dh->bsh', xn, W1[e]) + b1[e], approximate=False)
            y_e = jnp.einsum('bsh,hd->bsd', h, W2[e]) + b2[e]
            y = y + y_e * w_full[..., e, None]
        return y
    edge_index = jnp.stack([src, dst])
    xn = _layernorm(x, axis=-1)
    x = x + _L0_gnn_ref(xn, L0_gnn_filters, src, dst, edge_weight) + _L0_mix_ref(xn[None], L0_mix_kln_weight, L0_mix_kln_bias, L0_mix_vln_weight, L0_mix_vln_bias)[0]
    x = x + _L0_ffn_ref(_layernorm(x, axis=-1)[None], L0_ffn_W_fx, L0_ffn_b_fx, L0_ffn_W_x, L0_ffn_b_x, L0_ffn_W_slice, L0_ffn_b_slice, L0_ffn_W_q, L0_ffn_W_k, L0_ffn_W_v, L0_ffn_W_out, L0_ffn_b_out, L0_ffn_temperature)[0]
    xn = _layernorm(x, axis=-1)
    x = x + _L1_gnn_ref(xn, edge_attr_8, edge_attr_4, L1_gnn_w1_s, L1_gnn_w1_v, L1_gnn_wsc_s, L1_gnn_wsc_v, L1_gnn_w2_s, L1_gnn_w2_v, L1_gnn_fc_w1, L1_gnn_fc_w2, L1_gnn_fc_w3, L1_gnn_g_s, L1_gnn_g_v, edge_index) + _L1_mix_ref(xn[None], L1_mix_Wqkv, L1_mix_bqkv, L1_mix_Wproj, L1_mix_bproj, L1_mix_temperature)[0]
    x = x + _L1_ffn_ref(_layernorm(x, axis=-1)[None], L1_ffn_gamma, L1_ffn_beta, L1_ffn_Wr, L1_ffn_br, L1_ffn_W1, L1_ffn_b1, L1_ffn_W2, L1_ffn_b2)[0]
    return x

_drawn_inputs = setup_inputs


def setup_inputs(seed=0):
    import zlib

    import numpy as np

    out = dict(_drawn_inputs(seed))
    spreads = {'L0_mix_kln_weight': (1.0, 0.2),
     'L0_mix_kln_bias': (0.0, 0.609),
     'L0_mix_vln_weight': (1.0, 0.2),
     'L0_mix_vln_bias': (0.0, 0.604),
     'L0_ffn_b_fx': (0.0, 0.295),
     'L0_ffn_b_x': (0.0, 0.8),
     'L0_ffn_b_slice': (0.0, 0.8),
     'L0_ffn_b_out': (0.0, 0.293),
     'L0_ffn_temperature': (0.5, 0.6),
     'L1_gnn_g_s': (1.0, 0.6),
     'L1_gnn_g_v': (1.0, 0.2),
     'L1_mix_bqkv': (0.0, 0.8),
     'L1_mix_bproj': (0.0, 0.323),
     'L1_mix_temperature': (1.0, 0.6),
     'L1_ffn_br': (0.0, 0.782)}
    factors = {'L0_ffn_W_fx': 5.224,
     'L0_ffn_W_x': 8.0,
     'L0_ffn_W_slice': 8.0,
     'L0_ffn_W_q': 8.0,
     'L0_ffn_W_k': 8.0,
     'L1_mix_Wqkv': 8.0,
     'L1_mix_Wproj': 7.317,
     'L1_ffn_gamma': 8.0,
     'L1_ffn_beta': 8.0,
     'L1_ffn_Wr': 4.755,
     'L1_ffn_W1': 4.185,
     'L1_ffn_b1': 31.675,
     'L1_ffn_W2': 4.071,
     'L1_ffn_b2': 42.934}
    for name, (base, spread) in spreads.items():
        noise = np.random.default_rng([zlib.crc32(name.encode()), seed]).standard_normal(out[name].shape)
        drawn = base * np.exp(spread * noise) if base else spread * noise
        out[name] = jnp.asarray(drawn.astype(out[name].dtype))
    for name, factor in factors.items():
        out[name] = (out[name] * factor).astype(out[name].dtype)
    return out
```

```python
from contextlib import ExitStack

import numpy as np
import concourse.bass as bass
from concourse import mybir

F32 = mybir.dt.float32
BF16 = mybir.dt.bfloat16
I32 = mybir.dt.int32
ALU = mybir.AluOpType
ACT = mybir.ActivationFunctionType
X = mybir.AxisListType.X

P = 128
N, D, E = 3125, 256, 53125
NP_ = 125
NT = N // NP_
ET = -(-E // P)
EREST = E - (ET - 1) * P
ST = 440
assert (E + NT * (P - 1)) // P <= ST
RF = 16
R_W, R_SH, R_LOCAL, R_DST, R_ONE, R_ATTR = 0, 1, 5, 6, 7, 8
NONE = 32 * NP_
MAGIC = 1.5 * 2.0 ** 23
EPS = 1e-5
H0, HC = 8, 32
G = 64
MUL = 64
AG = 4 * MUL * 2


UN = 20
assert ST % UN == 0
HALF = UN // 2


class Chain:

    def __init__(self, engine, sem):
        self.engine, self.sem, self.base, self.n = engine, sem, 0, 0

    def __call__(self, ins):
        ins.then_inc(self.sem, 1)
        self.n += 1
        self.engine.wait_ge(self.sem, self.base + self.n)

    def loop(self):
        self.start = self.base + self.n

    def at(self, t, k):
        self.k, self.base, self.n = k, self.start + t * k, 0

    def end(self, tiles):
        assert self.n == self.k, (self.n, self.k)
        self.base, self.n = self.start + tiles * self.k, 0


UT = 4
assert NT % UT == 1


def each_node_tile(engine, body):
    for t in range(UT):
        body(t, t)
    with engine.Fori(1, NT // UT) as i:
        for u in range(UT):
            body(i * UT + u, u)
    body(NT - 1, 0)


def wait(engine, sem, value):
    if not (isinstance(value, int) and value <= 0):
        engine.wait_ge(sem, value)


def bcast(ap, shape):
    return ap.to_broadcast(shape)


class Core:

    def __init__(self, nc, ctx, args, out):
        self.nc, self.ctx, self.a, self.out, self.stage = nc, ctx, args, out, None
        self.held = []
        self.bank = [ctx.enter_context(nc.psum_tensor(f"bank{i}", [P, 512], F32)) for i in range(8)]
        self.x = self.sb("x", [NP_, NT, D])
        self.z = self.sb("z", [NP_, NT, D])
        self.mv = self.sb("mv", [NP_, NT, 2])
        self.rstd = self.sb("rstd", [NP_, NT])
        self.shift = self.sb("shift", [NP_, NT])
        self.ident = self.sb("ident", [P, P])
        self.ones = self.sb("ones", [P, P])
        self.ltri = self.sb("ltri", [P, P])
        self.iota = self.sb("iota", [P, NP_])
        self.bucket_of = self.sb("bucket_of", [1, ST], I32)
        self.kv = self.sb("kv", [P, 2, P])
        self.s_pass = self.sem("s_pass")
        self.s_scat = [self.sem(f"s_scat{h}") for h in range(2)]
        self.s_got = [self.sem(f"s_got{u}") for u in range(UN)]
        self.rec_dram = nc.dram_tensor("rec_sorted", (P * ST, RF), F32, kind="Internal").ap()
        self.z_dram = nc.dram_tensor("z_rows", (N, D), F32, kind="Internal").ap()
        self.y_dram = nc.dram_tensor("y_rows", (N, D), F32, kind="Internal").ap()

    def sb(self, name, shape, dt=F32, ctx=None):
        return (ctx or self.ctx).enter_context(self.nc.sbuf_tensor(name, shape, dt))

    def sem(self, name, ctx=None):
        if ctx is None and self.stage is not None:
            self.held.append(self.nc.alloc_semaphore(name=name))
            return self.held[-1]
        return self.ctx.enter_context(self.nc.semaphore(name))

    def clear_stages(self):
        self.nc.clear_and_free_semaphores(self.held)
        self.nc.all_engine_barrier()
        self.held = []


def rows(ap):
    return ap.rearrange("(t p) f -> p t f", p=NP_)


def row_to_all(ap, n, parts=P):
    return bass.AP(tensor=ap.tensor, offset=ap.offset, ap=[[0, parts], [1, n]])


def sort_and_first_norm(c):
    nc, a, bank = c.nc, c.a, c.bank
    with ExitStack() as ctx:
        c.stage = ctx

        def sb(name, shape, dt=F32):
            return c.sb(name, shape, dt, ctx)

        zeros = sb("zeros", [P, 8 * 220])
        src_i = sb("src_i", [P, ET], I32)
        dst_i = sb("dst_i", [P, ET], I32)
        srcf = sb("srcf", [P, ET])
        t0 = sb("t0", [P, ET])
        bucket = sb("bucket", [P, ET], BF16)
        rec_in = sb("rec_in", [P, ET, RF])
        inb = sb("inb", [P, NT, ET], BF16)
        ltri_b = sb("ltri_b", [P, P], BF16)
        pick = sb("pick", [P, 2 * NT - 1], BF16)
        scan = [sb(f"scan{i}", [NT, ET]) for i in range(2)]
        tot = sb("tot", [NT, ET])
        tiles = sb("tiles", [NT, 1])
        first = sb("first", [NT, 1])
        last = sb("last", [NT, 1])
        off = sb("off", [NT, ET])
        iota_tile = sb("iota_tile", [NT, ST])
        past = sb("past", [NT, ST])
        pos = sb("pos", [P, ET])
        part = sb("part", [P, ET])
        posi = sb("posi", [P, ET], I32)
        lo = sb("lo", [P, ET], I32)
        hi = sb("hi", [P, ET], I32)
        row = sb("row", [P, ET], I32)
        rec_ring = [sb(f"rec_ring{h}", [P, 8, RF]) for h in range(2)]
        row_ring = [sb(f"row_ring{h}", [P, 8], I32) for h in range(2)]
        stats = sb("stats", [NP_, NT, 6])
        varp = sb("varp", [NP_, NT])
        std = sb("std", [NP_, NT])
        hm = sb("hm", [NP_, 5 * H0])
        hs = sb("hs", [NP_, 5 * H0])
        hstd = sb("hstd", [NP_, 5 * H0])
        hr = sb("hr", [NP_, 5 * H0])
        zc = sb("zc", [NP_, 5, D])
        sq = sb("sq", [NP_, 5, D])
        zh = sb("zh", [NP_, 5, D])
        kw = sb("kw", [P, 2])
        kb = sb("kb", [P, 2])
        ks = sb("ks", [P, 2])
        vw = sb("vw", [P, D])
        vb = sb("vb", [P, D])
        kvt = sb("kvt", [P, 2, P])

        s_const = c.sem("s_const")
        s_x = c.sem("s_x")
        s_src = c.sem("s_src")
        s_rec = c.sem("s_rec")
        s_dst = c.sem("s_dst")
        s_zero = c.sem("s_zero")
        s_dve = c.sem("s_dve1")
        s_inb = c.sem("s_inb")
        s_tot = c.sem("s_tot")
        s_tiles = c.sem("s_tiles")
        s_first = c.sem("s_first")
        s_past = c.sem("s_past")
        s_bkt = c.sem("s_bkt")
        s_off = c.sem("s_off")
        s_rank = c.sem("s_rank")
        s_rank_used = c.sem("s_rank_used")
        s_row = c.sem("s_row")
        s_ring = c.sem("s_ring")
        s_scat = c.s_scat
        s_var = c.sem("s_var")
        s_std = c.sem("s_std")
        s_z = c.sem("s_z")
        s_zd = c.sem("s_zd")
        s_hs = c.sem("s_hs")
        s_hstd = c.sem("s_hstd")
        s_zh = c.sem("s_zh")
        s_zh_used = c.sem("s_zh_used")
        s_g = c.sem("s_g")
        s_kv = c.sem("s_kv")
        block = ctx.enter_context(nc.Block())

        @block.sync
        def _(sp):
            for dst, name in ((kw, "L0_mix_kln_weight"), (kb, "L0_mix_kln_bias")):
                with nc.allow_non_contiguous_dma("one column per chunk"):
                    for k in range(2):
                        sp.dma_start(dst[:, k:k + 1], a[name][k * P:k * P + P].unsqueeze(1)).then_inc(s_kv, 16)
            sp.dma_start(vw[:, :], row_to_all(a["L0_mix_vln_weight"], D)).then_inc(s_kv, 16)
            sp.dma_start(vb[:, :], row_to_all(a["L0_mix_vln_bias"], D)).then_inc(s_kv, 16)
            sp.wait_ge(s_const, 1)
            sp.dma_start(src_i[:, 0:ET - 1], a["src_cols"]).then_inc(s_src, 16)
            sp.dma_start(src_i[0:EREST, ET - 1:ET], a["src_rest"]).then_inc(s_src, 16)
            sp.dma_start(dst_i[:, 0:ET - 1], a["dst_cols"]).then_inc(s_dst, 16)
            sp.dma_start(dst_i[0:EREST, ET - 1:ET], a["dst_rest"]).then_inc(s_dst, 16)
            sp.dma_start(rec_in[:, 0:ET - 1, :], a["rec_cols"]).then_inc(s_rec, 16)
            sp.dma_start(rec_in[0:EREST, ET - 1, :], a["rec_rest"]).then_inc(s_rec, 16)
            sp.dma_start(c.x[:, :, :], rows(a["x"])).then_inc(s_x, 16)
            zr = c.rec_dram.rearrange("(p s r) f -> p s (r f)", p=P, s=4)
            for s in range(4):
                sp.dma_start(zr[:, s, :], zeros[:, :]).then_inc(s_zero, 16)
            sp.wait_ge(s_z, 1)
            sp.dma_start(rows(c.z_dram), c.z[:, :, :]).then_inc(s_zd, 16)
            sp.wait_ge(s_zd, 16)
            for h in range(2):
                sp.wait_ge(s_scat[h], 16 * ET // 2)

        @block.gpsimd
        def _(pool):
            nc.gpsimd.memset(zeros[:, :], 0.0)
            nc.gpsimd.memset(dst_i[:, ET - 1:ET], 0)
            nc.gpsimd.memset(rec_in[:, ET - 1, :], 0.0)
            nc.gpsimd.memset(src_i[:, ET - 1:ET], NONE).then_inc(s_const, 1)
            nc.gpsimd.memset(c.ones[:, :], 1.0)
            nc.gpsimd.memset(c.ident[:, :], 0.0)
            nc.gpsimd.memset(c.ltri[:, :], 1.0)
            nc.gpsimd.memset(pick[:, :], 0.0).then_inc(s_const, 1)
            pool.wait_ge(s_const, 2)
            nc.gpsimd.memset(pick[:, NT - 1:NT], 1.0)
            nc.gpsimd.affine_select(out=c.ident[:, :], in_=c.ident[:, :], compare_op=ALU.not_equal, fill=1.0,
                                    base=0, pattern=[[-1, P]], channel_multiplier=1)
            nc.gpsimd.affine_select(out=c.ltri[:, :], in_=c.ltri[:, :], compare_op=ALU.is_gt, fill=0.0,
                                    base=0, pattern=[[1, P]], channel_multiplier=-1)
            nc.gpsimd.iota(c.iota[:, :], pattern=[[1, NP_]], base=0, channel_multiplier=0,
                           allow_small_or_imprecise_dtypes=True)
            nc.gpsimd.iota(iota_tile[:, :], pattern=[[1, ST]], base=0, channel_multiplier=0,
                           allow_small_or_imprecise_dtypes=True).then_inc(s_const, 1)
            pool.wait_ge(s_zero, 64)
            pool.wait_ge(s_row, 1)

            def scatter(t, h, group, last):
                pool.wait_ge(s_scat[h], 8 * 16 * group)
                nc.gpsimd.tensor_copy(rec_ring[h][:, :, :], rec_in[:, bass.ds(t, 8), :])
                nc.gpsimd.tensor_copy(row_ring[h][:, :], row[:, bass.ds(t, 8)]).then_inc(s_ring, 1)
                pool.wait_ge(s_ring, group * 2 + h + 1)
                pool.sem_inc(c.s_pass, 1)
                for u in range(8):
                    n = EREST if last and u == 7 else P
                    nc.gpsimd.indirect_dma_start(
                        out=c.rec_dram, out_offset=bass.IndirectOffsetOnAxis(ap=row_ring[h][0:n, u:u + 1], axis=0),
                        in_=rec_ring[h][0:n, u, :], in_offset=None).then_inc(s_scat[h], 16)

            rounds = ET // 16 - 1
            with pool.Fori(0, rounds) as i:
                scatter(i * 16, 0, i, False)
                scatter(i * 16 + 8, 1, i, False)
            scatter(rounds * 16, 0, rounds, False)
            scatter(rounds * 16 + 8, 1, rounds, True)

        @block.scalar
        def _(act):
            act.wait_ge(s_var, 1)
            nc.scalar.activation(std[:, :], varp[:, :], ACT.Sqrt).then_inc(s_std, 1)
            with act.Fori(0, 5) as i:
                act.wait_ge(s_hs, i + 1)
                nc.scalar.activation(hstd[:, :], hs[:, :], ACT.Sqrt, scale=1.0 / (HC - 1)).then_inc(s_hstd, 1)

        @block.vector
        def _(dve):
            link = Chain(dve, s_dve)
            v = nc.vector
            dve.wait_ge(s_const, 3)
            dve.wait_ge(s_src, 32)
            link(v.tensor_copy(srcf[:, :], src_i[:, :]))
            link(v.tensor_scalar(t0[:, :], srcf[:, :], 1.0 / NP_, -62.0 / NP_, ALU.mult, ALU.add))
            link(v.tensor_scalar(t0[:, :], t0[:, :], MAGIC, None, ALU.add))
            link(v.tensor_scalar(t0[:, :], t0[:, :], -MAGIC, None, ALU.add))
            link(v.tensor_copy(bucket[:, :], t0[:, :]))
            link(v.tensor_copy(ltri_b[:, :], c.ltri[:, :]))
            for b in range(NT):
                v.tensor_scalar(inb[:, b, :], bucket[:, :], float(b), None, ALU.is_equal).then_inc(s_inb, 1)
            dve.wait_ge(s_rec, 32)
            dve.wait_ge(s_dst, 32)
            v.scalar_tensor_tensor(out=rec_in[:, :, R_LOCAL], in0=t0[:, :], scalar=-float(NP_), in1=srcf[:, :],
                                   op0=ALU.mult, op1=ALU.add)
            v.tensor_copy(rec_in[:, :, R_DST], dst_i[:, :])
            dve.wait_ge(s_tot, 1)
            link(v.tensor_copy(tot[:, :], bank[5][0:NT, 0:ET]))
            link(v.tensor_copy(scan[0][:, :], tot[:, :]))
            k, s = 1, 0
            while k < ET:
                v.tensor_copy(scan[1 - s][:, 0:k], scan[s][:, 0:k])
                link(v.tensor_tensor(scan[1 - s][:, k:ET], scan[s][:, k:ET], scan[s][:, 0:ET - k], ALU.add))
                k, s = 2 * k, 1 - s
            link(v.tensor_scalar(tiles[:, :], scan[s][:, ET - 1:ET], 1.0 / P, (P - 1) / 2 / P, ALU.mult, ALU.add))
            link(v.tensor_scalar(tiles[:, :], tiles[:, :], MAGIC, None, ALU.add))
            v.tensor_scalar(tiles[:, :], tiles[:, :], -MAGIC, None, ALU.add).then_inc(s_tiles, 1)
            link(v.tensor_tensor(off[:, :], scan[s][:, :], tot[:, :], ALU.subtract))
            dve.wait_ge(s_first, 1)
            link(v.tensor_scalar(first[:, :], bank[6][0:NT, 0:1], float(P), None, ALU.mult))
            v.tensor_scalar(off[:, :], off[:, :], first[:, 0:1], None, ALU.add).then_inc(s_off, 1)
            link(v.tensor_tensor(last[:, :], bank[6][0:NT, 0:1], tiles[:, :], ALU.add))
            v.tensor_scalar(past[:, :], iota_tile[:, :], last[:, 0:1], None, ALU.is_ge).then_inc(s_past, 1)
            link(v.memset(pos[:, :], 0.0))
            for b in range(NT):
                dve.wait_ge(s_rank, b + 1)
                r = v.tensor_tensor(part[:, :], bank[b % 2][:, 0:ET], inb[:, b, :], ALU.mult)
                r.then_inc(s_rank_used, 1)
                dve.wait_ge(s_rank_used, b + 1)
                link(v.tensor_tensor(pos[:, :], pos[:, :], part[:, :], ALU.add))
            dve.wait_ge(s_bkt, 1)
            v.tensor_copy(c.bucket_of[:, :], bank[7][0:1, 0:ST])
            link(v.tensor_copy(posi[:, :], pos[:, :]))
            v.tensor_scalar(lo[:, :], posi[:, :], P - 1, None, ALU.bitwise_and)
            link(v.tensor_scalar(hi[:, :], posi[:, :], 7, None, ALU.arith_shift_right))
            v.scalar_tensor_tensor(out=row[:, :], in0=lo[:, :], scalar=float(ST), in1=hi[:, :],
                                   op0=ALU.mult, op1=ALU.add).then_inc(s_row, 1)
            dve.wait_ge(s_x, 16)
            layer_norm_stats(c, dve, link, stats, varp)
            link(v.tensor_scalar(varp[:, :], c.mv[:, :, 1], EPS, None, ALU.add))
            dve.nop().then_inc(s_var, 1)
            dve.wait_ge(s_std, 1)
            link(v.reciprocal(c.rstd[:, :], std[:, :]))
            link(v.tensor_tensor(c.z[:, :, :], c.x[:, :, :], bcast(c.mv[:, :, 0:1], [NP_, NT, D]), ALU.subtract))
            link(v.tensor_tensor(c.z[:, :, :], c.z[:, :, :], bcast(c.rstd[:, :].unsqueeze(2), [NP_, NT, D]), ALU.mult))
            dve.nop().then_inc(s_z, 1)
            link.loop()
            with dve.Fori(0, 5) as i:
                link.at(i, 5)
                zi = c.z[:, bass.ds(i * 5, 5), :].rearrange("p t (h d) -> p (t h) d", h=H0)
                zc3 = zc[:, :, :].rearrange("p t (h d) -> p (t h) d", h=H0)
                sq3 = sq[:, :, :].rearrange("p t (h d) -> p (t h) d", h=H0)
                zh3 = zh[:, :, :].rearrange("p t (h d) -> p (t h) d", h=H0)
                full = [NP_, 5 * H0, HC]
                link(v.reduce_sum(hm[:, :], zi, X))
                link(v.tensor_scalar(hm[:, :], hm[:, :], 1.0 / HC, None, ALU.mult))
                link(v.tensor_tensor(zc3, zi, bcast(hm[:, :].unsqueeze(2), full), ALU.subtract))
                link(v.tensor_tensor(sq3, zc3, zc3, ALU.mult))
                v.reduce_sum(hs[:, :], sq3, X).then_inc(s_hs, 1)
                dve.wait_ge(s_hstd, i + 1)
                link(v.tensor_scalar(hstd[:, :], hstd[:, :], EPS, None, ALU.add))
                v.reciprocal(hr[:, :], hstd[:, :]).then_inc(s_zh, 1)
                dve.wait_ge(s_zh, i * 2 + 1)
                dve.wait_ge(s_zh_used, i)
                v.tensor_tensor(zh3, zc3, bcast(hr[:, :].unsqueeze(2), full), ALU.mult).then_inc(s_zh, 1)
            link.end(5)
            dve.wait_ge(s_g, 1)
            dve.wait_ge(s_kv, 96)
            link(v.memset(c.kv[:, :, :], 0.0))
            for k in range(2):
                cols = slice(k * P, k * P + P)
                link(v.tensor_scalar(kvt[:, k, :], bank[k][:, 0:P], kw[:, k:k + 1], None, ALU.mult))
                link(v.scalar_tensor_tensor(out=kvt[:, k, :], in0=bank[2][:, cols], scalar=kb[:, k:k + 1],
                                            in1=kvt[:, k, :], op0=ALU.mult, op1=ALU.add))
                link(v.tensor_tensor(kvt[:, k, :], kvt[:, k, :], vw[:, cols], ALU.mult))
                link(v.tensor_scalar(ks[:, k:k + 1], kb[:, k:k + 1], float(N), None, ALU.mult))
                link(v.scalar_tensor_tensor(out=ks[:, k:k + 1], in0=bank[3][:, k:k + 1], scalar=kw[:, k:k + 1],
                                            in1=ks[:, k:k + 1], op0=ALU.mult, op1=ALU.add))
                link(v.scalar_tensor_tensor(out=kvt[:, k, :], in0=vb[:, cols], scalar=ks[:, k:k + 1],
                                            in1=kvt[:, k, :], op0=ALU.mult, op1=ALU.add))
                for q in range(4):
                    own = slice(q * HC, q * HC + HC)
                    v.tensor_scalar(c.kv[own, k, own], kvt[own, k, own], 1.0 / N, None, ALU.mult)

        @block.tensor
        def _(pe):
            mm = nc.tensor.matmul
            pe.wait_ge(s_const, 3)
            for b in range(NT):
                pe.wait_ge(s_inb, b + 1)
                r = mm(bank[5][0:NT, 0:ET], pick[:, NT - 1 - b:2 * NT - 1 - b], inb[:, b, :],
                       start=b == 0, stop=b == NT - 1)
            r.then_inc(s_tot, 1)
            pe.wait_ge(s_tiles, 1)
            mm(bank[6][0:NT, 0:1], c.ltri[0:NT, 0:NT], tiles[:, :], start=True, stop=True).then_inc(s_first, 1)
            pe.wait_ge(s_off, 1)
            for b in range(NT):
                if b >= 2:
                    pe.wait_ge(s_rank_used, b - 1)
                mm(bank[b % 2][:, 0:ET], ltri_b[:, :], inb[:, b, :], start=True, stop=False)
                mm(bank[b % 2][:, 0:ET], bcast(c.ident[0:NT, b:b + 1], [NT, P]), off[:, :],
                   start=False, stop=True).then_inc(s_rank, 1)
            pe.wait_ge(s_past, 1)
            mm(bank[7][0:1, 0:ST], c.ones[0:NT, 0:1], past[:, :], start=True, stop=True).then_inc(s_bkt, 1)
            pe.wait_ge(s_rank_used, NT)

            def products(i, first, last):
                pe.wait_ge(s_zh, i * 2 + 2)
                for u in range(5):
                    go = first and u == 0
                    for k in range(2):
                        zk = zh[:, u, k * P:k * P + P]
                        mm(bank[k][:, 0:P], zk, zk, start=go, stop=last and u == 4)
                        mm(bank[3][:, k:k + 1], zk, c.ones[0:NP_, 0:1], start=go and k == 0, stop=last and u == 4 and k == 1)
                    r = mm(bank[2][:, 0:D], c.ones[0:NP_, :], zh[:, u, :], start=go, stop=last and u == 4)
                r.then_inc(s_zh_used, 1)

            products(0, True, False)
            with pe.Fori(1, 4) as i:
                products(i, False, False)
            products(4, False, True)
            pe.wait_ge(s_zh_used, 5)
            pe.nop().then_inc(s_g, 1)


def layer_norm_stats(c, dve, link, stats, varp):
    link.loop()
    with dve.Fori(0, NT) as i:
        link.at(i, 1)
        link(c.nc.vector.bn_stats(flat(stats, i), flat(c.x, i)))
    link.end(NT)
    for t in range(NT):
        r = c.nc.vector.bn_aggr(c.mv[:, t, :], stats[:, t, :])
    link(r)


class Norm:

    def __init__(self, c, name, ctx):
        self.c = c
        self.stats = c.sb(name + "_stats", [NP_, NT, 6], F32, ctx)
        self.varp = c.sb(name + "_varp", [NP_, NT], F32, ctx)
        self.std = c.sb(name + "_std", [NP_, NT], F32, ctx)
        self.s_tile = c.sem(name + "_s_tile")
        self.s_var = c.sem(name + "_s_var")
        self.s_std = c.sem(name + "_s_std")

    def tile(self, t):
        self.c.nc.vector.bn_stats(flat(self.stats, t), flat(self.c.x, t)).then_inc(self.s_tile, 1)

    def finish(self, dve, link):
        c, v = self.c, self.c.nc.vector
        dve.wait_ge(self.s_tile, NT)
        for t in range(NT):
            r = v.bn_aggr(c.mv[:, t, :], self.stats[:, t, :])
        link(r)
        v.tensor_scalar(self.varp[:, :], c.mv[:, :, 1], EPS, None, ALU.add).then_inc(self.s_var, 1)
        dve.wait_ge(self.s_std, 1)
        link(v.reciprocal(c.rstd[:, :], self.std[:, :]))
        link(v.scalar_tensor_tensor(out=c.shift[:, :], in0=c.mv[:, :, 0], scalar=-1.0, in1=c.rstd[:, :],
                                    op0=ALU.mult, op1=ALU.mult))

    def root(self, act):
        act.wait_ge(self.s_var, 1)
        self.c.nc.scalar.activation(self.std[:, :], self.varp[:, :], ACT.Sqrt).then_inc(self.s_std, 1)


def flat(buffer, t):
    return buffer[:, bass.ds(t, 1), :].rearrange("p o f -> p (o f)")


def gather_rows(c, pool, table, idx_ring, slots, s_ring, s_used, s_got, rec):
    nc = c.nc

    def half(i, h, free):
        j = i * UN + h * HALF
        if free:
            pool.wait_ge(s_used, j - HALF)
        nc.gpsimd.tensor_copy(idx_ring[h][:, :], rec[:, bass.ds(j, HALF), R_DST]).then_inc(s_ring, 1)
        pool.wait_ge(s_ring, i * 2 + h + 1)
        pool.sem_inc(c.s_pass, 1)
        for u in range(HALF):
            nc.gpsimd.indirect_dma_start(
                out=slots[h * HALF + u], out_offset=None, in_=table,
                in_offset=bass.IndirectOffsetOnAxis(ap=idx_ring[h][:, u:u + 1], axis=0)
            ).then_inc(s_got[h * HALF + u], 16)

    half(0, 0, False)
    half(0, 1, False)
    with pool.Fori(1, ST // UN) as i:
        half(i, 0, True)
        half(i, 1, True)


def first_edges(c, acc):
    nc, bank = c.nc, c.bank
    with ExitStack() as ctx:
        c.stage = ctx

        def sb(name, shape, dt=F32):
            return c.sb(name, shape, dt, ctx)

        idx_ring = [sb(f"idx_ring{h}", [P, HALF], I32) for h in range(2)]
        g = sb("g", [P, UN, D + 1])
        oh = sb("oh", [P, 4, NP_])
        s_rec = c.sem("s_e0_rec")
        s_ring = c.sem("s_e0_ring")
        s_got = c.s_got
        s_weighed = c.sem("s_e0_weighed")
        s_oh = c.sem("s_e0_oh")
        s_mm = c.sem("s_e0_mm")
        s_acc = c.sem("s_e0_acc")
        block = ctx.enter_context(nc.Block())
        rec = c.rec

        @block.sync
        def _(sp):
            sp.dma_start(rec[:, :, :], c.rec_dram.rearrange("(p j) f -> p j f", p=P)).then_inc(s_rec, 16)
            sp.wait_ge(s_rec, 16)

        @block.gpsimd
        def _(pool):
            pool.wait_ge(s_rec, 16)
            gather_rows(c, pool, c.z_dram, idx_ring, [g[:, u, 0:D] for u in range(UN)], s_ring, s_mm, s_got, rec)

        @block.scalar
        def _(act):
            with act.Fori(0, ST // UN) as i:
                for u in range(UN):
                    j = i * UN + u
                    act.wait_ge(s_got[u], i * 16 + 16)
                    nc.scalar.activation(g[:, u, 0:D], g[:, u, 0:D], ACT.Copy, scale=flat(rec, j)[:, R_W:R_W + 1])
                    nc.scalar.activation(g[:, u, D:D + 1], flat(rec, j)[:, R_ONE:R_ONE + 1],
                                         ACT.Copy).then_inc(s_weighed, 1)

        @block.vector
        def _(dve):
            v = nc.vector
            v.tensor_tensor(c.x[:, :, :], c.x[:, :, :], c.z[:, :, :], ALU.add)
            v.memset(acc[:, :, :], 0.0).then_inc(s_acc, 4)
            dve.wait_ge(s_rec, 16)

            def one_hot(j, u):
                v.tensor_scalar(oh[:, u % 4, :], c.iota[:, :], flat(rec, j)[:, R_LOCAL:R_LOCAL + 1], None,
                                ALU.is_equal).then_inc(s_oh, 1)

            def rounds(i, last):
                for u in range(UN):
                    j = i * UN + u
                    b = dve.value_load(c.bucket_of[0:1, bass.ds(j, 1)], min_val=0, max_val=NT)
                    dve.wait_ge(s_mm, j + 1)
                    dve.wait_ge(s_acc, j + 4)
                    v.tensor_tensor(flat(acc, b), flat(acc, b), bank[u % 4][0:NP_, 0:D + 1],
                                    ALU.add).then_inc(s_acc, 1)
                    if not (last and u >= UN - 3):
                        one_hot(j + 3, u + 3)

            for u in range(3):
                one_hot(u, u)
            with dve.Fori(0, ST // UN - 1) as i:
                rounds(i, False)
            rounds(ST // UN - 1, True)

        @block.tensor
        def _(pe):
            with pe.Fori(0, ST // UN) as i:
                for u in range(UN):
                    j = i * UN + u
                    pe.wait_ge(s_weighed, j + 1)
                    pe.wait_ge(s_oh, j + 1)
                    pe.wait_ge(s_acc, j + 1)
                    nc.tensor.matmul(bank[u % 4][0:NP_, 0:D + 1], oh[:, u % 4, :], g[:, u, :],
                                     start=True, stop=True).then_inc(s_mm, 1)



def column(buffer, t):
    return buffer[:, bass.ds(t, 1)]


def combine_first(c, acc):
    nc, a, bank = c.nc, c.a, c.bank
    with ExitStack() as ctx:
        c.stage = ctx

        def sb(name, shape, dt=F32):
            return c.sb(name, shape, dt, ctx)

        filt = sb("filt", [P, 2, D])
        rows_in = sb("rows_in", [NP_, 4, 2 * D])
        cols_in = sb("cols_in", [P, 2, 4 * NP_])
        norm = Norm(c, "n2", ctx)
        s_w = c.sem("cf_s_w")
        s_in = c.sem("cf_s_in")
        s_tp = c.sem("cf_s_tp")
        s_cols = c.sem("cf_s_cols")
        s_mm = c.sem("cf_s_mm")
        s_add = c.sem("cf_s_add")
        s_dve = c.sem("cf_s_dve")
        block = ctx.enter_context(nc.Block())

        @block.sync
        def _(sp):
            sp.dma_start(filt[:, :, :], a["L0_gnn_filters"].rearrange("(k p) f -> p k f", p=P)).then_inc(s_w, 16)
            sp.wait_ge(s_w, 16)

        @block.scalar
        def _(act):
            def load(t, u):
                wait(act, s_tp, t - 3)
                nc.scalar.copy(rows_in[:, u, 0:D], flat(acc, t)[:, 0:D])
                nc.scalar.copy(rows_in[:, u, D:2 * D], flat(c.z, t)).then_inc(s_in, 1)

            each_node_tile(act, load)
            norm.root(act)

        @block.vector
        def _(dve):
            v = nc.vector
            link = Chain(dve, s_dve)
            v.tensor_copy(c.deg[:, :], acc[:, 0:NT, D])

            def turn(t, u):
                wait(dve, s_tp, t + 1)
                wait(dve, s_mm, t - 1)
                v.tensor_copy(cols_in[:, u % 2, :], bank[u % 2][:, 0:4 * NP_]).then_inc(s_cols, 1)

            def add(t, u):
                if not (isinstance(t, int) and t == NT - 1):
                    turn(t + 1, (u + 1) % 4)
                dve.wait_ge(s_mm, t + 1)
                v.tensor_tensor(flat(c.x, t), flat(c.x, t), bank[2 + u % 2][0:NP_, 0:D], ALU.add).then_inc(s_add, 1)
                dve.wait_ge(s_add, t + 1)
                norm.tile(t)

            turn(0, 0)
            each_node_tile(dve, add)
            norm.finish(dve, link)

        @block.tensor
        def _(pe):
            def turn(t, u):
                wait(pe, s_in, t + 1)
                wait(pe, s_cols, t - 1)
                for k in range(4):
                    r = nc.tensor.transpose(bank[u % 2][:, k * NP_:(k + 1) * NP_],
                                            rows_in[:, u, k * P:(k + 1) * P], c.ident[0:NP_, 0:NP_])
                r.then_inc(s_tp, 1)

            def multiply(t, u):
                if not (isinstance(t, int) and t == NT - 1):
                    turn(t + 1, (u + 1) % 4)
                pe.wait_ge(s_cols, t + 1)
                wait(pe, s_add, t - 1)
                to, cols = bank[2 + u % 2], cols_in[:, u % 2, :]
                for k in range(2):
                    nc.tensor.matmul(to[0:NP_, 0:D], cols[:, k * NP_:(k + 1) * NP_], filt[:, k, :],
                                     start=k == 0, stop=False)
                for k in range(2):
                    r = nc.tensor.matmul(to[0:NP_, k * P:(k + 1) * P], cols[:, (2 + k) * NP_:(3 + k) * NP_],
                                         c.kv[:, k, :], start=False, stop=k == 1)
                r.then_inc(s_mm, 1)

            pe.wait_ge(s_w, 16)
            turn(0, 0)
            each_node_tile(pe, multiply)



def slice_weights(c, swt, tokens):
    nc, a, bank = c.nc, c.a, c.bank
    HG = H0 * G
    NC = HG // P
    with ExitStack() as ctx:
        c.stage = ctx

        def sb(name, shape, dt=F32):
            return c.sb(name, shape, dt, ctx)

        wxt = sb("wxt", [G, H0, D + 1])
        wslice = sb("wslice", [G, G])
        bslice = sb("bslice", [P, G])
        temp = sb("temp", [P, H0])
        rtemp = sb("rtemp", [P, H0])
        wxs = sb("wxs", [P, 2, HG])
        bxs = sb("bxs", [P, HG])
        zr = sb("zr", [NP_, 4, D + 1])
        ztr = sb("ztr", [P, 2, 2 * NP_])
        lg = sb("lg", [NP_, 2, HG])
        ex = sb("ex", [NP_, 2, HG])
        sw = sb("sw", [NP_, 4, HG])
        mx = sb("mx", [NP_, 2, H0])
        tot = sb("sw_tot", [NP_, 2, H0])
        inv = sb("sw_inv", [NP_, 2, H0])
        s_w = c.sem("sl_s_w")
        s_ones = c.sem("sl_s_ones")
        s_fold = c.sem("sl_s_fold")
        s_ready = c.sem("sl_s_ready")
        s_in = c.sem("sl_s_in")
        s_tp = c.sem("sl_s_tp")
        s_ztr = c.sem("sl_s_ztr")
        s_lg = c.sem("sl_s_lg")
        s_sub = c.sem("sl_s_sub")
        s_exp = c.sem("sl_s_exp")
        s_sw = c.sem("sl_s_sw")
        s_sum = c.sem("sl_s_sum")
        s_swt = c.sem("sl_s_swt")
        s_dve = c.sem("sl_s_dve")
        block = ctx.enter_context(nc.Block())

        def heads(ap):
            return ap.rearrange("p (h g) -> p h g", h=H0)

        @block.sync
        def _(sp):
            sp.dma_start(wxt[:, :, :], a["L0_ffn_wxt"].rearrange("(h d) f -> d h f", h=H0)).then_inc(s_w, 16)
            sp.dma_start(wslice[:, :], a["L0_ffn_W_slice"]).then_inc(s_w, 16)
            sp.dma_start(bslice[:, :], row_to_all(a["L0_ffn_b_slice"], G)).then_inc(s_w, 16)
            sp.dma_start(temp[:, :], row_to_all(a["L0_ffn_temperature"], H0)).then_inc(s_w, 16)
            sp.wait_ge(s_w, 64)

        @block.gpsimd
        def _(pool):
            nc.gpsimd.memset(zr[:, :, :], 1.0).then_inc(s_ones, 1)

        @block.scalar
        def _(act):
            def load(t, u):
                wait(act, s_sum, t - 3)
                nc.scalar.activation(zr[:, u, 0:D], flat(c.x, t), ACT.Identity, bias=column(c.shift, t),
                                     scale=column(c.rstd, t)).then_inc(s_in, 1)

            def keep(t, u):
                act.wait_ge(s_sum, t + 1)
                src = bank[u % 2][:, 0:4 * NP_].rearrange("p (k n) -> p k n", k=NC)
                nc.scalar.copy(swt[:, :, bass.ds(t * NP_, NP_)], src).then_inc(s_swt, 1)

            def tile(t, u):
                if not (isinstance(t, int) and t == NT - 1):
                    load(t + 1, (u + 1) % 4)
                act.wait_ge(s_sub, t + 1)
                nc.scalar.activation(ex[:, u % 2, :], lg[:, u % 2, :], ACT.Exp).then_inc(s_exp, 1)
                if not (isinstance(t, int) and t < 2):
                    keep(t - 2, (u + 2) % 4)

            act.wait_ge(s_ones, 1)
            load(0, 0)
            each_node_tile(act, tile)
            keep(NT - 2, 3)
            keep(NT - 1, 0)

        @block.vector
        def _(dve):
            v = nc.vector
            link = Chain(dve, s_dve)
            dve.wait_ge(s_w, 64)
            link(v.tensor_scalar(temp[:, :], temp[:, :], 5.0, 0.1, ALU.min, ALU.max))
            link(v.reciprocal(rtemp[:, :], temp[:, :]))
            dve.wait_ge(s_fold, 1)
            rt = bcast(rtemp[:, :].unsqueeze(2), [P, H0, G])
            for k in range(2):
                v.tensor_tensor(heads(wxs[:, k, :]), heads(bank[k][:, :]), rt, ALU.mult)
            link(v.tensor_tensor(heads(bxs[:, :]), heads(bank[2][:, :]),
                                 bcast(bslice[:, :].unsqueeze(1), [P, H0, G]), ALU.add))
            v.tensor_tensor(heads(bxs[:, :]), heads(bxs[:, :]), rt, ALU.mult).then_inc(s_ready, 1)
            dve.wait_ge(s_ready, 1)

            def turn(t, u):
                dve.wait_ge(s_tp, t + 1)
                wait(dve, s_lg, t - 1)
                v.tensor_copy(ztr[:, u % 2, :], bank[u % 2][:, 0:2 * NP_]).then_inc(s_ztr, 1)

            def normalize(t, u):
                dve.wait_ge(s_exp, t + 1)
                e3 = heads(ex[:, u % 2, :])
                link(v.reduce_sum(tot[:, u % 2, :], e3, X))
                link(v.reciprocal(inv[:, u % 2, :], tot[:, u % 2, :]))
                wait(dve, s_sum, t - 3)
                v.tensor_tensor(heads(sw[:, u, :]), e3, bcast(inv[:, u % 2, :].unsqueeze(2), [NP_, H0, G]),
                                ALU.mult).then_inc(s_sw, 1)

            def tile(t, u):
                link.at(t, 4)
                if isinstance(t, int) and t == 0:
                    link.n = 2
                if not (isinstance(t, int) and t == NT - 1):
                    turn(t + 1, (u + 1) % 4)
                dve.wait_ge(s_lg, t + 1)
                l3 = heads(lg[:, u % 2, :])
                link(v.tensor_tensor(lg[:, u % 2, :], bank[2 + u % 2][0:NP_, :], bxs[0:NP_, :], ALU.add))
                link(v.tensor_reduce(mx[:, u % 2, :], l3, X, ALU.max))
                v.tensor_tensor(l3, l3, bcast(mx[:, u % 2, :].unsqueeze(2), [NP_, H0, G]),
                                ALU.subtract).then_inc(s_sub, 1)
                if not (isinstance(t, int) and t == 0):
                    normalize(t - 1, (u + 3) % 4)

            turn(0, 0)
            link.loop()
            link.start -= 2
            each_node_tile(dve, tile)
            link.end(NT)
            normalize(NT - 1, 0)
            dve.wait_ge(s_sum, NT)
            for k in range(NC):
                v.tensor_copy(tokens[:, k, :], bank[4 + k][:, 0:D + 1])

        @block.tensor
        def _(pe):
            mm = nc.tensor.matmul
            pe.wait_ge(s_w, 64)
            for h in range(H0):
                own = slice(h * G, h * G + G)
                for k in range(2):
                    mm(bank[k][:, own], wxt[:, h, k * P:k * P + P], wslice[:, :], start=True, stop=True)
                r = mm(bank[2][:, own], bcast(wxt[:, h, D:D + 1], [G, P]), wslice[:, :], start=True, stop=True)
            r.then_inc(s_fold, 1)
            pe.wait_ge(s_ready, 1)

            def turn(t, u):
                pe.wait_ge(s_in, t + 1)
                wait(pe, s_swt, t - 3)
                for k in range(2):
                    r = nc.tensor.transpose(bank[u % 2][:, k * NP_:(k + 1) * NP_], zr[:, u, k * P:(k + 1) * P],
                                            c.ident[0:NP_, 0:NP_])
                r.then_inc(s_tp, 1)

            def gather(t, u, first, last):
                pe.wait_ge(s_sw, t + 1)
                wait(pe, s_swt, t - 1)
                for k in range(NC):
                    mm(bank[4 + k][:, 0:D + 1], sw[:, u, k * P:k * P + P], zr[:, u, :], start=first, stop=last)
                for k in range(NC):
                    r = nc.tensor.transpose(bank[u % 2][:, k * NP_:(k + 1) * NP_], sw[:, u, k * P:(k + 1) * P],
                                            c.ident[0:NP_, 0:NP_])
                r.then_inc(s_sum, 1)

            def tile(t, u):
                if not (isinstance(t, int) and t == NT - 1):
                    turn(t + 1, (u + 1) % 4)
                pe.wait_ge(s_ztr, t + 1)
                wait(pe, s_sub, t - 1)
                for k in range(2):
                    r = mm(bank[2 + u % 2][0:NP_, :], ztr[:, u % 2, k * NP_:(k + 1) * NP_], wxs[:, k, :],
                           start=k == 0, stop=k == 1)
                r.then_inc(s_lg, 1)
                if not (isinstance(t, int) and t < 2):
                    gather(t - 2, (u + 2) % 4, isinstance(t, int) and t == 2, False)

            turn(0, 0)
            each_node_tile(pe, tile)
            gather(NT - 2, 3, False, False)
            gather(NT - 1, 0, False, True)


def slice_attention(c, tokens, pw):
    nc, a, bank = c.nc, c.a, c.bank
    NC = H0 * G // P
    with ExitStack() as ctx:
        c.stage = ctx

        def sb(name, shape, dt=F32):
            return c.sb(name, shape, dt, ctx)

        wfx = sb("wfx", [P, 2, H0 * G])
        bfx = sb("bfx", [P, H0 * G])
        wq, wk, wv = (sb(n, [P, P]) for n in ("wq", "wk", "wv"))
        wout = sb("wout", [P, NC, D])
        tt = sb("tt", [P, 2, NC, P])
        inv = sb("tok_inv", [P, NC])
        ni = sb("tok_ni", [P, NC])
        tok, tokt, q, k_, v_ = (sb("sa_" + n, [P, NC, P]) for n in ("tok", "tokt", "q", "k", "v"))
        at, att, ost, sc = (sb("sa_" + n, [P, NC, P]) for n in ("at", "att", "ost", "sc"))
        mx = sb("sa_mx", [P, NC])
        tot = sb("sa_tot", [P, NC])
        rt = sb("sa_rt", [P, NC])
        s_zero = c.sem("sa_s_zero")
        s_w = c.sem("sa_s_w")
        s_pe = c.sem("sa_s_pe")
        s_out = c.sem("sa_s_out")
        s_dve = c.sem("sa_s_dve")
        s_exp = c.sem("sa_s_exp")
        block = ctx.enter_context(nc.Block())
        HALVES = [slice(0, G), slice(G, P)]

        @block.gpsimd
        def _(pool):
            for m in (wq, wk, wv):
                nc.gpsimd.memset(m[:, :], 0.0).then_inc(s_zero, 1)
            nc.gpsimd.memset(tok[:, :, :], 0.0).then_inc(s_zero, 1)
            nc.gpsimd.memset(at[:, :, :], 0.0).then_inc(s_zero, 1)

        @block.sync
        def _(sp):
            sp.dma_start(wfx[:, :, :], a["L0_ffn_W_fx"].rearrange("(k p) f -> p k f", p=P)).then_inc(s_w, 16)
            sp.dma_start(bfx[:, :], row_to_all(a["L0_ffn_b_fx"], H0 * G)).then_inc(s_w, 16)
            sp.dma_start(wout[:, :, :], a["L0_ffn_W_out"].rearrange("(k p) f -> p k f", p=P)).then_inc(s_w, 16)
            sp.wait_ge(s_zero, 3)
            for m, n in ((wq, "q"), (wk, "k"), (wv, "v")):
                for h in HALVES:
                    sp.dma_start(m[h, h], a["L0_ffn_W_" + n]).then_inc(s_w, 16)
            sp.wait_ge(s_w, 9 * 16)

        @block.scalar
        def _(act):
            act.wait_ge(s_out, 5)
            for h in HALVES:
                r = nc.scalar.activation(at[h, :, h], sc[h, :, h], ACT.Exp, scale=float(G) ** -0.5)
            r.then_inc(s_exp, 1)

        @block.vector
        def _(dve):
            v = nc.vector
            link = Chain(dve, s_dve)

            def out(dst, src, n):
                dve.wait_ge(s_pe, n)
                v.tensor_copy(dst, src).then_inc(s_out, 1)

            def banked(b):
                return bank[b][:, :].rearrange("p (c j) -> p c j", c=NC)

            dve.wait_ge(s_pe, 1)
            v.tensor_copy(tt[:, 0, :, :], banked(0))
            v.tensor_copy(tt[:, 1, :, :], banked(1)).then_inc(s_out, 1)
            link(v.tensor_scalar(inv[:, :], tokens[:, :, D], EPS, None, ALU.add))
            link(v.reciprocal(inv[:, :], inv[:, :]))
            link(v.tensor_tensor(ni[:, :], tokens[:, :, D], inv[:, :], ALU.mult))
            dve.wait_ge(s_zero, 5)
            dve.wait_ge(s_w, 9 * 16)
            dve.wait_ge(s_pe, 2)
            for k in range(NC):
                for h in HALVES:
                    v.tensor_scalar(tok[h, k, h], banked(2)[h, k, h], inv[h, k:k + 1], None, ALU.mult)
            link(v.memset(mx[:, :], 0.0))
            for k in range(NC):
                for h in HALVES:
                    r = v.scalar_tensor_tensor(out=tok[h, k, h], in0=bfx[h, k * P + h.start:k * P + h.stop],
                                               scalar=ni[h, k:k + 1], in1=tok[h, k, h], op0=ALU.mult, op1=ALU.add)
            r.then_inc(s_out, 1)
            out(tokt[:, :, :], banked(3), 3)
            dve.wait_ge(s_pe, 4)
            v.tensor_copy(q[:, :, :], banked(4))
            v.tensor_copy(k_[:, :, :], banked(5))
            v.tensor_copy(v_[:, :, :], banked(6)).then_inc(s_out, 1)
            dve.wait_ge(s_pe, 5)
            for h in HALVES:
                r = v.tensor_reduce(mx[h, :], banked(7)[h, :, h], X, ALU.max)
            link(r)
            for h in HALVES:
                r = v.tensor_tensor(sc[h, :, h], banked(7)[h, :, h], bcast(mx[h, :].unsqueeze(2), [G, NC, G]),
                                    ALU.subtract)
            r.then_inc(s_out, 1)
            dve.wait_ge(s_exp, 1)
            for h in HALVES:
                r = v.reduce_sum(tot[h, :], at[h, :, h], X)
            link(r)
            link(v.reciprocal(rt[:, :], tot[:, :]))
            for h in HALVES:
                r = v.tensor_tensor(at[h, :, h], at[h, :, h], bcast(rt[h, :].unsqueeze(2), [G, NC, G]), ALU.mult)
            r.then_inc(s_out, 1)
            out(att[:, :, :], banked(0), 6)
            out(ost[:, :, :], banked(1), 7)
            dve.wait_ge(s_pe, 8)
            for k in range(NC):
                v.tensor_copy(pw[:, k, :], bank[2 + k // 2][:, k % 2 * D:k % 2 * D + D])

        @block.tensor
        def _(pe):
            mm, tp = nc.tensor.matmul, nc.tensor.transpose

            def part(b, k):
                return bank[b][:, k * P:k * P + P]

            for k in range(NC):
                for j in range(2):
                    r = tp(part(j, k), tokens[:, k, j * P:j * P + P], c.ident[:, :])
            r.then_inc(s_pe, 1)
            pe.wait_ge(s_w, 9 * 16)
            pe.wait_ge(s_out, 1)
            for k in range(NC):
                for j in range(2):
                    r = mm(part(2, k), tt[:, j, k, :], wfx[:, j, k * P:k * P + P], start=j == 0, stop=j == 1)
            r.then_inc(s_pe, 1)
            pe.wait_ge(s_out, 2)
            for k in range(NC):
                r = tp(part(3, k), tok[:, k, :], c.ident[:, :])
            r.then_inc(s_pe, 1)
            pe.wait_ge(s_out, 3)
            tk = tokt[:, :, :].rearrange("p c j -> p (c j)")
            mm(bank[4][:, :], wq[:, :], tk, start=True, stop=True)
            mm(bank[5][:, :], wk[:, :], tk, start=True, stop=True)
            for k in range(NC):
                r = mm(part(6, k), tokt[:, k, :], wv[:, :], start=True, stop=True)
            r.then_inc(s_pe, 1)
            pe.wait_ge(s_out, 4)
            for k in range(NC):
                r = mm(part(7, k), q[:, k, :], k_[:, k, :], start=True, stop=True)
            r.then_inc(s_pe, 1)
            pe.wait_ge(s_out, 6)
            for k in range(NC):
                r = tp(part(0, k), at[:, k, :], c.ident[:, :])
            r.then_inc(s_pe, 1)
            pe.wait_ge(s_out, 7)
            for k in range(NC):
                r = mm(part(1, k), v_[:, k, :], att[:, k, :], start=True, stop=True)
            r.then_inc(s_pe, 1)
            pe.wait_ge(s_out, 8)
            for k in range(NC):
                r = mm(bank[2 + k // 2][:, k % 2 * D:k % 2 * D + D], ost[:, k, :], wout[:, k, :],
                       start=True, stop=True)
            r.then_inc(s_pe, 1)


def slices_back(c, swt, pw):
    nc, a, bank = c.nc, c.a, c.bank
    NC = H0 * G // P
    with ExitStack() as ctx:
        c.stage = ctx

        def sb(name, shape, dt=F32):
            return c.sb(name, shape, dt, ctx)

        bout = sb("bout", [NP_, D])
        ring = sb("sb_ring", [P, 4, NC, NP_])
        sum_ = sb("sb_sum", [NP_, 2, D])
        norm = Norm(c, "n3", ctx)
        s_w = c.sem("sb_s_w")
        s_in = c.sem("sb_s_in")
        s_mm = c.sem("sb_s_mm")
        s_b = c.sem("sb_s_b")
        s_add = c.sem("sb_s_add")
        s_dve = c.sem("sb_s_dve")
        block = ctx.enter_context(nc.Block())

        @block.sync
        def _(sp):
            sp.dma_start(bout[:, :], row_to_all(a["L0_ffn_b_out"], D, NP_)).then_inc(s_w, 16)
            sp.wait_ge(s_w, 16)

        @block.scalar
        def _(act):
            def load(t, u):
                wait(act, s_mm, t - 3)
                nc.scalar.copy(ring[:, u, :, :], swt[:, :, bass.ds(t * NP_, NP_)]).then_inc(s_in, 1)

            each_node_tile(act, load)
            norm.root(act)

        @block.vector
        def _(dve):
            v = nc.vector
            link = Chain(dve, s_dve)
            dve.wait_ge(s_w, 16)

            def add(t, u):
                dve.wait_ge(s_mm, t + 1)
                v.tensor_tensor(sum_[:, u % 2, :], bank[u][0:NP_, 0:D], bout[:, :], ALU.add).then_inc(s_b, 1)
                dve.wait_ge(s_b, t + 1)
                v.tensor_tensor(flat(c.x, t), flat(c.x, t), sum_[:, u % 2, :], ALU.add).then_inc(s_add, 1)
                dve.wait_ge(s_add, t + 1)
                norm.tile(t)

            each_node_tile(dve, add)
            norm.finish(dve, link)

        @block.tensor
        def _(pe):
            def multiply(t, u):
                pe.wait_ge(s_in, t + 1)
                wait(pe, s_b, t - 3)
                for k in range(NC):
                    r = nc.tensor.matmul(bank[u][0:NP_, 0:D], ring[:, u, k, :], pw[:, k, :],
                                         start=k == 0, stop=k == NC - 1)
                r.then_inc(s_mm, 1)

            each_node_tile(pe, multiply)



def second_inputs(c, qk, v1):
    nc, a, bank = c.nc, c.a, c.bank
    QS = float(HC) ** 0.25
    with ExitStack() as ctx:
        c.stage = ctx

        def sb(name, shape, dt=F32):
            return c.sb(name, shape, dt, ctx)

        wy = sb("wy", [P, 2, 2 * P])
        wqkv = sb("wqkv", [P, 2, 3 * D])
        bqkv = sb("bqkv", [NP_, 3 * D])
        tempb = sb("tempb", [NP_, H0])
        f1 = sb("f1", [NP_, 2 * H0])
        f2 = sb("f2", [NP_, 2 * H0])
        zr = sb("si_zr", [NP_, 4, D])
        ztr = sb("si_ztr", [P, 2, 2 * NP_])
        yr = sb("si_yr", [NP_, 4, 2, P])
        sq = sb("si_sq", [NP_, 2, 2 * D])
        ss = sb("si_ss", [NP_, NT, 2 * H0])
        nrm = sb("si_nrm", [NP_, NT, 2 * H0])
        s_zero = c.sem("si_s_zero")
        s_w = c.sem("si_s_w")
        s_in = c.sem("si_s_in")
        s_tp = c.sem("si_s_tp")
        s_ztr = c.sem("si_s_ztr")
        s_mm = c.sem("si_s_mm")
        s_y = c.sem("si_s_y")
        s_yd = [c.sem(f"si_s_yd{u}") for u in range(4)]
        s_qkv = c.sem("si_s_qkv")
        s_sq = c.sem("si_s_sq")
        s_ss = c.sem("si_s_ss")
        s_all = c.sem("si_s_all")
        s_nrm = c.sem("si_s_nrm")
        s_dve = c.sem("si_s_dve")
        block = ctx.enter_context(nc.Block())

        @block.gpsimd
        def _(pool):
            nc.gpsimd.memset(wy[:, :, :], 0.0).then_inc(s_zero, 1)
            nc.gpsimd.memset(v1[:, :, :, 0:1], 1.0)
            nc.gpsimd.memset(f1[:, 0:H0], QS)
            nc.gpsimd.memset(f1[:, H0:], 1.0)
            nc.gpsimd.memset(f2[:, :], QS).then_inc(s_zero, 1)

        @block.sync
        def _(sp):
            sp.dma_start(wqkv[0:MUL, 0, :], a["L1_mix_wqkvt"][0:MUL, :]).then_inc(s_w, 16)
            for d in range(3):
                lo = (1 + d) % 2 * MUL
                src = a["L1_mix_wqkvt"][MUL + d:MUL + d + 3 * MUL - 2:3, :]
                sp.dma_start(wqkv[lo:lo + MUL, (1 + d) // 2, :], src).then_inc(s_w, 16)
            sp.dma_start(bqkv[:, :], row_to_all(a["L1_mix_bqkv"], 3 * D, NP_)).then_inc(s_w, 16)
            sp.dma_start(tempb[:, :], row_to_all(a["L1_mix_temperature"], H0, NP_)).then_inc(s_w, 16)
            sp.wait_ge(s_zero, 1)
            for k, lo, kind in ((0, 0, "s"), (0, MUL, "v"), (1, 0, "v"), (1, MUL, "v")):
                for j, n in enumerate(("w1_", "wsc_")):
                    sp.dma_start(wy[lo:lo + MUL, k, j * P + lo:j * P + lo + MUL],
                                 a["L1_gnn_" + n + kind]).then_inc(s_w, 16)

            def store(t, u):
                sp.wait_ge(s_y, t + 1)
                sp.dma_start(c.y_dram[bass.ds(t * NP_, NP_), :],
                             yr[:, u, :, :].rearrange("p a b -> p (a b)")).then_inc(s_yd[u], 16)

            each_node_tile(sp, store)
            for u in range(4):
                sp.wait_ge(s_yd[u], 16 * (NT // UT + (u == 0)))

        @block.scalar
        def _(act):
            def load(t, u):
                wait(act, s_tp, t - 3)
                opts = dict(bias=column(c.shift, t), scale=column(c.rstd, t))
                nc.scalar.activation(zr[:, u, 0:MUL], flat(c.x, t)[:, 0:MUL], ACT.Identity, **opts)
                nc.scalar.activation(zr[:, u, MUL:D].rearrange("p (d m) -> p d m", d=3),
                                     flat(c.x, t)[:, MUL:D].rearrange("p (m d) -> p d m", d=3),
                                     ACT.Identity, **opts).then_inc(s_in, 1)

            def tile(t, u):
                if not (isinstance(t, int) and t == NT - 1):
                    load(t + 1, (u + 1) % 4)
                act.wait_ge(s_mm, t + 1)
                if isinstance(t, int):
                    if t >= 4:
                        act.wait_ge(s_yd[u], t // 4 * 16)
                else:
                    act.wait_ge(s_yd[u], (t - u) * 4)
                y3 = bank[2 + u % 2][0:NP_, :].rearrange("p (k f) -> p k f", k=2)
                nc.scalar.activation(yr[:, u, :, :], y3[:, :, 0:P], ACT.Copy, scale=MUL ** -0.5)
                nc.scalar.activation(flat(c.z, t).rearrange("p (k f) -> p k f", k=2), y3[:, :, P:2 * P],
                                     ACT.Copy, scale=MUL ** -0.5).then_inc(s_y, 1)
                act.wait_ge(s_qkv, t + 1)
                wait(act, s_ss, t - 1)
                nc.scalar.activation(sq[:, u % 2, :], flat(qk, t), ACT.Square).then_inc(s_sq, 1)

            load(0, 0)
            each_node_tile(act, tile)
            act.wait_ge(s_ss, NT)
            nc.scalar.activation(nrm[:, :, :], ss[:, :, :], ACT.Sqrt).then_inc(s_nrm, 1)

        @block.vector
        def _(dve):
            v = nc.vector
            link = Chain(dve, s_dve)
            dve.wait_ge(s_w, 14 * 16)
            dve.wait_ge(s_zero, 2)
            link(v.tensor_scalar(f2[:, 0:H0], tempb[:, :], QS * QS, None, ALU.mult))

            def turn(t, u):
                dve.wait_ge(s_tp, t + 1)
                wait(dve, s_mm, t - 1)
                v.tensor_copy(ztr[:, u % 2, :], bank[u % 2][:, 0:2 * NP_]).then_inc(s_ztr, 1)

            def reduce(t, u):
                dve.wait_ge(s_sq, t + 1)
                v.reduce_sum(flat(ss, t), sq[:, u % 2, :].rearrange("p (h d) -> p h d", d=HC), X).then_inc(s_ss, 1)

            def tile(t, u):
                if not (isinstance(t, int) and t == NT - 1):
                    turn(t + 1, (u + 1) % 4)
                dve.wait_ge(s_mm, t + 1)
                v.tensor_tensor(flat(qk, t), bank[4 + u % 2][0:NP_, :], bqkv[:, 0:2 * D], ALU.add)
                v.tensor_tensor(v1[:, bass.ds(t, 1), :, 1:].rearrange("p o h d -> p (o h) d"),
                                bank[6 + u % 2][0:NP_, 0:D].rearrange("p (h d) -> p h d", h=H0),
                                bqkv[:, 2 * D:].rearrange("p (h d) -> p h d", h=H0), ALU.add).then_inc(s_qkv, 1)
                if not (isinstance(t, int) and t == 0):
                    reduce(t - 1, (u + 3) % 4)

            turn(0, 0)
            each_node_tile(dve, tile)
            reduce(NT - 1, 0)
            dve.wait_ge(s_nrm, 1)
            shape = [NP_, NT, 2 * H0]
            link(v.tensor_tensor(nrm[:, :, :], nrm[:, :, :], bcast(f1[:, :].unsqueeze(1), shape), ALU.mult))
            link(v.tensor_scalar(nrm[:, :, :], nrm[:, :, :], 1e-12, None, ALU.max))
            link(v.reciprocal(nrm[:, :, :], nrm[:, :, :]))
            link(v.tensor_tensor(nrm[:, :, :], nrm[:, :, :], bcast(f2[:, :].unsqueeze(1), shape), ALU.mult))
            q3 = qk[:, :, :].rearrange("p t (h d) -> p (t h) d", d=HC)
            link(v.tensor_tensor(q3, q3, bcast(nrm[:, :, :].rearrange("p t h -> p (t h)").unsqueeze(2),
                                               [NP_, NT * 2 * H0, HC]), ALU.mult))

        @block.tensor
        def _(pe):
            mm = nc.tensor.matmul
            pe.wait_ge(s_w, 14 * 16)

            def turn(t, u):
                pe.wait_ge(s_in, t + 1)
                wait(pe, s_ztr, t - 1)
                for k in range(2):
                    r = nc.tensor.transpose(bank[u % 2][:, k * NP_:(k + 1) * NP_], zr[:, u, k * P:(k + 1) * P],
                                            c.ident[0:NP_, 0:NP_])
                r.then_inc(s_tp, 1)

            def tile(t, u):
                if not (isinstance(t, int) and t == NT - 1):
                    turn(t + 1, (u + 1) % 4)
                pe.wait_ge(s_ztr, t + 1)
                wait(pe, s_y, t - 1)
                wait(pe, s_qkv, t - 1)
                z = [ztr[:, u % 2, k * NP_:(k + 1) * NP_] for k in range(2)]
                for k in range(2):
                    mm(bank[2 + u % 2][0:NP_, k * D:k * D + D], z[k], wy[:, k, :], start=True, stop=True)
                for b, lo, n in ((4, 0, 2 * D), (6, 2 * D, D)):
                    for k in range(2):
                        r = mm(bank[b + u % 2][0:NP_, 0:n], z[k], wqkv[:, k, lo:lo + n], start=k == 0, stop=k == 1)
                r.then_inc(s_mm, 1)

            turn(0, 0)
            each_node_tile(pe, tile)


def second_mix(c, qk, v1):
    nc, a, bank = c.nc, c.a, c.bank
    A = 0.5
    SC2, SC4 = float(HC) ** 0.5, float(HC)
    NPAIR = HC * HC // 2
    FW = NPAIR + 2 * HC + 1
    NC = -(-FW // P)
    LAST = FW - (NC - 1) * P
    CH = 5
    NCH = NT // CH
    with ExitStack() as ctx:
        c.stage = ctx

        def sb(name, shape, dt=F32):
            return c.sb(name, shape, dt, ctx)

        dbl = [sb(f"dbl{i}", [NP_, CH, 2 * HC]) for i in range(2)]
        feat = [sb(f"feat{i}", [NP_, CH, FW]) for i in range(2)]
        wts = sb("wts", [P, NC])
        m = sb("m2", [P, NC, HC + 1])
        ft = sb("ft", [P, 2, NC * NP_])
        rden = sb("rden", [NP_, 2, CH])
        s_c = c.sem("m2_s_c")
        s_dbl = c.sem("m2_s_dbl")
        s_sqr = c.sem("m2_s_sqr")
        s_feat = c.sem("m2_s_feat")
        s_used = c.sem("m2_s_used")
        s_m = c.sem("m2_s_m")
        s_mc = c.sem("m2_s_mc")
        s_ft = c.sem("m2_s_ft")
        s_ftc = c.sem("m2_s_ftc")
        s_y = c.sem("m2_s_y")
        s_den = c.sem("m2_s_den")
        s_out = c.sem("m2_s_out")
        block = ctx.enter_context(nc.Block())

        def steps(body):
            def run(h):
                for n in range(2 * NCH):
                    body(h, n, n % 2)
            return run

        @block.gpsimd
        def _(pool):
            nc.gpsimd.memset(wts[:, :], 2 * A / N)
            for i in range(2):
                r = nc.gpsimd.memset(feat[i][:, :, FW - 1:FW], 1.0)
            r.then_inc(s_c, 1)
            pool.wait_ge(s_c, 1)
            nc.gpsimd.memset(wts[96:P, NC - 2:NC - 1], A / N)
            nc.gpsimd.memset(wts[0:HC, NC - 1:NC], A / N)
            nc.gpsimd.memset(wts[HC:2 * HC, NC - 1:NC], SC2 / N)
            nc.gpsimd.memset(wts[2 * HC:LAST, NC - 1:NC], SC4 / N).then_inc(s_c, 1)
            pool.wait_ge(s_c, 2)

            def copy(h, n, s):
                i = h * 2 * NCH + n
                wait(pool, s_used, i - 1)
                chunk = n % NCH * CH
                src = qk[:, chunk:chunk + CH, bass.ds(h * HC + (D if n < NCH else 0), HC)]
                nc.gpsimd.tensor_copy(dbl[s][:, :, 0:HC], src)
                nc.gpsimd.tensor_copy(dbl[s][:, :, HC:], src)
                nc.gpsimd.tensor_copy(feat[s][:, :, NPAIR + HC:NPAIR + 2 * HC], src).then_inc(s_dbl, 1)

            run = steps(copy)
            run(0)
            with pool.Fori(1, H0) as h:
                run(h)

        @block.scalar
        def _(act):
            def squares(i, s):
                act.wait_ge(s_dbl, i + 1)
                nc.scalar.activation(feat[s][:, :, NPAIR:NPAIR + HC], dbl[s][:, :, 0:HC], ACT.Square).then_inc(s_sqr, 1)

            def step(h, n, s):
                i = h * 2 * NCH + n
                squares(i, s)
                if n >= NCH:
                    for k in range(CH):
                        q = h * NT + (n - NCH) * CH + k
                        act.wait_ge(s_ft, q + 1)
                        wait(act, s_y, q - 1)
                        b = 2 + 2 * ((n * CH + k) % 2)
                        to = ft[:, (n * CH + k) % 2, :]
                        nc.scalar.copy(to[:, 0:4 * NP_], bank[b][:, 0:4 * NP_])
                        nc.scalar.copy(to[0:LAST, 4 * NP_:], bank[b + 1][0:LAST, 0:NP_]).then_inc(s_ftc, 1)

            run = steps(step)
            run(0)
            with act.Fori(1, H0) as h:
                run(h)

        @block.vector
        def _(dve):
            v = nc.vector
            dve.wait_ge(s_c, 2)

            def products(h, n, s):
                i = h * 2 * NCH + n
                dve.wait_ge(s_dbl, i + 1)
                one, two = dbl[s][:, :, :], feat[s][:, :, 0:NPAIR].rearrange("p t (s d) -> p t s d", d=HC)
                part = list(one.ap[0])
                fixed = bass.AP(tensor=one.tensor, offset=one.offset, ap=[part, [2 * HC, CH], [0, HC // 2], [1, HC]])
                moved = bass.AP(tensor=one.tensor, offset=one.offset + 1,
                                ap=[part, [2 * HC, CH], [1, HC // 2], [1, HC]])
                v.tensor_tensor(two, fixed, moved, ALU.mult).then_inc(s_feat, 1)

            def outputs(h, n):
                g = h * NCH + n
                dve.wait_ge(s_y, (g + 1) * CH)
                y3 = bank[6 + n % 2][0:NP_, 0:CH * (HC + 1)].rearrange("p (t e) -> p t e", t=CH)
                v.reciprocal(rden[:, n % 2, :], y3[:, :, 0]).then_inc(s_den, 1)
                dve.wait_ge(s_den, g + 1)
                v.tensor_tensor(qk[:, n * CH:n * CH + CH, bass.ds(h * HC, HC)], y3[:, :, 1:],
                                bcast(rden[:, n % 2, :].unsqueeze(2), [NP_, CH, HC]), ALU.mult).then_inc(s_out, 1)

            def step(h, n, s):
                products(h, n, s)
                if n == NCH:
                    dve.wait_ge(s_m, h + 1)
                    m3 = bank[0][:, 0:NC * (HC + 1)].rearrange("p (c e) -> p c e", c=NC)
                    w3 = bcast(wts[:, :].unsqueeze(2), [P, NC, HC + 1])
                    for r, k in ((slice(0, P), slice(0, NC - 1)), (slice(0, LAST), slice(NC - 1, NC))):
                        last = v.tensor_tensor(m[r, k, :], m3[r, k, :], w3[r, k, :], ALU.mult)
                    last.then_inc(s_mc, 1)
                if n > NCH:
                    outputs(h, n - NCH - 1)
                if n == 2 * NCH - 1:
                    outputs(h, NCH - 1)

            run = steps(step)
            run(0)
            with dve.Fori(1, H0) as h:
                run(h)

        @block.tensor
        def _(pe):
            mm = nc.tensor.matmul
            E1 = HC + 1

            def cols(k):
                return slice(k * P, min(k * P + P, FW))

            def turn(h, n, k):
                q = h * NT + (n - NCH) * CH + k
                b = 2 + 2 * ((n * CH + k) % 2)
                wait(pe, s_ftc, q - 1)
                f = feat[n % 2]
                for j in range(NC - 1):
                    nc.tensor.transpose(bank[b][:, j * NP_:(j + 1) * NP_], f[:, k, cols(j)], c.ident[0:NP_, 0:NP_])
                nc.tensor.transpose(bank[b + 1][0:LAST, 0:NP_], f[:, k, cols(NC - 1)],
                                    c.ident[0:NP_, 0:NP_]).then_inc(s_ft, 1)

            def query(h, n, k):
                q = h * NT + (n - NCH) * CH + k
                pe.wait_ge(s_ftc, q + 1)
                g = h * NCH + n - NCH
                if k == 0:
                    wait(pe, s_out, g - 1)
                from_ = ft[:, (n * CH + k) % 2, :]
                y = bank[6 + (n - NCH) % 2][0:NP_, k * E1:(k + 1) * E1]
                for j in range(NC - 1):
                    mm(y, from_[:, j * NP_:(j + 1) * NP_], m[:, j, :], start=j == 0, stop=False)
                mm(y, from_[0:LAST, (NC - 1) * NP_:], m[0:LAST, NC - 1, :], start=False, stop=True).then_inc(s_y, 1)

            def step(h, n, s):
                i = h * 2 * NCH + n
                pe.wait_ge(s_feat, i + 1)
                pe.wait_ge(s_sqr, i + 1)
                if n == 0:
                    wait(pe, s_mc, h)
                if n < NCH:
                    for k in range(CH):
                        t = n * CH + k
                        for j in (0, 1, 2, NC - 1, NC - 2):
                            f = feat[s][:, k, cols(j)]
                            w = f.shape[1]
                            r = mm(bank[0][0:w, j * E1:(j + 1) * E1], f,
                                   v1[:, t, bass.ds(h, 1), :].rearrange("p o e -> p (o e)"),
                                   start=n == 0 and k == 0 and j == 0,
                                   stop=n == NCH - 1 and k == CH - 1 and j == NC - 2)
                    r.then_inc(s_used, 1)
                    if n == NCH - 1:
                        pe.wait_ge(s_used, i + 1)
                        pe.sem_inc(s_m, 1)
                else:
                    if n == NCH:
                        pe.wait_ge(s_mc, h + 1)
                    turn(h, n, 0)
                    for k in range(CH):
                        if k + 1 < CH:
                            turn(h, n, k + 1)
                        query(h, n, k)
                    pe.wait_ge(s_y, (h * NCH + n - NCH + 1) * CH)
                    pe.sem_inc(s_used, 1)

            run = steps(step)
            run(0)
            with pe.Fori(1, H0) as h:
                run(h)


def mix_out(c, qk):
    nc, a, bank = c.nc, c.a, c.bank
    with ExitStack() as ctx:
        c.stage = ctx

        def sb(name, shape, dt=F32):
            return c.sb(name, shape, dt, ctx)

        wp = sb("wp", [P, 2, D])
        bp = sb("bp", [NP_, D])
        zr = sb("mo_zr", [NP_, 4, D])
        ztr = sb("mo_ztr", [P, 2, 2 * NP_])
        sum_ = sb("mo_sum", [NP_, 2, D])
        s_w = c.sem("mo_s_w")
        s_in = c.sem("mo_s_in")
        s_tp = c.sem("mo_s_tp")
        s_ztr = c.sem("mo_s_ztr")
        s_mm = c.sem("mo_s_mm")
        s_b = c.sem("mo_s_b")
        block = ctx.enter_context(nc.Block())

        @block.sync
        def _(sp):
            sp.dma_start(wp[:, :, :], a["L1_mix_wprojt"].rearrange("(k p) f -> p k f", p=P)).then_inc(s_w, 16)
            sp.dma_start(bp[:, :], row_to_all(a["L1_mix_bproj"], D, NP_)).then_inc(s_w, 16)
            sp.wait_ge(s_w, 32)

        @block.scalar
        def _(act):
            def load(t, u):
                wait(act, s_tp, t - 3)
                nc.scalar.copy(zr[:, u, :], flat(qk, t)[:, 0:D]).then_inc(s_in, 1)

            each_node_tile(act, load)

        @block.vector
        def _(dve):
            v = nc.vector
            dve.wait_ge(s_w, 32)

            def turn(t, u):
                dve.wait_ge(s_tp, t + 1)
                wait(dve, s_mm, t - 1)
                v.tensor_copy(ztr[:, u % 2, :], bank[u % 2][:, 0:2 * NP_]).then_inc(s_ztr, 1)

            def tile(t, u):
                if not (isinstance(t, int) and t == NT - 1):
                    turn(t + 1, (u + 1) % 4)
                dve.wait_ge(s_mm, t + 1)
                v.tensor_tensor(sum_[:, u % 2, :], bank[2 + u % 2][0:NP_, 0:D], bp[:, :], ALU.add).then_inc(s_b, 1)
                dve.wait_ge(s_b, t + 1)
                v.tensor_tensor(flat(c.x, t), flat(c.x, t), sum_[:, u % 2, :], ALU.add)

            turn(0, 0)
            each_node_tile(dve, tile)

        @block.tensor
        def _(pe):
            def turn(t, u):
                pe.wait_ge(s_in, t + 1)
                wait(pe, s_ztr, t - 1)
                for k in range(2):
                    r = nc.tensor.transpose(bank[u % 2][:, k * NP_:(k + 1) * NP_], zr[:, u, k * P:(k + 1) * P],
                                            c.ident[0:NP_, 0:NP_])
                r.then_inc(s_tp, 1)

            def tile(t, u):
                if not (isinstance(t, int) and t == NT - 1):
                    turn(t + 1, (u + 1) % 4)
                pe.wait_ge(s_ztr, t + 1)
                wait(pe, s_b, t - 1)
                for k in range(2):
                    r = nc.tensor.matmul(bank[2 + u % 2][0:NP_, 0:D], ztr[:, u % 2, k * NP_:(k + 1) * NP_],
                                         wp[:, k, :], start=k == 0, stop=k == 1)
                r.then_inc(s_mm, 1)

            pe.wait_ge(s_w, 32)
            turn(0, 0)
            each_node_tile(pe, tile)



GM = 4
NG = ST // GM
GR = UN // GM


def second_edges(c, acc):
    nc, a, bank = c.nc, c.a, c.bank
    NB = 8
    with ExitStack() as ctx:
        c.stage = ctx

        def sb(name, shape, dt=F32):
            return c.sb(name, shape, dt, ctx)

        rec = c.rec
        idx_ring = [sb(f"e1_idx{h}", [P, HALF], I32) for h in range(2)]
        g = sb("e1_g", [P, UN, D])
        w1 = sb("e1_w1", [GM * NB, 2, P])
        w2 = sb("e1_w2", [P, P])
        w3 = sb("e1_w3", [P, 4 * MUL])
        attr = sb("e1_attr", [P, GR, GM * NB])
        attr_t = sb("e1_attr_t", [GM * NB, GR, P])
        h1 = sb("e1_h1", [P, GR, 2 * P])
        h2 = sb("e1_h2", [P, GR, 2 * P])
        oh = sb("e1_oh", [P, 4, NP_])
        ohs = sb("e1_ohs", [P, 4, 4, NP_])
        prod = sb("e1_prod", [P, 4, AG])
        s_zero = c.sem("e1_s_zero")
        s_w = c.sem("e1_s_w")
        s_w3 = c.sem("e1_s_w3")
        s_rec = c.sem("e1_s_rec")
        s_ring = c.sem("e1_s_ring")
        s_got = c.s_got
        s_at = c.sem("e1_s_at")
        s_tp = c.sem("e1_s_tp")
        s_att = c.sem("e1_s_att")
        s_l1 = c.sem("e1_s_l1")
        s_h1 = c.sem("e1_s_h1")
        s_l2 = c.sem("e1_s_l2")
        s_h2 = c.sem("e1_s_h2")
        s_wt = c.sem("e1_s_wt")
        s_oh = c.sem("e1_s_oh")
        s_ohs = c.sem("e1_s_ohs")
        s_prod = c.sem("e1_s_prod")
        s_agg = c.sem("e1_s_agg")
        s_acc = c.sem("e1_s_acc")
        block = ctx.enter_context(nc.Block())

        def rounds(engine, body):
            for u in range(UN):
                body(0, u, False)
            with engine.Fori(1, ST // UN - 1) as i:
                for u in range(UN):
                    body(i, u, False)
            for u in range(UN):
                body(ST // UN - 1, u, True)

        @block.sync
        def _(sp):
            sp.dma_start(rec[:, :, :], c.rec_dram.rearrange("(p j) f -> p j f", p=P)).then_inc(s_rec, 16)
            for h in range(2):
                sp.dma_start(w3[h * MUL:h * MUL + MUL, :], a["L1_gnn_fc_w3"]).then_inc(s_w, 16)
            sp.wait_ge(s_zero, 2)
            for q in range(2):
                sp.dma_start(w2[q * MUL:q * MUL + MUL, q * MUL:q * MUL + MUL], a["L1_gnn_fc_w2"]).then_inc(s_w, 16)
            for j in range(GM):
                lo = j % 2 * MUL
                sp.dma_start(w1[j * NB:j * NB + NB, j // 2, lo:lo + MUL], a["L1_gnn_fc_w1"]).then_inc(s_w, 16)
            sp.wait_ge(s_w, 8 * 16)

        @block.gpsimd
        def _(pool):
            nc.gpsimd.memset(w1[:, :, :], 0.0).then_inc(s_zero, 1)
            nc.gpsimd.memset(w2[:, :], 0.0).then_inc(s_zero, 1)
            pool.wait_ge(s_rec, 16)
            gather_rows(c, pool, c.y_dram, idx_ring, [g[:, u, :] for u in range(UN)], s_ring, s_prod, s_got, rec)

        @block.scalar
        def _(act):
            def attributes(g_, k):
                nc.scalar.copy(attr[:, k % GR, :].rearrange("p (j b) -> p j b", j=GM),
                               rec[:, bass.ds(g_ * GM, GM), R_ATTR:R_ATTR + NB]).then_inc(s_at, 1)

            def turned(g_, k):
                act.wait_ge(s_tp, g_ + 1)
                nc.scalar.copy(attr_t[:, k % GR, :], bank[0][0:GM * NB, 0:P]).then_inc(s_att, 1)

            def layer1(g_, k):
                act.wait_ge(s_l1, g_ + 1)
                nc.scalar.activation(h1[:, k % GR, :], bank[0][:, P:3 * P], ACT.Silu,
                                     scale=float(NB) ** -0.5).then_inc(s_h1, 1)

            def layer2(g_, k):
                act.wait_ge(s_l2, g_ + 1)
                nc.scalar.activation(h2[:, k % GR, :], bank[1][:, 0:2 * P], ACT.Silu,
                                     scale=float(MUL) ** -0.5).then_inc(s_h2, 1)

            def scaled(j, u):
                act.wait_ge(s_oh, j + 1)
                wait(act, s_agg, j - 3)
                for d in range(4):
                    r = nc.scalar.activation(ohs[:, u % 4, d, :], oh[:, u % 4, :], ACT.Copy,
                                             scale=flat(rec, j)[:, R_SH + d:R_SH + d + 1])
                r.then_inc(s_ohs, 1)

            def tile(i, u, last):
                j, g_, k, at = i * UN + u, i * GR + u // GM, u // GM, u % GM
                left = NG - 1 - g_ if last else GR
                if at == 0 and left >= 1:
                    layer2(g_ + 1, k + 1)
                if at == 1 and left >= 2:
                    attributes(g_ + 2, k + 2)
                if at == 2 and left >= 2:
                    turned(g_ + 2, k + 2)
                if at == 3 and left >= 2:
                    layer1(g_ + 2, k + 2)
                if not (last and u == UN - 1):
                    scaled(j + 1, u + 1)

            act.wait_ge(s_rec, 16)
            attributes(0, 0)
            attributes(1, 1)
            turned(0, 0)
            layer1(0, 0)
            layer2(0, 0)
            turned(1, 1)
            layer1(1, 1)
            scaled(0, 0)
            rounds(act, tile)

        @block.vector
        def _(dve):
            v = nc.vector
            v.memset(acc[:, :, :], 0.0).then_inc(s_acc, 1)
            dve.wait_ge(s_w, 8 * 16)
            v.tensor_scalar(w3[:, 0:3 * MUL], w3[:, 0:3 * MUL], MUL ** -0.5, None, ALU.mult)
            v.tensor_scalar(w3[:, 3 * MUL:], w3[:, 3 * MUL:], MUL ** -0.5 * 0.5773502691896258, None,
                            ALU.mult).then_inc(s_w3, 1)
            dve.wait_ge(s_rec, 16)

            def one_hot(j, u):
                wait(dve, s_ohs, j - 3)
                v.tensor_scalar(oh[:, u % 4, :], c.iota[:, :], flat(rec, j)[:, R_LOCAL:R_LOCAL + 1], None,
                                ALU.is_equal).then_inc(s_oh, 1)

            def products(i, j, u):
                dve.wait_ge(s_wt, j + 1)
                dve.wait_ge(s_got[u % UN], (i + ST // UN) * 16 + 16)
                w, y, to = bank[2 + u % 2], g[:, u % UN, :], prod[:, u % 4, :]
                v.tensor_tensor(to.rearrange("p (b f) -> p b f", b=2)[:, :, 0:MUL],
                                w[:, 0:2 * MUL].rearrange("p (b f) -> p b f", b=2),
                                bcast(y[:, 0:MUL].unsqueeze(1), [P, 2, MUL]), ALU.mult)
                v.tensor_tensor(to.rearrange("p (b d f) -> p b d f", b=2, d=4)[:, :, 1:, :],
                                bcast(w[:, 2 * MUL:4 * MUL].rearrange("p (b f) -> p b f", b=2).unsqueeze(2),
                                      [P, 2, 3, MUL]),
                                bcast(y[:, MUL:D].rearrange("p (d f) -> p d f", d=3).unsqueeze(1), [P, 2, 3, MUL]),
                                ALU.mult).then_inc(s_prod, 1)

            def tile(i, u, last):
                j = i * UN + u
                b = dve.value_load(c.bucket_of[0:1, bass.ds(j, 1)], min_val=0, max_val=NT)
                if not (last and u >= UN - 2):
                    one_hot(j + 2, u + 2)
                if not (last and u == UN - 1):
                    products(i + (u + 1) // UN, j + 1, u + 1)
                dve.wait_ge(s_agg, j + 1)
                dve.wait_ge(s_acc, j + 1)
                v.tensor_tensor(flat(acc, b), flat(acc, b), bank[4 + u % 4][0:NP_, :], ALU.add).then_inc(s_acc, 1)

            one_hot(0, 0)
            one_hot(1, 1)
            products(0, 0, 0)
            rounds(dve, tile)

        @block.tensor
        def _(pe):
            mm = nc.tensor.matmul

            def turn(g_, k):
                pe.wait_ge(s_at, g_ + 1)
                wait(pe, s_h1, g_)
                nc.tensor.transpose(bank[0][0:GM * NB, 0:P], attr[:, k % GR, :], c.ident[:, :]).then_inc(s_tp, 1)

            def layer1(g_, k):
                pe.wait_ge(s_att, g_ + 1)
                for q in range(2):
                    r = mm(bank[0][:, (1 + q) * P:(2 + q) * P], w1[:, q, :], attr_t[:, k % GR, :],
                           start=True, stop=True)
                r.then_inc(s_l1, 1)

            def layer2(g_, k):
                pe.wait_ge(s_h1, g_ + 1)
                wait(pe, s_h2, g_)
                mm(bank[1][:, 0:2 * P], w2[:, :], h1[:, k % GR, :], start=True, stop=True).then_inc(s_l2, 1)

            def weights(g_, j, u):
                pe.wait_ge(s_h2, g_ + 1)
                wait(pe, s_prod, j - 1)
                half, pair = slice(u % 2 * MUL, u % 2 * MUL + MUL), u % GM // 2
                mm(bank[2 + u % 2][:, 0:4 * MUL], h2[half, u // GM % GR, pair * P:pair * P + P], w3[half, :],
                   start=True, stop=True).then_inc(s_wt, 1)

            def sums(j, u):
                pe.wait_ge(s_prod, j + 1)
                pe.wait_ge(s_ohs, j + 1)
                wait(pe, s_acc, j - 2)
                p4 = prod[:, u % 4, :]
                to = bank[4 + u % 4][0:NP_, :]
                mm(to[:, MUL:5 * MUL], ohs[:, u % 4, 0, :], p4[:, 0:4 * MUL], start=True, stop=False)
                for d in range(3):
                    by = ohs[:, u % 4, 1 + d, :]
                    mm(to[:, (5 + d) * MUL:(6 + d) * MUL], by, p4[:, 4 * MUL:5 * MUL], start=False, stop=False)
                    r = mm(to[:, 0:MUL], by, p4[:, (5 + d) * MUL:(6 + d) * MUL], start=False, stop=d == 2)
                r.then_inc(s_agg, 1)

            def tile(i, u, last):
                j, g_, k, at = i * UN + u, i * GR + u // GM, u // GM, u % GM
                left = NG - 1 - g_ if last else GR
                if at == 0 and left >= 1:
                    layer2(g_ + 1, k + 1)
                if at == 2 and left >= 2:
                    turn(g_ + 2, k + 2)
                if at == 3 and left >= 2:
                    layer1(g_ + 2, k + 2)
                if not (last and u >= UN - 2):
                    weights(i * GR + (u + 2) // GM, j + 2, u + 2)
                sums(j, u)

            pe.wait_ge(s_w3, 1)
            turn(0, 0)
            layer1(0, 0)
            layer2(0, 0)
            turn(1, 1)
            layer1(1, 1)
            weights(0, 0, 0)
            weights(0, 1, 1)
            rounds(pe, tile)


def second_nodes(c, acc):
    nc, a, bank = c.nc, c.a, c.bank
    with ExitStack() as ctx:
        c.stage = ctx

        def sb(name, shape, dt=F32):
            return c.sb(name, shape, dt, ctx)

        w2 = sb("sn_w2", [P, 2, MUL])
        gain = sb("sn_gain", [NP_, D])
        dn = sb("sn_dn", [NP_, NT])
        root = sb("sn_root", [NP_, NT])
        rows_in = sb("sn_rows", [NP_, 4, AG])
        cols_in = sb("sn_cols", [P, 2, 4 * NP_])
        junk = sb("sn_junk", [NP_, D])
        ss = sb("sn_ss", [NP_, NT, 2])
        rms = sb("sn_rms", [NP_, NT, 2])
        norm = Norm(c, "n4", ctx)
        s_w = c.sem("sn_s_w")
        s_dn = c.sem("sn_s_dn")
        s_root = c.sem("sn_s_root")
        s_in = c.sem("sn_s_in")
        s_tp = c.sem("sn_s_tp")
        s_cols = c.sem("sn_s_cols")
        s_mm = c.sem("sn_s_mm")
        s_add = c.sem("sn_s_add")
        s_ss = c.sem("sn_s_ss")
        s_ms = c.sem("sn_s_ms")
        s_rms = c.sem("sn_s_rms")
        s_dve = c.sem("sn_s_dve")
        block = ctx.enter_context(nc.Block())

        @block.sync
        def _(sp):
            sp.dma_start(w2[0:MUL, 0, :], a["L1_gnn_w2_s"][MUL:, :]).then_inc(s_w, 16)
            sp.dma_start(w2[MUL:P, 0, :], a["L1_gnn_w2_s"][0:MUL, :]).then_inc(s_w, 16)
            sp.dma_start(w2[:, 1, :], a["L1_gnn_w2_v"]).then_inc(s_w, 16)
            sp.dma_start(gain[:, 0:MUL], row_to_all(a["L1_gnn_g_s"], MUL, NP_)).then_inc(s_w, 16)
            for d in range(3):
                sp.dma_start(gain[:, (1 + d) * MUL:(2 + d) * MUL], row_to_all(a["L1_gnn_g_v"], MUL, NP_)).then_inc(s_w, 16)
            sp.wait_ge(s_w, 7 * 16)

        @block.scalar
        def _(act):
            act.wait_ge(s_dn, 1)
            nc.scalar.activation(root[:, :], root[:, :], ACT.Sqrt).then_inc(s_root, 1)
            act.wait_ge(s_dn, 2)

            def load(t, u):
                wait(act, s_tp, t - 3)
                src, to = flat(acc, t), rows_in[:, u, :]
                to3 = to[:, P:].rearrange("p (d f) -> p d f", d=3)
                by = column(dn, t)
                nc.scalar.activation(to[:, 0:P], src[:, 0:P], ACT.Copy, scale=by)
                nc.scalar.activation(to3[:, :, 0:MUL], src[:, 5 * MUL:].rearrange("p (d f) -> p d f", d=3),
                                     ACT.Copy, scale=by)
                nc.scalar.activation(to3[:, :, MUL:], src[:, 2 * MUL:5 * MUL].rearrange("p (d f) -> p d f", d=3),
                                     ACT.Copy, scale=by).then_inc(s_in, 1)

            def tile(t, u):
                if not (isinstance(t, int) and t == NT - 1):
                    load(t + 1, (u + 1) % 4)
                act.wait_ge(s_add, t + 1)
                for k, lo, hi in ((0, 0, MUL), (1, MUL, D)):
                    if k == 0:
                        wait(act, s_ss, t)
                    r = nc.scalar.activation(junk[:, lo:hi], flat(c.z, t)[:, lo:hi], ACT.Square,
                                             accum_out=flat(ss, t)[:, k:k + 1])
                r.then_inc(s_ss, 1)

            load(0, 0)
            each_node_tile(act, tile)
            act.wait_ge(s_ms, 1)
            nc.scalar.activation(rms[:, :, :], rms[:, :, :], ACT.Sqrt).then_inc(s_rms, 1)
            norm.root(act)

        @block.vector
        def _(dve):
            v = nc.vector
            link = Chain(dve, s_dve)
            v.tensor_scalar(root[:, :], c.deg[:, :], 1.0, None, ALU.max).then_inc(s_dn, 1)
            dve.wait_ge(s_w, 7 * 16)
            link(v.tensor_scalar(w2[:, :, :], w2[:, :, :], (2.0 * MUL) ** -0.5, None, ALU.mult))
            dve.wait_ge(s_root, 1)
            v.reciprocal(dn[:, :], root[:, :]).then_inc(s_dn, 1)

            def turn(t, u):
                dve.wait_ge(s_tp, t + 1)
                wait(dve, s_mm, t - 1)
                v.tensor_copy(cols_in[:, u % 2, :], bank[u % 2][:, 0:4 * NP_]).then_inc(s_cols, 1)

            def tile(t, u):
                if not (isinstance(t, int) and t == NT - 1):
                    turn(t + 1, (u + 1) % 4)
                dve.wait_ge(s_mm, t + 1)
                v.tensor_tensor(flat(c.z, t), flat(c.z, t), bank[2 + u % 2][0:NP_, 0:D], ALU.add).then_inc(s_add, 1)

            turn(0, 0)
            each_node_tile(dve, tile)
            dve.wait_ge(s_ss, NT)
            link(v.tensor_scalar(rms[:, :, 0], ss[:, :, 0], 1.0 / MUL, EPS, ALU.mult, ALU.add))
            v.tensor_scalar(rms[:, :, 1], ss[:, :, 1], 1.0 / (3 * MUL), EPS, ALU.mult, ALU.add).then_inc(s_ms, 1)
            dve.wait_ge(s_rms, 1)
            link(v.reciprocal(rms[:, :, :], rms[:, :, :]))
            for k, lo, hi in ((0, 0, MUL), (1, MUL, D)):
                z3 = c.z[:, :, lo:hi]
                link(v.tensor_tensor(z3, z3, bcast(rms[:, :, k:k + 1], [NP_, NT, hi - lo]), ALU.mult))
            link(v.tensor_tensor(c.z[:, :, :], c.z[:, :, :], bcast(gain[:, :].unsqueeze(1), [NP_, NT, D]), ALU.mult))
            v.tensor_tensor(c.x[:, :, 0:MUL], c.x[:, :, 0:MUL], c.z[:, :, 0:MUL], ALU.add)
            x4 = c.x[:, :, MUL:].rearrange("p t (m d) -> p t d m", d=3)
            link(v.tensor_tensor(x4, x4, c.z[:, :, MUL:].rearrange("p t (d m) -> p t d m", d=3), ALU.add))
            with dve.Fori(0, NT) as t:
                norm.tile(t)
            norm.finish(dve, link)

        @block.tensor
        def _(pe):
            def turn(t, u):
                pe.wait_ge(s_in, t + 1)
                wait(pe, s_cols, t - 1)
                for k in range(4):
                    r = nc.tensor.transpose(bank[u % 2][:, k * NP_:(k + 1) * NP_],
                                            rows_in[:, u, k * P:(k + 1) * P], c.ident[0:NP_, 0:NP_])
                r.then_inc(s_tp, 1)

            def tile(t, u):
                if not (isinstance(t, int) and t == NT - 1):
                    turn(t + 1, (u + 1) % 4)
                pe.wait_ge(s_cols, t + 1)
                wait(pe, s_add, t - 1)
                for k in range(4):
                    r = nc.tensor.matmul(bank[2 + u % 2][0:NP_, k * MUL:(k + 1) * MUL],
                                         cols_in[:, u % 2, k * NP_:(k + 1) * NP_], w2[:, min(k, 1), :],
                                         start=True, stop=True)
                r.then_inc(s_mm, 1)

            pe.wait_ge(s_dn, 2)
            turn(0, 0)
            each_node_tile(pe, tile)


NE, FH = 8, 512
MG = 4
GROUPS = [(t, min(MG, NT - t)) for t in range(0, NT, MG)]


def route(c, z4t, wfull):
    nc, a, bank = c.nc, c.a, c.bank
    with ExitStack() as ctx:
        c.stage = ctx

        def sb(name, shape, dt=F32):
            return c.sb(name, shape, dt, ctx)

        gamma = sb("gamma", [P, 2])
        beta = sb("beta", [P, 2])
        wr = sb("wr", [P, 2, NE])
        br = sb("br", [NE, 1])
        b2 = sb("b2", [NE, D])
        zr = sb("ro_zr", [NP_, 4, D])
        lgt = sb("ro_lgt", [NE, N])
        lg = sb("ro_lg", [NP_, NT, NE])
        gt = sb("ro_gt", [NP_, NT, NE, NE])
        eq = sb("ro_eq", [NP_, NT, NE, NE])
        earlier = sb("ro_earlier", [P, NE, NE])
        mx = sb("ro_mx", [NP_, NT])
        rank = sb("ro_rank", [NP_, NT, NE])
        ex = sb("ro_ex", [NP_, NT, NE])
        tot = sb("ro_tot", [NP_, NT])
        inv = sb("ro_inv", [NP_, NT])
        wt = sb("ro_wt", [NE, N])
        s_w = c.sem("ro_s_w")
        s_one = c.sem("ro_s_one")
        s_in = c.sem("ro_s_in")
        s_tp = c.sem("ro_s_tp")
        s_z = c.sem("ro_s_z")
        s_lg = c.sem("ro_s_lg")
        s_lgt = c.sem("ro_s_lgt")
        s_back = c.sem("ro_s_back")
        s_sub = c.sem("ro_s_sub")
        s_exp = c.sem("ro_s_exp")
        s_wf = c.sem("ro_s_wf")
        s_wtp = c.sem("ro_s_wtp")
        s_wt = c.sem("ro_s_wt")
        s_b2 = c.sem("ro_s_b2")
        s_add = c.sem("ro_s_add")
        s_dve = c.sem("ro_s_dve")
        block = ctx.enter_context(nc.Block())
        SIX = [(n, min(4 * NP_, N - n)) for n in range(0, N, 4 * NP_)]

        @block.gpsimd
        def _(pool):
            nc.gpsimd.memset(earlier[:, :, :], 1.0).then_inc(s_one, 1)
            pool.wait_ge(s_one, 1)
            nc.gpsimd.affine_select(out=earlier[:, :, :], in_=earlier[:, :, :], compare_op=ALU.is_gt, fill=0.0,
                                    base=0, pattern=[[1, NE], [-1, NE]], channel_multiplier=0).then_inc(s_one, 1)

        @block.sync
        def _(sp):
            with nc.allow_non_contiguous_dma("one column per chunk"):
                for k in range(2):
                    sp.dma_start(gamma[:, k:k + 1], a["L1_ffn_gamma"][k * P:k * P + P].unsqueeze(1)).then_inc(s_w, 16)
                    sp.dma_start(beta[:, k:k + 1], a["L1_ffn_beta"][k * P:k * P + P].unsqueeze(1)).then_inc(s_w, 16)
                sp.dma_start(br[:, :], a["L1_ffn_br"].unsqueeze(1)).then_inc(s_w, 16)
            sp.dma_start(wr[:, :, :], a["L1_ffn_Wr"].rearrange("(k p) e -> p k e", p=P)).then_inc(s_w, 16)
            sp.dma_start(b2[:, :], a["L1_ffn_b2"]).then_inc(s_w, 16)
            sp.wait_ge(s_w, 7 * 16)

        @block.scalar
        def _(act):
            def load(t, u):
                wait(act, s_tp, t - 3)
                nc.scalar.activation(zr[:, u, :], flat(c.x, t), ACT.Identity, bias=column(c.shift, t),
                                     scale=column(c.rstd, t)).then_inc(s_in, 1)

            each_node_tile(act, load)
            act.wait_ge(s_sub, 1)
            nc.scalar.activation(ex[:, :, :], lg[:, :, :], ACT.Exp).then_inc(s_exp, 1)

        @block.vector
        def _(dve):
            v = nc.vector
            link = Chain(dve, s_dve)
            dve.wait_ge(s_w, 7 * 16)
            dve.wait_ge(s_one, 2)

            def tile(t, u):
                dve.wait_ge(s_tp, t + 1)
                for k in range(2):
                    r = v.tensor_scalar(z4t[:, k, bass.ds(t * NP_, NP_)], bank[u % 2][:, k * NP_:(k + 1) * NP_],
                                        gamma[:, k:k + 1], beta[:, k:k + 1], ALU.mult, ALU.add)
                r.then_inc(s_z, 1)

            each_node_tile(dve, tile)
            for i, (n, w) in enumerate(SIX):
                dve.wait_ge(s_lg, i + 1)
                v.tensor_scalar(lgt[:, n:n + w], bank[2 + i % 2][0:NE, 0:w], br[:, 0:1], None, ALU.add).then_inc(s_lgt, 1)
            dve.wait_ge(s_back, 1)
            link(v.tensor_copy(lg[:, :, :].rearrange("p t e -> p (t e)"), bank[4][0:NP_, 0:NT * NE]))
            full = [NP_, NT, NE, NE]
            mine, other = bcast(lg[:, :, :].unsqueeze(3), full), bcast(lg[:, :, :].unsqueeze(2), full)
            v.tensor_tensor(gt[:, :, :, :], other, mine, ALU.is_gt)
            link(v.tensor_tensor(eq[:, :, :, :], other, mine, ALU.is_equal))
            e3 = eq[:, :, :, :].rearrange("p t a b -> p t (a b)")
            link(v.tensor_tensor(e3, e3, bcast(earlier[0:NP_, :, :].rearrange("p a b -> p (a b)").unsqueeze(1),
                                               [NP_, NT, NE * NE]), ALU.mult))
            link(v.tensor_tensor(gt[:, :, :, :], gt[:, :, :, :], eq[:, :, :, :], ALU.add))
            v.tensor_reduce(mx[:, :], lg[:, :, :], X, ALU.max)
            link(v.reduce_sum(rank[:, :, :], gt[:, :, :, :], X))
            v.tensor_tensor(lg[:, :, :], lg[:, :, :], bcast(mx[:, :].unsqueeze(2), [NP_, NT, NE]),
                            ALU.subtract).then_inc(s_sub, 1)
            dve.wait_ge(s_exp, 1)
            link(v.tensor_scalar(rank[:, :, :], rank[:, :, :], 2.0, None, ALU.is_lt))
            link(v.tensor_tensor(ex[:, :, :], ex[:, :, :], rank[:, :, :], ALU.mult))
            link(v.reduce_sum(tot[:, :], ex[:, :, :], X))
            link(v.reciprocal(inv[:, :], tot[:, :]))
            v.tensor_tensor(wfull[:, :, :], ex[:, :, :], bcast(inv[:, :].unsqueeze(2), [NP_, NT, NE]),
                            ALU.mult).then_inc(s_wf, 1)
            for i, (n, w) in enumerate(SIX):
                dve.wait_ge(s_wtp, i + 1)
                v.tensor_copy(wt[:, n:n + w], bank[5 + i % 2][0:NE, 0:w]).then_inc(s_wt, 1)
            for t in range(NT):
                dve.wait_ge(s_b2, t + 1)
                v.tensor_tensor(c.x[:, t, :], c.x[:, t, :], bank[t % 4][0:NP_, 0:D], ALU.add).then_inc(s_add, 1)

        @block.tensor
        def _(pe):
            def turn(t, u):
                pe.wait_ge(s_in, t + 1)
                wait(pe, s_z, t - 1)
                for k in range(2):
                    r = nc.tensor.transpose(bank[u % 2][:, k * NP_:(k + 1) * NP_], zr[:, u, k * P:(k + 1) * P],
                                            c.ident[0:NP_, 0:NP_])
                r.then_inc(s_tp, 1)

            each_node_tile(pe, turn)
            pe.wait_ge(s_z, NT)
            pe.wait_ge(s_w, 7 * 16)
            for i, (n, w) in enumerate(SIX):
                wait(pe, s_lgt, i - 1)
                for k in range(2):
                    r = nc.tensor.matmul(bank[2 + i % 2][0:NE, 0:w], wr[:, k, :], z4t[:, k, n:n + w],
                                         start=k == 0, stop=k == 1)
                r.then_inc(s_lg, 1)
            pe.wait_ge(s_lgt, len(SIX))
            for t in range(NT):
                r = nc.tensor.transpose(bank[4][0:NP_, t * NE:(t + 1) * NE], lgt[:, t * NP_:(t + 1) * NP_],
                                        c.ident[0:NE, 0:NE])
            r.then_inc(s_back, 1)
            pe.wait_ge(s_wf, 1)
            for i, (n, w) in enumerate(SIX):
                wait(pe, s_wt, i - 1)
                for t in range(n // NP_, (n + w) // NP_):
                    r = nc.tensor.transpose(bank[5 + i % 2][0:NE, t * NP_ - n:(t + 1) * NP_ - n], wfull[:, t, :],
                                            c.ident[0:NP_, 0:NP_])
                r.then_inc(s_wtp, 1)
            pe.wait_ge(s_wt, len(SIX))
            for t in range(NT):
                wait(pe, s_add, t - 3)
                nc.tensor.matmul(bank[t % 4][0:NP_, 0:D], wt[:, t * NP_:(t + 1) * NP_], b2[:, :],
                                 start=True, stop=True).then_inc(s_b2, 1)


def experts(c, z4t, wfull):
    nc, a, bank = c.nc, c.a, c.bank
    KD, KH = D // P, FH // P
    with ExitStack() as ctx:
        c.stage = ctx

        def sb(name, shape, dt=F32):
            return c.sb(name, shape, dt, ctx)

        w1 = sb("ex_w1", [P, 2, KD, FH])
        w2 = sb("ex_w2", [P, 2, KH, D])
        b1 = sb("ex_b1", [P, 2, KH])
        h = sb("ex_h", [P, 2, KH, MG * NP_])
        s_w = [c.sem(f"ex_s_w{s}") for s in range(2)]
        s_h = c.sem("ex_s_h")
        s_gelu = c.sem("ex_s_gelu")
        s_y = c.sem("ex_s_y")
        s_add = c.sem("ex_s_add")
        s_out = c.sem("ex_s_out")
        block = ctx.enter_context(nc.Block())
        n_groups = len(GROUPS)

        def each_expert(engine, body):
            body(0, 0)
            body(1, 1)
            with engine.Fori(1, NE // 2) as i:
                body(i * 2, 0)
                body(i * 2 + 1, 1)

        @block.sync
        def _(sp):
            def load(e, s):
                wait(sp, s_y, (e - 1) * NT)
                sp.dma_start(b1[:, s, :], a["L1_ffn_b1t"][:, bass.ds(e * KH, KH)]).then_inc(s_w[s], 16)
                sp.dma_start(w1[:, s, :, :], a["L1_ffn_W1"][bass.ds(e * D, D), :].rearrange("(k p) f -> p k f", p=P))\
                  .then_inc(s_w[s], 16)
                sp.dma_start(w2[:, s, :, :], a["L1_ffn_W2"][bass.ds(e * FH, FH), :].rearrange("(k p) f -> p k f", p=P))\
                  .then_inc(s_w[s], 16)

            each_expert(sp, load)
            sp.wait_ge(s_add, NE * NT)
            sp.dma_start(rows(c.out), c.x[:, :, :]).then_inc(s_out, 16)
            sp.wait_ge(s_out, 16)

        @block.scalar
        def _(act):
            def expert(e, s):
                act.wait_ge(s_w[s], e * 24 + 48 - s * 24)
                for i, (t, n) in enumerate(GROUPS):
                    g_ = e * n_groups + i
                    wait(act, s_y, e * NT + (t - MG if i else -1))
                    for k in range(KH):
                        q = g_ * KH + k
                        act.wait_ge(s_h, q + 1)
                        nc.scalar.activation(h[:, (i + s) % 2, k, 0:n * NP_], bank[k][:, 0:n * NP_], ACT.Gelu,
                                             bias=b1[:, s, k:k + 1])\
                          .then_inc(s_gelu, 1)

            each_expert(act, expert)

        @block.vector
        def _(dve):
            def expert(e, s):
                for t in range(NT):
                    dve.wait_ge(s_y, e * NT + t + 1)
                    wait(dve, s_add, e * NT + t - NT + 1)
                    nc.vector.scalar_tensor_tensor(
                        out=c.x[:, t, :], in0=bank[4 + t % 4][0:NP_, 0:D],
                        scalar=wfull[:, t, bass.ds(e, 1)], in1=c.x[:, t, :], op0=ALU.mult, op1=ALU.add)\
                      .then_inc(s_add, 1)

            each_expert(dve, expert)

        @block.tensor
        def _(pe):
            mm = nc.tensor.matmul

            def hidden(e, s, i):
                t, n = GROUPS[i]
                for k in range(KH):
                    wait(pe, s_gelu, (e * n_groups + i - 1) * KH + k + 1)
                    for j in range(KD):
                        r = mm(bank[k][:, 0:n * NP_], w1[:, s, j, k * P:k * P + P], z4t[:, j, t * NP_:(t + n) * NP_],
                               start=j == 0, stop=j == KD - 1)
                    r.then_inc(s_h, 1)

            def output(e, s, i):
                t0, n = GROUPS[i]
                pe.wait_ge(s_gelu, (e * n_groups + i + 1) * KH)
                for t in range(t0, t0 + n):
                    back = 4 if t >= 4 else (1 if t == 0 else 4)
                    wait(pe, s_add, e * NT + t - back + 1)
                    for k in range(KH):
                        r = mm(bank[4 + t % 4][0:NP_, 0:D], h[:, (i + s) % 2, k, (t - t0) * NP_:(t - t0 + 1) * NP_],
                               w2[:, s, k, :], start=k == 0, stop=k == KH - 1)
                    r.then_inc(s_y, 1)

            def expert(e, s):
                pe.wait_ge(s_w[s], e * 24 + 48 - s * 24)
                hidden(e, s, 0)
                for i in range(n_groups):
                    if i + 1 < n_groups:
                        hidden(e, s, i + 1)
                    output(e, s, i)

            each_expert(pe, expert)


def build(nc, args, out):
    with ExitStack() as ctx:
        c = Core(nc, ctx, args, out)
        sort_and_first_norm(c)
        c.deg = c.sb("deg", [NP_, NT])
        with ExitStack() as graph:
            c.rec = c.sb("rec", [P, ST, RF], F32, graph)
            acc = c.sb("acc0", [NP_, NT + 1, D + 1], F32, graph)
            first_edges(c, acc)
            combine_first(c, acc)
        with ExitStack() as slices:
            swt = c.sb("swt", [P, 4, N], F32, slices)
            tokens = c.sb("tokens", [P, 4, D + 1], F32, slices)
            pw = c.sb("pw", [P, 4, D], F32, slices)
            slice_weights(c, swt, tokens)
            slice_attention(c, tokens, pw)
            slices_back(c, swt, pw)
        c.clear_stages()
        with ExitStack() as mix:
            qk = c.sb("qk", [NP_, NT, 2 * D], F32, mix)
            v1 = c.sb("v1", [NP_, NT, H0, HC + 1], F32, mix)
            second_inputs(c, qk, v1)
            second_mix(c, qk, v1)
            mix_out(c, qk)
        with ExitStack() as graph:
            c.rec = c.sb("rec2", [P, ST, RF], F32, graph)
            acc = c.sb("acc1", [NP_, NT + 1, AG], F32, graph)
            second_edges(c, acc)
            second_nodes(c, acc)
        with ExitStack() as ffn:
            z4t = c.sb("z4t", [P, 2, N], F32, ffn)
            wfull = c.sb("wfull", [NP_, NT, NE], F32, ffn)
            route(c, z4t, wfull)
            experts(c, z4t, wfull)


def kernel(**inputs):
    import concourse.bacc as bacc
    from concourse.bass_utils import run_bass_kernel_spmd

    def cols(v):
        n = (ET - 1) * P
        return (np.ascontiguousarray(np.swapaxes(v[:n].reshape((ET - 1, P) + v.shape[1:]), 0, 1)),
                np.ascontiguousarray(v[n:]))

    given = {k: np.asarray(v) for k, v in inputs.items()}
    rec = np.concatenate([given["edge_weight"][:, None], given["edge_attr_4"],
                          np.zeros((E, 2), np.float32), np.ones((E, 1), np.float32), given["edge_attr_8"]], axis=1)
    arrays = {"x": given["x"]}
    arrays["L0_ffn_wxt"] = np.concatenate([given["L0_ffn_W_x"].T, given["L0_ffn_b_x"][:, None]], axis=1)
    arrays["L1_ffn_W1"] = given["L1_ffn_W1"].reshape(NE * D, FH)
    arrays["L1_ffn_W2"] = given["L1_ffn_W2"].reshape(NE * FH, D)
    arrays["L1_ffn_b1t"] = np.ascontiguousarray(given["L1_ffn_b1"].reshape(NE, FH // P, P).transpose(2, 0, 1)).reshape(P, -1)
    arrays["L1_mix_wqkvt"] = np.ascontiguousarray(given["L1_mix_Wqkv"].T)
    arrays["L1_mix_wprojt"] = np.ascontiguousarray(given["L1_mix_Wproj"].T)
    arrays["L1_mix_temperature"] = given["L1_mix_temperature"].reshape(H0)
    arrays["L0_ffn_temperature"] = given["L0_ffn_temperature"].reshape(H0)
    for name in ("L0_gnn_filters", "L0_ffn_W_slice", "L0_ffn_b_slice", "L0_ffn_W_fx", "L0_ffn_b_fx", "L0_ffn_W_q",
                 "L0_ffn_W_k", "L0_ffn_W_v", "L0_ffn_W_out", "L0_ffn_b_out", "L1_gnn_w1_s", "L1_gnn_w1_v",
                 "L1_gnn_fc_w1", "L1_gnn_fc_w2", "L1_gnn_fc_w3", "L1_gnn_w2_s", "L1_gnn_w2_v", "L1_gnn_g_s",
                 "L1_gnn_g_v", "L1_ffn_gamma", "L1_ffn_beta", "L1_ffn_Wr", "L1_ffn_br", "L1_ffn_b2", "L1_gnn_wsc_s", "L1_gnn_wsc_v", "L1_mix_bqkv", "L1_mix_bproj"):
        arrays[name] = given[name]
    for name in ("kln_weight", "kln_bias", "vln_weight", "vln_bias"):
        arrays["L0_mix_" + name] = given["L0_mix_" + name].reshape(D)
    arrays["rec_cols"], arrays["rec_rest"] = cols(rec)
    arrays["src_cols"], arrays["src_rest"] = cols(given["src"])
    arrays["dst_cols"], arrays["dst_rest"] = cols(given["dst"])
    arrays["src_rest"] = arrays["src_rest"][:, None]
    arrays["dst_rest"] = arrays["dst_rest"][:, None]
    nc = bacc.Bacc("TRN2", target_bir_lowering=False, num_devices=1)
    args = {k: nc.dram_tensor("in_" + k, v.shape, mybir.dt.from_np(v.dtype), kind="ExternalInput").ap()
            for k, v in arrays.items()}
    out = nc.dram_tensor("out", (N, D), F32, kind="ExternalOutput").ap()
    build(nc, args, out)
    r = run_bass_kernel_spmd(nc, [{"in_" + k: v for k, v in arrays.items()}], core_ids=[0])
    return r.results[0]["out"]
```

```python
from contextlib import ExitStack

import numpy as np
import concourse.bass as bass
from concourse import mybir

F32 = mybir.dt.float32
BF16 = mybir.dt.bfloat16
I32 = mybir.dt.int32
ALU = mybir.AluOpType
ACT = mybir.ActivationFunctionType
X = mybir.AxisListType.X

P = 128
N, D, E = 3125, 256, 53125
NP_ = 125
NT = N // NP_
ET = -(-E // P)
EREST = E - (ET - 1) * P
ST = 440
assert (E + NT * (P - 1)) // P <= ST
RF = 16
R_W, R_SH, R_LOCAL, R_DST, R_ONE, R_ATTR = 0, 1, 5, 6, 7, 8
NONE = 32 * NP_
MAGIC = 1.5 * 2.0 ** 23
EPS = 1e-5
H0, HC = 8, 32
G = 64
MUL = 64
AG = 4 * MUL * 2


UN0, UN = 40, 20
assert ST % UN0 == 0 and ST % UN == 0
SG = 26
assert ET % (2 * SG) == 0


class Chain:

    def __init__(self, engine, sem):
        self.engine, self.sem, self.base, self.n = engine, sem, 0, 0

    def __call__(self, ins):
        ins.then_inc(self.sem, 1)
        self.n += 1
        self.engine.wait_ge(self.sem, self.base + self.n)

    def loop(self):
        self.start = self.base + self.n

    def at(self, t, k):
        self.k, self.base, self.n = k, self.start + t * k, 0

    def end(self, tiles):
        assert self.n == self.k, (self.n, self.k)
        self.base, self.n = self.start + tiles * self.k, 0


UT = 4
assert NT % UT == 1


def each_node_tile(engine, body):
    for t in range(UT):
        body(t, t)
    with engine.Fori(1, NT // UT - 1) as i:
        for u in range(UT):
            body(i * UT + u, u)
    for t in range(NT - UT - 1, NT):
        body(t, t % UT)


def wait(engine, sem, value):
    if not (isinstance(value, int) and value <= 0):
        engine.wait_ge(sem, value)


def bcast(ap, shape):
    return ap.to_broadcast(shape)


class Core:

    def __init__(self, nc, ctx, args, out):
        self.nc, self.ctx, self.a, self.out, self.stage = nc, ctx, args, out, None
        self.held = []
        self.bank = [ctx.enter_context(nc.psum_tensor(f"bank{i}", [P, 512], F32)) for i in range(8)]
        self.x = self.sb("x", [NP_, NT, D])
        self.z = self.sb("z", [NP_, NT, D])
        self.mv = self.sb("mv", [NP_, NT, 2])
        self.rstd = self.sb("rstd", [NP_, NT])
        self.shift = self.sb("shift", [NP_, NT])
        self.ident = self.sb("ident", [P, P])
        self.ones = self.sb("ones", [P, P])
        self.ltri = self.sb("ltri", [P, P])
        self.iota = self.sb("iota", [P, NP_])
        self.bucket_of = self.sb("bucket_of", [1, ST], I32)
        self.kv = self.sb("kv", [P, 2, P])
        self.s_pass = self.sem("s_pass")
        self.s_scat = [self.sem(f"s_scat{h}") for h in range(2)]
        self.s_got = [self.sem(f"s_got{u}") for u in range(UN0)]
        self.rec_dram = nc.dram_tensor("rec_sorted", (P * ST, RF), F32, kind="Internal").ap()
        self.z_dram = nc.dram_tensor("z_rows", (N, D), F32, kind="Internal").ap()
        self.y_dram = nc.dram_tensor("y_rows", (N, D), F32, kind="Internal").ap()

    def sb(self, name, shape, dt=F32, ctx=None):
        return (ctx or self.ctx).enter_context(self.nc.sbuf_tensor(name, shape, dt))

    def sem(self, name, ctx=None):
        if ctx is None and self.stage is not None:
            self.held.append(self.nc.alloc_semaphore(name=name))
            return self.held[-1]
        return self.ctx.enter_context(self.nc.semaphore(name))

    def clear_stages(self):
        self.nc.clear_and_free_semaphores(self.held)
        self.nc.all_engine_barrier()
        self.held = []


def rows(ap):
    return ap.rearrange("(t p) f -> p t f", p=NP_)


def row_to_all(ap, n, parts=P):
    return bass.AP(tensor=ap.tensor, offset=ap.offset, ap=[[0, parts], [1, n]])


def sort_and_first_norm(c):
    nc, a, bank = c.nc, c.a, c.bank
    with ExitStack() as ctx:
        c.stage = ctx

        def sb(name, shape, dt=F32):
            return c.sb(name, shape, dt, ctx)

        zeros = sb("zeros", [P, 8 * 220])
        src_i = sb("src_i", [P, ET], I32)
        dst_i = sb("dst_i", [P, ET], I32)
        srcf = sb("srcf", [P, ET])
        t0 = sb("t0", [P, ET])
        bucket = sb("bucket", [P, ET], BF16)
        rec_in = sb("rec_in", [P, ET, RF])
        inb = sb("inb", [P, NT, ET], BF16)
        ltri_b = sb("ltri_b", [P, P], BF16)
        pick = sb("pick", [P, 2 * NT - 1], BF16)
        scan = [sb(f"scan{i}", [NT, ET]) for i in range(2)]
        tot = sb("tot", [NT, ET])
        tiles = sb("tiles", [NT, 1])
        first = sb("first", [NT, 1])
        last = sb("last", [NT, 1])
        off = sb("off", [NT, ET])
        off_hi = sb("off_hi", [NT, ET], BF16)
        off_lo = sb("off_lo", [NT, ET], BF16)
        hi_f = sb("hi_f", [NT, ET])
        pick_row = sb("pick_row", [NT, NT, P], BF16)
        iota_tile = sb("iota_tile", [NT, ST])
        past = sb("past", [NT, ST])
        pos = sb("pos", [P, ET])
        part = sb("part", [P, ET])
        posi = sb("posi", [P, ET], I32)
        lo = sb("lo", [P, ET], I32)
        hi = sb("hi", [P, ET], I32)
        row = sb("row", [P, ET], I32)
        rec_ring = [sb(f"rec_ring{h}", [P, SG, RF]) for h in range(2)]
        row_ring = [sb(f"row_ring{h}", [P, SG], I32) for h in range(2)]
        stats = sb("stats", [NP_, NT, 6])
        varp = sb("varp", [NP_, NT])
        std = sb("std", [NP_, NT])
        hm = sb("hm", [NP_, 5 * H0])
        hs = sb("hs", [NP_, 5 * H0])
        hstd = sb("hstd", [NP_, 5 * H0])
        hr = sb("hr", [NP_, 5 * H0])
        zc = sb("zc", [NP_, 5, D])
        sq = sb("sq", [NP_, 5, D])
        zh = sb("zh", [NP_, 5, D])
        kw = sb("kw", [P, 2])
        kb = sb("kb", [P, 2])
        ks = sb("ks", [P, 2])
        vw = sb("vw", [P, D])
        vb = sb("vb", [P, D])
        kvt = sb("kvt", [P, 2, P])

        s_const = c.sem("s_const")
        s_x = c.sem("s_x")
        s_src = c.sem("s_src")
        s_rec = c.sem("s_rec")
        s_dst = c.sem("s_dst")
        s_zero = c.sem("s_zero")
        s_dve = c.sem("s_dve1")
        s_inb = c.sem("s_inb")
        s_tot = c.sem("s_tot")
        s_tiles = c.sem("s_tiles")
        s_first = c.sem("s_first")
        s_past = c.sem("s_past")
        s_bkt = c.sem("s_bkt")
        s_off = c.sem("s_off")
        s_rank = c.sem("s_rank")
        s_rank_used = c.sem("s_rank_used")
        s_row = c.sem("s_row")
        s_ring = c.sem("s_ring")
        s_scat = c.s_scat
        s_var = c.sem("s_var")
        s_std = c.sem("s_std")
        s_z = c.sem("s_z")
        s_zd = c.sem("s_zd")
        s_hs = c.sem("s_hs")
        s_hstd = c.sem("s_hstd")
        s_zh = c.sem("s_zh")
        s_zh_used = c.sem("s_zh_used")
        s_g = c.sem("s_g")
        s_kv = c.sem("s_kv")
        block = ctx.enter_context(nc.Block())

        @block.sync
        def _(sp):
            for dst, name in ((kw, "L0_mix_kln_weight"), (kb, "L0_mix_kln_bias")):
                with nc.allow_non_contiguous_dma("one column per chunk"):
                    for k in range(2):
                        sp.dma_start(dst[:, k:k + 1], a[name][k * P:k * P + P].unsqueeze(1)).then_inc(s_kv, 16)
            sp.dma_start(vw[:, :], row_to_all(a["L0_mix_vln_weight"], D)).then_inc(s_kv, 16)
            sp.dma_start(vb[:, :], row_to_all(a["L0_mix_vln_bias"], D)).then_inc(s_kv, 16)
            sp.wait_ge(s_const, 1)
            sp.dma_start(src_i[:, 0:ET - 1], a["src_cols"]).then_inc(s_src, 16)
            sp.dma_start(src_i[0:EREST, ET - 1:ET], a["src_rest"]).then_inc(s_src, 16)
            sp.dma_start(dst_i[:, 0:ET - 1], a["dst_cols"]).then_inc(s_dst, 16)
            sp.dma_start(dst_i[0:EREST, ET - 1:ET], a["dst_rest"]).then_inc(s_dst, 16)
            sp.dma_start(rec_in[:, 0:ET - 1, :], a["rec_cols"]).then_inc(s_rec, 16)
            sp.dma_start(rec_in[0:EREST, ET - 1, :], a["rec_rest"]).then_inc(s_rec, 16)
            sp.dma_start(c.x[:, :, :], rows(a["x"])).then_inc(s_x, 16)
            zr = c.rec_dram.rearrange("(p s r) f -> p s (r f)", p=P, s=4)
            for s in range(4):
                sp.dma_start(zr[:, s, :], zeros[:, :]).then_inc(s_zero, 16)
            sp.wait_ge(s_z, 1)
            sp.dma_start(rows(c.z_dram), c.z[:, :, :]).then_inc(s_zd, 16)
            sp.wait_ge(s_zd, 16)
            for h in range(2):
                sp.wait_ge(s_scat[h], 16 * ET // 2)

        @block.gpsimd
        def _(pool):
            nc.gpsimd.memset(zeros[:, :], 0.0)
            nc.gpsimd.memset(dst_i[:, ET - 1:ET], 0)
            nc.gpsimd.memset(rec_in[:, ET - 1, :], 0.0)
            nc.gpsimd.memset(src_i[:, ET - 1:ET], NONE).then_inc(s_const, 1)
            nc.gpsimd.memset(c.ones[:, :], 1.0)
            nc.gpsimd.memset(c.ident[:, :], 0.0)
            nc.gpsimd.memset(c.ltri[:, :], 1.0)
            nc.gpsimd.memset(pick[:, :], 0.0).then_inc(s_const, 1)
            pool.wait_ge(s_const, 2)
            nc.gpsimd.memset(pick[:, NT - 1:NT], 1.0)
            nc.gpsimd.affine_select(out=c.ident[:, :], in_=c.ident[:, :], compare_op=ALU.not_equal, fill=1.0,
                                    base=0, pattern=[[-1, P]], channel_multiplier=1)
            nc.gpsimd.affine_select(out=c.ltri[:, :], in_=c.ltri[:, :], compare_op=ALU.is_gt, fill=0.0,
                                    base=0, pattern=[[1, P]], channel_multiplier=-1)
            nc.gpsimd.iota(c.iota[:, :], pattern=[[1, NP_]], base=0, channel_multiplier=0,
                           allow_small_or_imprecise_dtypes=True)
            nc.gpsimd.iota(iota_tile[:, :], pattern=[[1, ST]], base=0, channel_multiplier=0,
                           allow_small_or_imprecise_dtypes=True).then_inc(s_const, 1)
            pool.wait_ge(s_zero, 64)
            pool.wait_ge(s_row, 1)

            def scatter(t, h, group, last):
                wait(pool, s_scat[h], SG * 16 * group)
                nc.gpsimd.tensor_copy(rec_ring[h][:, :, :], rec_in[:, bass.ds(t, SG), :])
                nc.gpsimd.tensor_copy(row_ring[h][:, :], row[:, bass.ds(t, SG)]).then_inc(s_ring, 1)
                pool.wait_ge(s_ring, group * 2 + h + 1)
                pool.sem_inc(c.s_pass, 1)
                for u in range(SG):
                    n = EREST if last and u == SG - 1 else P
                    nc.gpsimd.indirect_dma_start(
                        out=c.rec_dram, out_offset=bass.IndirectOffsetOnAxis(ap=row_ring[h][0:n, u:u + 1], axis=0),
                        in_=rec_ring[h][0:n, u, :], in_offset=None).then_inc(s_scat[h], 16)

            rounds = ET // (2 * SG)
            scatter(0, 0, 0, False)
            scatter(SG, 1, 0, False)
            with pool.Fori(1, rounds - 1) as i:
                scatter(i * (2 * SG), 0, i, False)
                scatter(i * (2 * SG) + SG, 1, i, False)
            scatter(ET - 2 * SG, 0, rounds - 1, False)
            scatter(ET - SG, 1, rounds - 1, True)

        @block.scalar
        def _(act):
            act.wait_ge(s_var, 1)
            nc.scalar.activation(std[:, :], varp[:, :], ACT.Sqrt).then_inc(s_std, 1)
            with act.Fori(0, 5) as i:
                act.wait_ge(s_hs, i + 1)
                nc.scalar.activation(hstd[:, :], hs[:, :], ACT.Sqrt, scale=1.0 / (HC - 1)).then_inc(s_hstd, 1)

        @block.vector
        def _(dve):
            link = Chain(dve, s_dve)
            v = nc.vector
            dve.wait_ge(s_const, 3)
            dve.wait_ge(s_src, 32)
            link(v.tensor_copy(srcf[:, :], src_i[:, :]))
            link(v.tensor_scalar(t0[:, :], srcf[:, :], 1.0 / NP_, -62.0 / NP_, ALU.mult, ALU.add))
            link(v.tensor_scalar(t0[:, :], t0[:, :], MAGIC, None, ALU.add))
            link(v.tensor_scalar(t0[:, :], t0[:, :], -MAGIC, None, ALU.add))
            link(v.tensor_copy(bucket[:, :], t0[:, :]))
            v.tensor_copy(pick_row[:, :, :], bcast(c.ident[0:NT, 0:NT].unsqueeze(2), [NT, NT, P]))
            link(v.tensor_copy(ltri_b[:, :], c.ltri[:, :]))
            for b in range(NT):
                v.tensor_scalar(inb[:, b, :], bucket[:, :], float(b), None, ALU.is_equal).then_inc(s_inb, 1)
            dve.wait_ge(s_rec, 32)
            dve.wait_ge(s_dst, 32)
            v.scalar_tensor_tensor(out=rec_in[:, :, R_LOCAL], in0=t0[:, :], scalar=-float(NP_), in1=srcf[:, :],
                                   op0=ALU.mult, op1=ALU.add)
            v.tensor_copy(rec_in[:, :, R_DST], dst_i[:, :])
            dve.wait_ge(s_tot, 1)
            link(v.tensor_copy(tot[:, :], bank[5][0:NT, 0:ET]))
            link(v.tensor_copy(scan[0][:, :], tot[:, :]))
            k, s = 1, 0
            while k < ET:
                v.tensor_copy(scan[1 - s][:, 0:k], scan[s][:, 0:k])
                link(v.tensor_tensor(scan[1 - s][:, k:ET], scan[s][:, k:ET], scan[s][:, 0:ET - k], ALU.add))
                k, s = 2 * k, 1 - s
            link(v.tensor_scalar(tiles[:, :], scan[s][:, ET - 1:ET], 1.0 / P, (P - 1) / 2 / P, ALU.mult, ALU.add))
            link(v.tensor_scalar(tiles[:, :], tiles[:, :], MAGIC, None, ALU.add))
            v.tensor_scalar(tiles[:, :], tiles[:, :], -MAGIC, None, ALU.add).then_inc(s_tiles, 1)
            link(v.tensor_tensor(off[:, :], scan[s][:, :], tot[:, :], ALU.subtract))
            dve.wait_ge(s_first, 1)
            link(v.tensor_scalar(first[:, :], bank[6][0:NT, 0:1], float(P), None, ALU.mult))
            link(v.tensor_scalar(off[:, :], off[:, :], first[:, 0:1], None, ALU.add))
            link(v.tensor_scalar(hi_f[:, :], off[:, :], 1.0 / 256, -127.5 / 256, ALU.mult, ALU.add))
            link(v.tensor_scalar(hi_f[:, :], hi_f[:, :], MAGIC, None, ALU.add))
            link(v.tensor_scalar(hi_f[:, :], hi_f[:, :], -MAGIC, None, ALU.add))
            v.scalar_tensor_tensor(out=off_lo[:, :], in0=hi_f[:, :], scalar=-256.0, in1=off[:, :],
                                   op0=ALU.mult, op1=ALU.add).then_inc(s_off, 1)
            v.tensor_scalar(off_hi[:, :], hi_f[:, :], 256.0, None, ALU.mult).then_inc(s_off, 1)
            link(v.tensor_tensor(last[:, :], bank[6][0:NT, 0:1], tiles[:, :], ALU.add))
            v.tensor_scalar(past[:, :], iota_tile[:, :], last[:, 0:1], None, ALU.is_ge).then_inc(s_past, 1)
            link(v.memset(pos[:, :], 0.0))
            for b in range(NT):
                dve.wait_ge(s_rank, b + 1)
                r = v.tensor_tensor(part[:, :], bank[b % 2][:, 0:ET], inb[:, b, :], ALU.mult)
                r.then_inc(s_rank_used, 1)
                dve.wait_ge(s_rank_used, b + 1)
                link(v.tensor_tensor(pos[:, :], pos[:, :], part[:, :], ALU.add))
            dve.wait_ge(s_bkt, 1)
            v.tensor_copy(c.bucket_of[:, :], bank[7][0:1, 0:ST])
            link(v.tensor_copy(posi[:, :], pos[:, :]))
            v.tensor_scalar(lo[:, :], posi[:, :], P - 1, None, ALU.bitwise_and)
            link(v.tensor_scalar(hi[:, :], posi[:, :], 7, None, ALU.arith_shift_right))
            v.scalar_tensor_tensor(out=row[:, :], in0=lo[:, :], scalar=float(ST), in1=hi[:, :],
                                   op0=ALU.mult, op1=ALU.add).then_inc(s_row, 1)
            dve.wait_ge(s_x, 16)
            layer_norm_stats(c, dve, link, stats, varp)
            link(v.tensor_scalar(varp[:, :], c.mv[:, :, 1], EPS, None, ALU.add))
            dve.nop().then_inc(s_var, 1)
            dve.wait_ge(s_std, 1)
            link(v.reciprocal(c.rstd[:, :], std[:, :]))
            link(v.tensor_tensor(c.z[:, :, :], c.x[:, :, :], bcast(c.mv[:, :, 0:1], [NP_, NT, D]), ALU.subtract))
            link(v.tensor_tensor(c.z[:, :, :], c.z[:, :, :], bcast(c.rstd[:, :].unsqueeze(2), [NP_, NT, D]), ALU.mult))
            dve.nop().then_inc(s_z, 1)
            link.loop()
            with dve.Fori(0, 5) as i:
                link.at(i, 5)
                zi = c.z[:, bass.ds(i * 5, 5), :].rearrange("p t (h d) -> p (t h) d", h=H0)
                zc3 = zc[:, :, :].rearrange("p t (h d) -> p (t h) d", h=H0)
                sq3 = sq[:, :, :].rearrange("p t (h d) -> p (t h) d", h=H0)
                zh3 = zh[:, :, :].rearrange("p t (h d) -> p (t h) d", h=H0)
                full = [NP_, 5 * H0, HC]
                link(v.reduce_sum(hm[:, :], zi, X))
                link(v.tensor_scalar(hm[:, :], hm[:, :], 1.0 / HC, None, ALU.mult))
                link(v.tensor_tensor(zc3, zi, bcast(hm[:, :].unsqueeze(2), full), ALU.subtract))
                link(v.tensor_tensor(sq3, zc3, zc3, ALU.mult))
                v.reduce_sum(hs[:, :], sq3, X).then_inc(s_hs, 1)
                dve.wait_ge(s_hstd, i + 1)
                link(v.tensor_scalar(hstd[:, :], hstd[:, :], EPS, None, ALU.add))
                v.reciprocal(hr[:, :], hstd[:, :]).then_inc(s_zh, 1)
                dve.wait_ge(s_zh, i * 2 + 1)
                dve.wait_ge(s_zh_used, i)
                v.tensor_tensor(zh3, zc3, bcast(hr[:, :].unsqueeze(2), full), ALU.mult).then_inc(s_zh, 1)
            link.end(5)
            dve.wait_ge(s_g, 1)
            dve.wait_ge(s_kv, 96)
            link(v.memset(c.kv[:, :, :], 0.0))
            for k in range(2):
                cols = slice(k * P, k * P + P)
                link(v.tensor_scalar(kvt[:, k, :], bank[k][:, 0:P], kw[:, k:k + 1], None, ALU.mult))
                link(v.scalar_tensor_tensor(out=kvt[:, k, :], in0=bank[2][:, cols], scalar=kb[:, k:k + 1],
                                            in1=kvt[:, k, :], op0=ALU.mult, op1=ALU.add))
                link(v.tensor_tensor(kvt[:, k, :], kvt[:, k, :], vw[:, cols], ALU.mult))
                link(v.tensor_scalar(ks[:, k:k + 1], kb[:, k:k + 1], float(N), None, ALU.mult))
                link(v.scalar_tensor_tensor(out=ks[:, k:k + 1], in0=bank[3][:, k:k + 1], scalar=kw[:, k:k + 1],
                                            in1=ks[:, k:k + 1], op0=ALU.mult, op1=ALU.add))
                link(v.scalar_tensor_tensor(out=kvt[:, k, :], in0=vb[:, cols], scalar=ks[:, k:k + 1],
                                            in1=kvt[:, k, :], op0=ALU.mult, op1=ALU.add))
                for q in range(4):
                    own = slice(q * HC, q * HC + HC)
                    v.tensor_scalar(c.kv[own, k, own], kvt[own, k, own], 1.0 / N, None, ALU.mult)

        @block.tensor
        def _(pe):
            mm = nc.tensor.matmul
            pe.wait_ge(s_const, 3)
            for b in range(NT):
                pe.wait_ge(s_inb, b + 1)
                r = mm(bank[5][0:NT, 0:ET], pick[:, NT - 1 - b:2 * NT - 1 - b], inb[:, b, :],
                       start=b == 0, stop=b == NT - 1)
            r.then_inc(s_tot, 1)
            pe.wait_ge(s_tiles, 1)
            mm(bank[6][0:NT, 0:1], c.ltri[0:NT, 0:NT], tiles[:, :], start=True, stop=True).then_inc(s_first, 1)
            pe.wait_ge(s_off, 2)
            for b in range(NT):
                if b >= 2:
                    pe.wait_ge(s_rank_used, b - 1)
                mm(bank[b % 2][:, 0:ET], ltri_b[:, :], inb[:, b, :], start=True, stop=False)
                mm(bank[b % 2][:, 0:ET], pick_row[:, b, :], off_hi[:, :], start=False, stop=False)
                mm(bank[b % 2][:, 0:ET], pick_row[:, b, :], off_lo[:, :], start=False, stop=True).then_inc(s_rank, 1)
            pe.wait_ge(s_past, 1)
            mm(bank[7][0:1, 0:ST], c.ones[0:NT, 0:1], past[:, :], start=True, stop=True).then_inc(s_bkt, 1)
            pe.wait_ge(s_rank_used, NT)

            def products(i, first, last):
                pe.wait_ge(s_zh, i * 2 + 2)
                for u in range(5):
                    go = first and u == 0
                    for k in range(2):
                        zk = zh[:, u, k * P:k * P + P]
                        mm(bank[k][:, 0:P], zk, zk, start=go, stop=last and u == 4)
                        mm(bank[3][:, k:k + 1], zk, c.ones[0:NP_, 0:1], start=go and k == 0, stop=last and u == 4 and k == 1)
                    r = mm(bank[2][:, 0:D], c.ones[0:NP_, :], zh[:, u, :], start=go, stop=last and u == 4)
                r.then_inc(s_zh_used, 1)

            products(0, True, False)
            with pe.Fori(1, 4) as i:
                products(i, False, False)
            products(4, False, True)
            pe.wait_ge(s_zh_used, 5)
            pe.nop().then_inc(s_g, 1)


def layer_norm_stats(c, dve, link, stats, varp):
    link.loop()
    with dve.Fori(0, NT) as i:
        link.at(i, 1)
        link(c.nc.vector.bn_stats(flat(stats, i), flat(c.x, i)))
    link.end(NT)
    for t in range(NT):
        r = c.nc.vector.bn_aggr(c.mv[:, t, :], stats[:, t, :])
    link(r)


class Norm:

    def __init__(self, c, name, ctx):
        self.c = c
        self.stats = c.sb(name + "_stats", [NP_, NT, 6], F32, ctx)
        self.varp = c.sb(name + "_varp", [NP_, NT], F32, ctx)
        self.std = c.sb(name + "_std", [NP_, NT], F32, ctx)
        self.s_tile = c.sem(name + "_s_tile")
        self.s_var = c.sem(name + "_s_var")
        self.s_std = c.sem(name + "_s_std")

    def tile(self, t):
        self.c.nc.vector.bn_stats(flat(self.stats, t), flat(self.c.x, t)).then_inc(self.s_tile, 1)

    def finish(self, dve, link):
        c, v = self.c, self.c.nc.vector
        dve.wait_ge(self.s_tile, NT)
        for t in range(NT):
            r = v.bn_aggr(c.mv[:, t, :], self.stats[:, t, :])
        link(r)
        v.tensor_scalar(self.varp[:, :], c.mv[:, :, 1], EPS, None, ALU.add).then_inc(self.s_var, 1)
        dve.wait_ge(self.s_std, 1)
        link(v.reciprocal(c.rstd[:, :], self.std[:, :]))
        link(v.scalar_tensor_tensor(out=c.shift[:, :], in0=c.mv[:, :, 0], scalar=-1.0, in1=c.rstd[:, :],
                                    op0=ALU.mult, op1=ALU.mult))

    def root(self, act):
        act.wait_ge(self.s_var, 1)
        self.c.nc.scalar.activation(self.std[:, :], self.varp[:, :], ACT.Sqrt).then_inc(self.s_std, 1)


def flat(buffer, t):
    return buffer[:, bass.ds(t, 1), :].rearrange("p o f -> p (o f)")


def indices(c, idx_ring, rec, i, h, s_ring):
    half = idx_ring[h].shape[1]
    c.nc.vector.tensor_copy(idx_ring[h][:, :], rec[:, bass.ds((2 * i + h) * half, half), R_DST]).then_inc(s_ring, 1)


def gather_rows(c, pool, table, idx_ring, slots, s_ring, s_used, s_got, rec):
    nc = c.nc
    UN, HALF = len(slots), len(slots) // 2

    def half(i, h, free):
        j = i * UN + h * HALF
        if free:
            pool.wait_ge(s_used, j - HALF)
        pool.wait_ge(s_ring, i * 2 + h + 1)
        pool.sem_inc(c.s_pass, 1)
        for u in range(HALF):
            nc.gpsimd.indirect_dma_start(
                out=slots[h * HALF + u], out_offset=None, in_=table,
                in_offset=bass.IndirectOffsetOnAxis(ap=idx_ring[h][:, u:u + 1], axis=0)
            ).then_inc(s_got[h * HALF + u], 16)

    half(0, 0, False)
    half(0, 1, False)
    with pool.Fori(1, ST // UN) as i:
        half(i, 0, True)
        half(i, 1, True)


def first_edges(c, acc):
    nc, bank = c.nc, c.bank
    UN, HALF = UN0, UN0 // 2
    OG = 4
    with ExitStack() as ctx:
        c.stage = ctx

        def sb(name, shape, dt=F32):
            return c.sb(name, shape, dt, ctx)

        idx_ring = [sb(f"idx_ring{h}", [P, HALF], I32) for h in range(2)]
        g = sb("g", [P, UN, D + 1])
        oh = sb("oh", [P, 2 * OG, NP_])
        s_rec = c.sem("s_e0_rec")
        s_ring = c.sem("s_e0_ring")
        s_got = c.s_got
        s_weighed = c.sem("s_e0_weighed")
        s_oh = c.sem("s_e0_oh")
        s_mm = c.sem("s_e0_mm")
        s_acc = c.sem("s_e0_acc")
        block = ctx.enter_context(nc.Block())
        rec = c.rec

        @block.sync
        def _(sp):
            sp.dma_start(rec[:, :, :], c.rec_dram.rearrange("(p j) f -> p j f", p=P)).then_inc(s_rec, 16)
            sp.wait_ge(s_rec, 16)

        @block.gpsimd
        def _(pool):
            pool.wait_ge(s_rec, 16)
            gather_rows(c, pool, c.z_dram, idx_ring, [g[:, u, 0:D] for u in range(UN)], s_ring, s_mm, s_got, rec)

        @block.scalar
        def _(act):
            with act.Fori(0, ST // UN) as i:
                for u in range(UN):
                    j = i * UN + u
                    act.wait_ge(s_got[u], i * 16 + 16)
                    nc.scalar.activation(g[:, u, 0:D], g[:, u, 0:D], ACT.Copy, scale=flat(rec, j)[:, R_W:R_W + 1])
                    nc.scalar.activation(g[:, u, D:D + 1], flat(rec, j)[:, R_ONE:R_ONE + 1],
                                         ACT.Copy).then_inc(s_weighed, 1)

        @block.vector
        def _(dve):
            v = nc.vector
            v.tensor_tensor(c.x[:, :, :], c.x[:, :, :], c.z[:, :, :], ALU.add)
            v.memset(acc[:, :, :], 0.0).then_inc(s_acc, 4)
            dve.wait_ge(s_rec, 16)

            def one_hots(j, u):
                v.tensor_tensor(oh[:, u % (2 * OG):u % (2 * OG) + OG, :],
                                bcast(c.iota[:, :].unsqueeze(1), [P, OG, NP_]),
                                bcast(rec[:, bass.ds(j, OG), R_LOCAL:R_LOCAL + 1], [P, OG, NP_]),
                                ALU.is_equal).then_inc(s_oh, 1)

            def rounds(i, last):
                for u in range(UN):
                    j = i * UN + u
                    b = dve.value_load(c.bucket_of[0:1, bass.ds(j, 1)], min_val=0, max_val=NT)
                    dve.wait_ge(s_mm, j + 1)
                    dve.wait_ge(s_acc, j + 4)
                    v.tensor_tensor(flat(acc, b), flat(acc, b), bank[u % 4][0:NP_, 0:D + 1],
                                    ALU.add).then_inc(s_acc, 1)
                    if u == 0:
                        indices(c, idx_ring, rec, i, 1, s_ring)
                    if u == HALF and not last:
                        indices(c, idx_ring, rec, i + 1, 0, s_ring)
                    if u % OG == 0 and not (last and u == UN - OG):
                        one_hots(j + OG, u + OG)

            indices(c, idx_ring, rec, 0, 0, s_ring)
            one_hots(0, 0)
            with dve.Fori(0, ST // UN - 1) as i:
                rounds(i, False)
            rounds(ST // UN - 1, True)

        @block.tensor
        def _(pe):
            with pe.Fori(0, ST // UN) as i:
                for u in range(UN):
                    j = i * UN + u
                    pe.wait_ge(s_weighed, j + 1)
                    pe.wait_ge(s_oh, i * (UN // OG) + u // OG + 1)
                    pe.wait_ge(s_acc, j + 1)
                    nc.tensor.matmul(bank[u % 4][0:NP_, 0:D + 1], oh[:, u % (2 * OG), :], g[:, u, :],
                                     start=True, stop=True).then_inc(s_mm, 1)



def column(buffer, t):
    return buffer[:, bass.ds(t, 1)]


def combine_first(c, acc):
    nc, a, bank = c.nc, c.a, c.bank
    with ExitStack() as ctx:
        c.stage = ctx

        def sb(name, shape, dt=F32):
            return c.sb(name, shape, dt, ctx)

        filt = sb("filt", [P, 2, D])
        rows_in = sb("rows_in", [NP_, 4, 2 * D])
        cols_in = sb("cols_in", [P, 2, 4 * NP_])
        norm = Norm(c, "n2", ctx)
        s_w = c.sem("cf_s_w")
        s_in = c.sem("cf_s_in")
        s_tp = c.sem("cf_s_tp")
        s_cols = c.sem("cf_s_cols")
        s_mm = c.sem("cf_s_mm")
        s_add = c.sem("cf_s_add")
        s_dve = c.sem("cf_s_dve")
        block = ctx.enter_context(nc.Block())

        @block.sync
        def _(sp):
            sp.dma_start(filt[:, :, :], a["L0_gnn_filters"].rearrange("(k p) f -> p k f", p=P)).then_inc(s_w, 16)
            sp.wait_ge(s_w, 16)

        @block.scalar
        def _(act):
            def load(t, u):
                wait(act, s_tp, t - 3)
                nc.scalar.copy(rows_in[:, u, 0:D], flat(acc, t)[:, 0:D])
                nc.scalar.copy(rows_in[:, u, D:2 * D], flat(c.z, t)).then_inc(s_in, 1)

            each_node_tile(act, load)
            norm.root(act)

        @block.vector
        def _(dve):
            v = nc.vector
            link = Chain(dve, s_dve)
            v.tensor_copy(c.deg[:, :], acc[:, 0:NT, D])

            def turn(t, u):
                wait(dve, s_tp, t + 1)
                wait(dve, s_mm, t - 1)
                v.tensor_copy(cols_in[:, u % 2, :], bank[u % 2][:, 0:4 * NP_]).then_inc(s_cols, 1)

            def add(t, u):
                if not (isinstance(t, int) and t == NT - 1):
                    turn(t + 1, (u + 1) % 4)
                dve.wait_ge(s_mm, t + 1)
                v.tensor_tensor(flat(c.x, t), flat(c.x, t), bank[2 + u % 2][0:NP_, 0:D], ALU.add).then_inc(s_add, 1)
                dve.wait_ge(s_add, t + 1)
                norm.tile(t)

            turn(0, 0)
            each_node_tile(dve, add)
            norm.finish(dve, link)

        @block.tensor
        def _(pe):
            def turn(t, u):
                wait(pe, s_in, t + 1)
                wait(pe, s_cols, t - 1)
                for k in range(4):
                    r = nc.tensor.transpose(bank[u % 2][:, k * NP_:(k + 1) * NP_],
                                            rows_in[:, u, k * P:(k + 1) * P], c.ident[0:NP_, 0:NP_])
                r.then_inc(s_tp, 1)

            def multiply(t, u):
                if not (isinstance(t, int) and t == NT - 1):
                    turn(t + 1, (u + 1) % 4)
                pe.wait_ge(s_cols, t + 1)
                wait(pe, s_add, t - 1)
                to, cols = bank[2 + u % 2], cols_in[:, u % 2, :]
                for k in range(2):
                    nc.tensor.matmul(to[0:NP_, 0:D], cols[:, k * NP_:(k + 1) * NP_], filt[:, k, :],
                                     start=k == 0, stop=False)
                for k in range(2):
                    r = nc.tensor.matmul(to[0:NP_, k * P:(k + 1) * P], cols[:, (2 + k) * NP_:(3 + k) * NP_],
                                         c.kv[:, k, :], start=False, stop=k == 1)
                r.then_inc(s_mm, 1)

            pe.wait_ge(s_w, 16)
            turn(0, 0)
            each_node_tile(pe, multiply)



def slice_weights(c, swt, tokens):
    nc, a, bank = c.nc, c.a, c.bank
    HG = H0 * G
    NC = HG // P
    with ExitStack() as ctx:
        c.stage = ctx

        def sb(name, shape, dt=F32):
            return c.sb(name, shape, dt, ctx)

        wxt = sb("wxt", [G, H0, D + 1])
        wslice = sb("wslice", [G, G])
        bslice = sb("bslice", [P, G])
        temp = sb("temp", [P, H0])
        rtemp = sb("rtemp", [P, H0])
        wxs = sb("wxs", [P, 2, HG])
        bxs = sb("bxs", [P, HG])
        zr = sb("zr", [NP_, 4, D])
        zall = sb("zall", [NP_, NT, D + 1])
        ztr = sb("ztr", [P, 2, 2 * NP_])
        lg = sb("lg", [NP_, 2, HG])
        ex = sb("ex", [NP_, 2, HG])
        sw = sb("sw", [NP_, 4, HG])
        mx = sb("mx", [NP_, 2, H0])
        tot = sb("sw_tot", [NP_, 2, H0])
        inv = sb("sw_inv", [NP_, 2, H0])
        s_w = c.sem("sl_s_w")
        s_ones = c.sem("sl_s_ones")
        s_fold = c.sem("sl_s_fold")
        s_ready = c.sem("sl_s_ready")
        s_in = c.sem("sl_s_in")
        s_tp = c.sem("sl_s_tp")
        s_ztr = c.sem("sl_s_ztr")
        s_lg = c.sem("sl_s_lg")
        s_sub = c.sem("sl_s_sub")
        s_exp = c.sem("sl_s_exp")
        s_sw = c.sem("sl_s_sw")
        s_sum = c.sem("sl_s_sum")
        s_swt = c.sem("sl_s_swt")
        s_dve = c.sem("sl_s_dve")
        block = ctx.enter_context(nc.Block())

        def heads(ap):
            return ap.rearrange("p (h g) -> p h g", h=H0)

        @block.sync
        def _(sp):
            sp.dma_start(wxt[:, :, :], a["L0_ffn_wxt"].rearrange("(h d) f -> d h f", h=H0)).then_inc(s_w, 16)
            sp.dma_start(wslice[:, :], a["L0_ffn_W_slice"]).then_inc(s_w, 16)
            sp.dma_start(bslice[:, :], row_to_all(a["L0_ffn_b_slice"], G)).then_inc(s_w, 16)
            sp.dma_start(temp[:, :], row_to_all(a["L0_ffn_temperature"], H0)).then_inc(s_w, 16)
            sp.wait_ge(s_w, 64)

        @block.gpsimd
        def _(pool):
            nc.gpsimd.memset(zall[:, :, D:D + 1], 1.0).then_inc(s_ones, 1)

        @block.scalar
        def _(act):
            def load(t, u):
                wait(act, s_tp, t - 3)
                for to in (flat(zall, t)[:, 0:D], zr[:, u, :]):
                    r = nc.scalar.activation(to, flat(c.x, t), ACT.Identity, bias=column(c.shift, t),
                                             scale=column(c.rstd, t))
                r.then_inc(s_in, 1)

            def keep(t, u):
                act.wait_ge(s_sum, t + 1)
                src = bank[u % 2][:, 0:4 * NP_].rearrange("p (k n) -> p k n", k=NC)
                nc.scalar.copy(swt[:, :, bass.ds(t * NP_, NP_)], src).then_inc(s_swt, 1)

            def tile(t, u):
                if not (isinstance(t, int) and t >= NT - 2):
                    load(t + 2, (u + 2) % 4)
                act.wait_ge(s_sub, t + 1)
                nc.scalar.activation(ex[:, u % 2, :], lg[:, u % 2, :], ACT.Exp).then_inc(s_exp, 1)
                if not (isinstance(t, int) and t < 3):
                    keep(t - 3, (u + 1) % 4)

            act.wait_ge(s_ones, 1)
            load(0, 0)
            load(1, 1)
            each_node_tile(act, tile)
            keep(NT - 3, 2)
            keep(NT - 2, 3)
            keep(NT - 1, 0)

        @block.vector
        def _(dve):
            v = nc.vector
            link = Chain(dve, s_dve)
            dve.wait_ge(s_w, 64)
            link(v.tensor_scalar(temp[:, :], temp[:, :], 5.0, 0.1, ALU.min, ALU.max))
            link(v.reciprocal(rtemp[:, :], temp[:, :]))
            dve.wait_ge(s_fold, 1)
            rt = bcast(rtemp[:, :].unsqueeze(2), [P, H0, G])
            for k in range(2):
                v.tensor_tensor(heads(wxs[:, k, :]), heads(bank[k][:, :]), rt, ALU.mult)
            link(v.tensor_tensor(heads(bxs[:, :]), heads(bank[2][:, :]),
                                 bcast(bslice[:, :].unsqueeze(1), [P, H0, G]), ALU.add))
            v.tensor_tensor(heads(bxs[:, :]), heads(bxs[:, :]), rt, ALU.mult).then_inc(s_ready, 1)
            dve.wait_ge(s_ready, 1)

            def turn(t, u):
                dve.wait_ge(s_tp, t + 1)
                wait(dve, s_lg, t - 1)
                v.tensor_copy(ztr[:, u % 2, :], bank[u % 2][:, 0:2 * NP_]).then_inc(s_ztr, 1)

            def normalize(t, u):
                dve.wait_ge(s_exp, t + 1)
                e3 = heads(ex[:, u % 2, :])
                link(v.reduce_sum(tot[:, u % 2, :], e3, X))
                link(v.reciprocal(inv[:, u % 2, :], tot[:, u % 2, :]))
                wait(dve, s_sum, t - 3)
                v.tensor_tensor(heads(sw[:, u, :]), e3, bcast(inv[:, u % 2, :].unsqueeze(2), [NP_, H0, G]),
                                ALU.mult).then_inc(s_sw, 1)

            def tile(t, u):
                link.at(t, 4)
                if isinstance(t, int) and t == 0:
                    link.n = 2
                if not (isinstance(t, int) and t == NT - 1):
                    turn(t + 1, (u + 1) % 4)
                dve.wait_ge(s_lg, t + 1)
                l3 = heads(lg[:, u % 2, :])
                link(v.tensor_tensor(lg[:, u % 2, :], bank[2 + u % 2][0:NP_, :], bxs[0:NP_, :], ALU.add))
                link(v.tensor_reduce(mx[:, u % 2, :], l3, X, ALU.max))
                v.tensor_tensor(l3, l3, bcast(mx[:, u % 2, :].unsqueeze(2), [NP_, H0, G]),
                                ALU.subtract).then_inc(s_sub, 1)
                if not (isinstance(t, int) and t == 0):
                    normalize(t - 1, (u + 3) % 4)

            turn(0, 0)
            link.loop()
            link.start -= 2
            each_node_tile(dve, tile)
            link.end(NT)
            normalize(NT - 1, 0)
            dve.wait_ge(s_sum, NT)
            for k in range(NC):
                v.tensor_copy(tokens[:, k, :], bank[4 + k][:, 0:D + 1])

        @block.tensor
        def _(pe):
            mm = nc.tensor.matmul
            pe.wait_ge(s_w, 64)
            for h in range(H0):
                own = slice(h * G, h * G + G)
                for k in range(2):
                    mm(bank[k][:, own], wxt[:, h, k * P:k * P + P], wslice[:, :], start=True, stop=True)
                r = mm(bank[2][:, own], bcast(wxt[:, h, D:D + 1], [G, P]), wslice[:, :], start=True, stop=True)
            r.then_inc(s_fold, 1)
            pe.wait_ge(s_ready, 1)

            def turn(t, u):
                pe.wait_ge(s_in, t + 1)
                wait(pe, s_swt, t - 5)
                for k in range(2):
                    r = nc.tensor.transpose(bank[u % 2][:, k * NP_:(k + 1) * NP_], zr[:, u, k * P:(k + 1) * P],
                                            c.ident[0:NP_, 0:NP_])
                r.then_inc(s_tp, 1)

            def gather(t, u, first, last):
                pe.wait_ge(s_sw, t + 1)
                for k in range(NC):
                    mm(bank[4 + k][:, 0:D + 1], sw[:, u, k * P:k * P + P], flat(zall, t), start=first, stop=last)
                if isinstance(t, int) and t > NT - 5:
                    wait(pe, s_swt, t - 1)
                else:
                    pe.wait_ge(s_ztr, t + 5)
                for k in range(NC):
                    r = nc.tensor.transpose(bank[u % 2][:, k * NP_:(k + 1) * NP_], sw[:, u, k * P:(k + 1) * P],
                                            c.ident[0:NP_, 0:NP_])
                r.then_inc(s_sum, 1)

            def tile(t, u):
                if not (isinstance(t, int) and t == NT - 1):
                    turn(t + 1, (u + 1) % 4)
                pe.wait_ge(s_ztr, t + 1)
                wait(pe, s_sub, t - 1)
                for k in range(2):
                    r = mm(bank[2 + u % 2][0:NP_, :], ztr[:, u % 2, k * NP_:(k + 1) * NP_], wxs[:, k, :],
                           start=k == 0, stop=k == 1)
                r.then_inc(s_lg, 1)
                if not (isinstance(t, int) and t < 3):
                    gather(t - 3, (u + 1) % 4, isinstance(t, int) and t == 3, False)

            turn(0, 0)
            each_node_tile(pe, tile)
            gather(NT - 3, 2, False, False)
            gather(NT - 2, 3, False, False)
            gather(NT - 1, 0, False, True)


def slice_attention(c, tokens, pw):
    nc, a, bank = c.nc, c.a, c.bank
    NC = H0 * G // P
    with ExitStack() as ctx:
        c.stage = ctx

        def sb(name, shape, dt=F32):
            return c.sb(name, shape, dt, ctx)

        wfx = sb("wfx", [P, 2, H0 * G])
        bfx = sb("bfx", [P, H0 * G])
        wq, wk, wv = (sb(n, [P, P]) for n in ("wq", "wk", "wv"))
        wout = sb("wout", [P, NC, D])
        tt = sb("tt", [P, 2, NC, P])
        inv = sb("tok_inv", [P, NC])
        ni = sb("tok_ni", [P, NC])
        tok, tokt, q, k_, v_ = (sb("sa_" + n, [P, NC, P]) for n in ("tok", "tokt", "q", "k", "v"))
        at, att, ost, sc = (sb("sa_" + n, [P, NC, P]) for n in ("at", "att", "ost", "sc"))
        mx = sb("sa_mx", [P, NC])
        tot = sb("sa_tot", [P, NC])
        rt = sb("sa_rt", [P, NC])
        s_zero = c.sem("sa_s_zero")
        s_w = c.sem("sa_s_w")
        s_pe = c.sem("sa_s_pe")
        s_out = c.sem("sa_s_out")
        s_dve = c.sem("sa_s_dve")
        s_exp = c.sem("sa_s_exp")
        block = ctx.enter_context(nc.Block())
        HALVES = [slice(0, G), slice(G, P)]

        @block.gpsimd
        def _(pool):
            for m in (wq, wk, wv):
                nc.gpsimd.memset(m[:, :], 0.0).then_inc(s_zero, 1)
            nc.gpsimd.memset(tok[:, :, :], 0.0).then_inc(s_zero, 1)
            nc.gpsimd.memset(at[:, :, :], 0.0).then_inc(s_zero, 1)

        @block.sync
        def _(sp):
            sp.dma_start(wfx[:, :, :], a["L0_ffn_W_fx"].rearrange("(k p) f -> p k f", p=P)).then_inc(s_w, 16)
            sp.dma_start(bfx[:, :], row_to_all(a["L0_ffn_b_fx"], H0 * G)).then_inc(s_w, 16)
            sp.dma_start(wout[:, :, :], a["L0_ffn_W_out"].rearrange("(k p) f -> p k f", p=P)).then_inc(s_w, 16)
            sp.wait_ge(s_zero, 3)
            for m, n in ((wq, "q"), (wk, "k"), (wv, "v")):
                for h in HALVES:
                    sp.dma_start(m[h, h], a["L0_ffn_W_" + n]).then_inc(s_w, 16)
            sp.wait_ge(s_w, 9 * 16)

        @block.scalar
        def _(act):
            act.wait_ge(s_out, 5)
            for h in HALVES:
                r = nc.scalar.activation(at[h, :, h], sc[h, :, h], ACT.Exp, scale=float(G) ** -0.5)
            r.then_inc(s_exp, 1)

        @block.vector
        def _(dve):
            v = nc.vector
            link = Chain(dve, s_dve)

            def out(dst, src, n):
                dve.wait_ge(s_pe, n)
                v.tensor_copy(dst, src).then_inc(s_out, 1)

            def banked(b):
                return bank[b][:, :].rearrange("p (c j) -> p c j", c=NC)

            dve.wait_ge(s_pe, 1)
            v.tensor_copy(tt[:, 0, :, :], banked(0))
            v.tensor_copy(tt[:, 1, :, :], banked(1)).then_inc(s_out, 1)
            link(v.tensor_scalar(inv[:, :], tokens[:, :, D], EPS, None, ALU.add))
            link(v.reciprocal(inv[:, :], inv[:, :]))
            link(v.tensor_tensor(ni[:, :], tokens[:, :, D], inv[:, :], ALU.mult))
            dve.wait_ge(s_zero, 5)
            dve.wait_ge(s_w, 9 * 16)
            dve.wait_ge(s_pe, 2)
            for k in range(NC):
                for h in HALVES:
                    v.tensor_scalar(tok[h, k, h], banked(2)[h, k, h], inv[h, k:k + 1], None, ALU.mult)
            link(v.memset(mx[:, :], 0.0))
            for k in range(NC):
                for h in HALVES:
                    r = v.scalar_tensor_tensor(out=tok[h, k, h], in0=bfx[h, k * P + h.start:k * P + h.stop],
                                               scalar=ni[h, k:k + 1], in1=tok[h, k, h], op0=ALU.mult, op1=ALU.add)
            r.then_inc(s_out, 1)
            out(tokt[:, :, :], banked(3), 3)
            dve.wait_ge(s_pe, 4)
            v.tensor_copy(q[:, :, :], banked(4))
            v.tensor_copy(k_[:, :, :], banked(5))
            v.tensor_copy(v_[:, :, :], banked(6)).then_inc(s_out, 1)
            dve.wait_ge(s_pe, 5)
            for h in HALVES:
                r = v.tensor_reduce(mx[h, :], banked(7)[h, :, h], X, ALU.max)
            link(r)
            for h in HALVES:
                r = v.tensor_tensor(sc[h, :, h], banked(7)[h, :, h], bcast(mx[h, :].unsqueeze(2), [G, NC, G]),
                                    ALU.subtract)
            r.then_inc(s_out, 1)
            dve.wait_ge(s_exp, 1)
            for h in HALVES:
                r = v.reduce_sum(tot[h, :], at[h, :, h], X)
            link(r)
            link(v.reciprocal(rt[:, :], tot[:, :]))
            for h in HALVES:
                r = v.tensor_tensor(at[h, :, h], at[h, :, h], bcast(rt[h, :].unsqueeze(2), [G, NC, G]), ALU.mult)
            r.then_inc(s_out, 1)
            out(att[:, :, :], banked(0), 6)
            out(ost[:, :, :], banked(1), 7)
            dve.wait_ge(s_pe, 8)
            for k in range(NC):
                v.tensor_copy(pw[:, k, :], bank[2 + k // 2][:, k % 2 * D:k % 2 * D + D])

        @block.tensor
        def _(pe):
            mm, tp = nc.tensor.matmul, nc.tensor.transpose

            def part(b, k):
                return bank[b][:, k * P:k * P + P]

            for k in range(NC):
                for j in range(2):
                    r = tp(part(j, k), tokens[:, k, j * P:j * P + P], c.ident[:, :])
            r.then_inc(s_pe, 1)
            pe.wait_ge(s_w, 9 * 16)
            pe.wait_ge(s_out, 1)
            for k in range(NC):
                for j in range(2):
                    r = mm(part(2, k), tt[:, j, k, :], wfx[:, j, k * P:k * P + P], start=j == 0, stop=j == 1)
            r.then_inc(s_pe, 1)
            pe.wait_ge(s_out, 2)
            for k in range(NC):
                r = tp(part(3, k), tok[:, k, :], c.ident[:, :])
            r.then_inc(s_pe, 1)
            pe.wait_ge(s_out, 3)
            tk = tokt[:, :, :].rearrange("p c j -> p (c j)")
            mm(bank[4][:, :], wq[:, :], tk, start=True, stop=True)
            mm(bank[5][:, :], wk[:, :], tk, start=True, stop=True)
            for k in range(NC):
                r = mm(part(6, k), tokt[:, k, :], wv[:, :], start=True, stop=True)
            r.then_inc(s_pe, 1)
            pe.wait_ge(s_out, 4)
            for k in range(NC):
                r = mm(part(7, k), q[:, k, :], k_[:, k, :], start=True, stop=True)
            r.then_inc(s_pe, 1)
            pe.wait_ge(s_out, 6)
            for k in range(NC):
                r = tp(part(0, k), at[:, k, :], c.ident[:, :])
            r.then_inc(s_pe, 1)
            pe.wait_ge(s_out, 7)
            for k in range(NC):
                r = mm(part(1, k), v_[:, k, :], att[:, k, :], start=True, stop=True)
            r.then_inc(s_pe, 1)
            pe.wait_ge(s_out, 8)
            for k in range(NC):
                r = mm(bank[2 + k // 2][:, k % 2 * D:k % 2 * D + D], ost[:, k, :], wout[:, k, :],
                       start=True, stop=True)
            r.then_inc(s_pe, 1)


def slices_back(c, swt, pw):
    nc, a, bank = c.nc, c.a, c.bank
    NC = H0 * G // P
    with ExitStack() as ctx:
        c.stage = ctx

        def sb(name, shape, dt=F32):
            return c.sb(name, shape, dt, ctx)

        bout = sb("bout", [NP_, D])
        ring = sb("sb_ring", [P, 4, NC, NP_])
        sum_ = sb("sb_sum", [NP_, 2, D])
        norm = Norm(c, "n3", ctx)
        s_w = c.sem("sb_s_w")
        s_in = c.sem("sb_s_in")
        s_mm = c.sem("sb_s_mm")
        s_b = c.sem("sb_s_b")
        s_add = c.sem("sb_s_add")
        s_dve = c.sem("sb_s_dve")
        block = ctx.enter_context(nc.Block())

        @block.sync
        def _(sp):
            sp.dma_start(bout[:, :], row_to_all(a["L0_ffn_b_out"], D, NP_)).then_inc(s_w, 16)
            sp.wait_ge(s_w, 16)

        @block.scalar
        def _(act):
            def load(t, u):
                wait(act, s_mm, t - 3)
                nc.scalar.copy(ring[:, u, :, :], swt[:, :, bass.ds(t * NP_, NP_)]).then_inc(s_in, 1)

            each_node_tile(act, load)
            norm.root(act)

        @block.vector
        def _(dve):
            v = nc.vector
            link = Chain(dve, s_dve)
            dve.wait_ge(s_w, 16)

            def add(t, u):
                dve.wait_ge(s_mm, t + 1)
                v.tensor_tensor(sum_[:, u % 2, :], bank[u][0:NP_, 0:D], bout[:, :], ALU.add).then_inc(s_b, 1)
                dve.wait_ge(s_b, t + 1)
                v.tensor_tensor(flat(c.x, t), flat(c.x, t), sum_[:, u % 2, :], ALU.add).then_inc(s_add, 1)
                dve.wait_ge(s_add, t + 1)
                norm.tile(t)

            each_node_tile(dve, add)
            norm.finish(dve, link)

        @block.tensor
        def _(pe):
            def multiply(t, u):
                pe.wait_ge(s_in, t + 1)
                wait(pe, s_b, t - 3)
                for k in range(NC):
                    r = nc.tensor.matmul(bank[u][0:NP_, 0:D], ring[:, u, k, :], pw[:, k, :],
                                         start=k == 0, stop=k == NC - 1)
                r.then_inc(s_mm, 1)

            each_node_tile(pe, multiply)



def second_inputs(c, qk, v1):
    nc, a, bank = c.nc, c.a, c.bank
    QS = float(HC) ** 0.25
    with ExitStack() as ctx:
        c.stage = ctx

        def sb(name, shape, dt=F32):
            return c.sb(name, shape, dt, ctx)

        wy = sb("wy", [P, 2, 2 * P])
        wqkv = sb("wqkv", [P, 2, 3 * D])
        bqkv = sb("bqkv", [NP_, 3 * D])
        tempb = sb("tempb", [NP_, H0])
        f1 = sb("f1", [NP_, 2 * H0])
        f2 = sb("f2", [NP_, 2 * H0])
        zr = sb("si_zr", [NP_, 4, D])
        ztr = sb("si_ztr", [P, 2, 2 * NP_])
        yr = sb("si_yr", [NP_, 4, 2, P])
        sq = sb("si_sq", [NP_, 2, 2 * D])
        ss = sb("si_ss", [NP_, NT, 2 * H0])
        nrm = sb("si_nrm", [NP_, NT, 2 * H0])
        s_zero = c.sem("si_s_zero")
        s_w = c.sem("si_s_w")
        s_in = c.sem("si_s_in")
        s_tp = c.sem("si_s_tp")
        s_ztr = c.sem("si_s_ztr")
        s_mm = c.sem("si_s_mm")
        s_y = c.sem("si_s_y")
        s_yd = [c.sem(f"si_s_yd{u}") for u in range(4)]
        s_qkv = c.sem("si_s_qkv")
        s_sq = c.sem("si_s_sq")
        s_ss = c.sem("si_s_ss")
        s_nrm = c.sem("si_s_nrm")
        s_dve = c.sem("si_s_dve")
        block = ctx.enter_context(nc.Block())

        @block.gpsimd
        def _(pool):
            nc.gpsimd.memset(wy[:, :, :], 0.0).then_inc(s_zero, 1)
            nc.gpsimd.memset(v1[:, :, :, 0:1], 1.0)
            nc.gpsimd.memset(f1[:, 0:H0], QS)
            nc.gpsimd.memset(f1[:, H0:], 1.0)
            nc.gpsimd.memset(f2[:, :], QS).then_inc(s_zero, 1)

        @block.sync
        def _(sp):
            sp.dma_start(wqkv[0:MUL, 0, :], a["L1_mix_wqkvt"][0:MUL, :]).then_inc(s_w, 16)
            for d in range(3):
                lo = (1 + d) % 2 * MUL
                src = a["L1_mix_wqkvt"][MUL + d:MUL + d + 3 * MUL - 2:3, :]
                sp.dma_start(wqkv[lo:lo + MUL, (1 + d) // 2, :], src).then_inc(s_w, 16)
            sp.dma_start(bqkv[:, :], row_to_all(a["L1_mix_bqkv"], 3 * D, NP_)).then_inc(s_w, 16)
            sp.dma_start(tempb[:, :], row_to_all(a["L1_mix_temperature"], H0, NP_)).then_inc(s_w, 16)
            sp.wait_ge(s_zero, 1)
            for k, lo, kind in ((0, 0, "s"), (0, MUL, "v"), (1, 0, "v"), (1, MUL, "v")):
                for j, n in enumerate(("w1_", "wsc_")):
                    sp.dma_start(wy[lo:lo + MUL, k, j * P + lo:j * P + lo + MUL],
                                 a["L1_gnn_" + n + kind]).then_inc(s_w, 16)

            def store(t, u):
                sp.wait_ge(s_y, t + 1)
                sp.dma_start(c.y_dram[bass.ds(t * NP_, NP_), :],
                             yr[:, u, :, :].rearrange("p a b -> p (a b)")).then_inc(s_yd[u], 16)

            each_node_tile(sp, store)
            for u in range(4):
                sp.wait_ge(s_yd[u], 16 * (NT // UT + (u == 0)))

        @block.scalar
        def _(act):
            def load(t, u):
                wait(act, s_tp, t - 3)
                opts = dict(bias=column(c.shift, t), scale=column(c.rstd, t))
                nc.scalar.activation(zr[:, u, 0:MUL], flat(c.x, t)[:, 0:MUL], ACT.Identity, **opts)
                nc.scalar.activation(zr[:, u, MUL:D].rearrange("p (d m) -> p d m", d=3),
                                     flat(c.x, t)[:, MUL:D].rearrange("p (m d) -> p d m", d=3),
                                     ACT.Identity, **opts).then_inc(s_in, 1)

            def tile(t, u):
                if not (isinstance(t, int) and t >= NT - 2):
                    load(t + 2, (u + 2) % 4)
                act.wait_ge(s_mm, t + 1)
                if isinstance(t, int):
                    if t >= 4:
                        act.wait_ge(s_yd[u], t // 4 * 16)
                else:
                    act.wait_ge(s_yd[u], (t - u) * 4)
                y3 = bank[2 + u % 2][0:NP_, :].rearrange("p (k f) -> p k f", k=2)
                nc.scalar.activation(yr[:, u, :, :], y3[:, :, 0:P], ACT.Copy, scale=MUL ** -0.5)
                nc.scalar.activation(flat(c.z, t).rearrange("p (k f) -> p k f", k=2), y3[:, :, P:2 * P],
                                     ACT.Copy, scale=MUL ** -0.5).then_inc(s_y, 1)
                act.wait_ge(s_qkv, t + 1)
                wait(act, s_ss, t - 1)
                nc.scalar.activation(sq[:, u % 2, :], flat(qk, t), ACT.Square).then_inc(s_sq, 1)

            load(0, 0)
            load(1, 1)
            each_node_tile(act, tile)
            act.wait_ge(s_ss, NT)
            nc.scalar.activation(nrm[:, :, :], ss[:, :, :], ACT.Sqrt).then_inc(s_nrm, 1)

        @block.vector
        def _(dve):
            v = nc.vector
            link = Chain(dve, s_dve)
            dve.wait_ge(s_w, 14 * 16)
            dve.wait_ge(s_zero, 2)
            link(v.tensor_scalar(f2[:, 0:H0], tempb[:, :], QS * QS, None, ALU.mult))

            def turn(t, u):
                dve.wait_ge(s_tp, t + 1)
                wait(dve, s_mm, t - 1)
                v.tensor_copy(ztr[:, u % 2, :], bank[u % 2][:, 0:2 * NP_]).then_inc(s_ztr, 1)

            def reduce(t, u):
                dve.wait_ge(s_sq, t + 1)
                v.reduce_sum(flat(ss, t), sq[:, u % 2, :].rearrange("p (h d) -> p h d", d=HC), X).then_inc(s_ss, 1)

            def tile(t, u):
                if not (isinstance(t, int) and t == NT - 1):
                    turn(t + 1, (u + 1) % 4)
                dve.wait_ge(s_mm, t + 1)
                v.tensor_tensor(flat(qk, t), bank[4 + u % 2][0:NP_, :], bqkv[:, 0:2 * D], ALU.add)
                v.tensor_tensor(v1[:, bass.ds(t, 1), :, 1:].rearrange("p o h d -> p (o h) d"),
                                bank[6 + u % 2][0:NP_, 0:D].rearrange("p (h d) -> p h d", h=H0),
                                bqkv[:, 2 * D:].rearrange("p (h d) -> p h d", h=H0), ALU.add).then_inc(s_qkv, 1)
                if not (isinstance(t, int) and t == 0):
                    reduce(t - 1, (u + 3) % 4)

            turn(0, 0)
            each_node_tile(dve, tile)
            reduce(NT - 1, 0)
            dve.wait_ge(s_nrm, 1)
            shape = [NP_, NT, 2 * H0]
            link(v.tensor_tensor(nrm[:, :, :], nrm[:, :, :], bcast(f1[:, :].unsqueeze(1), shape), ALU.mult))
            link(v.tensor_scalar(nrm[:, :, :], nrm[:, :, :], 1e-12, None, ALU.max))
            link(v.reciprocal(nrm[:, :, :], nrm[:, :, :]))
            link(v.tensor_tensor(nrm[:, :, :], nrm[:, :, :], bcast(f2[:, :].unsqueeze(1), shape), ALU.mult))
            q3 = qk[:, :, :].rearrange("p t (h d) -> p (t h) d", d=HC)
            link(v.tensor_tensor(q3, q3, bcast(nrm[:, :, :].rearrange("p t h -> p (t h)").unsqueeze(2),
                                               [NP_, NT * 2 * H0, HC]), ALU.mult))

        @block.tensor
        def _(pe):
            mm = nc.tensor.matmul
            pe.wait_ge(s_w, 14 * 16)

            def turn(t, u):
                pe.wait_ge(s_in, t + 1)
                wait(pe, s_ztr, t - 1)
                for k in range(2):
                    r = nc.tensor.transpose(bank[u % 2][:, k * NP_:(k + 1) * NP_], zr[:, u, k * P:(k + 1) * P],
                                            c.ident[0:NP_, 0:NP_])
                r.then_inc(s_tp, 1)

            def tile(t, u):
                if not (isinstance(t, int) and t == NT - 1):
                    turn(t + 1, (u + 1) % 4)
                pe.wait_ge(s_ztr, t + 1)
                wait(pe, s_y, t - 1)
                wait(pe, s_qkv, t - 1)
                z = [ztr[:, u % 2, k * NP_:(k + 1) * NP_] for k in range(2)]
                for k in range(2):
                    mm(bank[2 + u % 2][0:NP_, k * D:k * D + D], z[k], wy[:, k, :], start=True, stop=True)
                for b, lo, n in ((4, 0, 2 * D), (6, 2 * D, D)):
                    for k in range(2):
                        r = mm(bank[b + u % 2][0:NP_, 0:n], z[k], wqkv[:, k, lo:lo + n], start=k == 0, stop=k == 1)
                r.then_inc(s_mm, 1)

            turn(0, 0)
            each_node_tile(pe, tile)


def second_mix(c, qk, v1):
    nc, bank = c.nc, c.bank
    A = 0.5
    SC2, SC4 = float(HC) ** 0.5, float(HC)
    NPAIR = HC * HC // 2
    FW = NPAIR + 2 * HC + 1
    NC = -(-FW // P)
    LAST = FW - (NC - 1) * P
    E1 = HC + 1
    CH = 5
    NCH = NT // CH
    with ExitStack() as ctx:
        c.stage = ctx

        def sb(name, shape, dt=F32):
            return c.sb(name, shape, dt, ctx)

        dbl = [sb(f"dbl{i}", [NP_, CH, 2 * HC]) for i in range(2)]
        feat = [sb(f"feat{i}", [NP_, CH, FW]) for i in range(2)]
        vals = [sb(f"vals{i}", [NP_, CH, E1]) for i in range(2)]
        wts = sb("wts", [P, NC])
        mt = sb("m2t", [E1, FW])
        m = sb("m2", [P, NC, E1])
        ft = sb("ft", [P, 2, NC * NP_])
        yt = sb("yt", [E1, 2, NP_])
        rden = sb("rden", [NP_, NCH, CH])
        s_c = c.sem("m2_s_c")
        s_dbl = c.sem("m2_s_dbl")
        s_sqr = c.sem("m2_s_sqr")
        s_feat = c.sem("m2_s_feat")
        s_used = c.sem("m2_s_used")
        s_mt = c.sem("m2_s_mt")
        s_m = c.sem("m2_s_m")
        s_mc = c.sem("m2_s_mc")
        s_ft = c.sem("m2_s_ft")
        s_ftc = c.sem("m2_s_ftc")
        s_yt = c.sem("m2_s_yt")
        s_ytc = c.sem("m2_s_ytc")
        s_go = c.sem("m2_s_go")
        s_y = c.sem("m2_s_y")
        s_den = c.sem("m2_s_den")
        s_out = c.sem("m2_s_out")
        block = ctx.enter_context(nc.Block())

        def heads(engine, run):
            run(0, True, False)
            with engine.Fori(1, H0 - 1) as h:
                run(h, False, False)
            run(H0 - 1, False, True)

        def cols(k):
            return slice(k * P, min(k * P + P, FW))

        @block.gpsimd
        def _(pool):
            nc.gpsimd.memset(wts[:, :], 2 * A / N)
            for i in range(2):
                r = nc.gpsimd.memset(feat[i][:, :, FW - 1:FW], 1.0)
            r.then_inc(s_c, 1)
            pool.wait_ge(s_c, 1)
            nc.gpsimd.memset(wts[96:P, NC - 2:NC - 1], A / N)
            nc.gpsimd.memset(wts[0:HC, NC - 1:NC], A / N)
            nc.gpsimd.memset(wts[HC:2 * HC, NC - 1:NC], SC2 / N)
            nc.gpsimd.memset(wts[2 * HC:LAST, NC - 1:NC], SC4 / N).then_inc(s_c, 1)
            pool.wait_ge(s_c, 2)

            def run(h, first, last):
                for n in range(2 * NCH):
                    s = n % 2
                    if n < 2:
                        wait(pool, s_ft, h * NT + (n - 1) * CH)
                    elif n < NCH + 2:
                        wait(pool, s_used, h * NCH + n - 1)
                    else:
                        wait(pool, s_ft, h * NT + (n - NCH - 1) * CH)
                    tiles = slice(n % NCH * CH, n % NCH * CH + CH)
                    src = qk[:, tiles, bass.ds(h * HC + (D if n < NCH else 0), HC)]
                    nc.gpsimd.tensor_copy(dbl[s][:, :, 0:HC], src)
                    nc.gpsimd.tensor_copy(dbl[s][:, :, HC:], src)
                    if n < NCH:
                        nc.gpsimd.tensor_copy(vals[s][:, :, :],
                                              v1[:, tiles, bass.ds(h, 1), :].rearrange("p t o e -> p t (o e)"))
                    nc.gpsimd.tensor_copy(feat[s][:, :, NPAIR + HC:NPAIR + 2 * HC], src).then_inc(s_dbl, 1)

            heads(pool, run)

        @block.scalar
        def _(act):
            def squares(h, n):
                s = n % 2
                act.wait_ge(s_dbl, h * 2 * NCH + n + 1)
                nc.scalar.activation(feat[s][:, :, NPAIR:NPAIR + HC], dbl[s][:, :, 0:HC], ACT.Square).then_inc(s_sqr, 1)

            def features(h, p):
                q = h * NT + p
                act.wait_ge(s_ft, q + 1)
                wait(act, s_yt, q - 1 if p else q)
                to = ft[:, p % 2, :]
                nc.scalar.copy(to[:, 0:4 * NP_], bank[2 + p % 2][:, 0:4 * NP_])
                nc.scalar.copy(to[0:LAST, 4 * NP_:], bank[4 + p % 2][0:LAST, 0:NP_]).then_inc(s_ftc, 1)

            def sums(h, p):
                q = h * NT + p
                act.wait_ge(s_yt, q + 1)
                wait(act, s_y, q - 1 if p else q)
                nc.scalar.copy(yt[:, p % 2, :], bank[4 + p % 2][0:E1, P:P + NP_]).then_inc(s_ytc, 1)

            def run(h, first, last):
                for n in range(0 if first else 1, NCH + 1):
                    squares(h, n)
                act.wait_ge(s_used, (h + 1) * NCH)
                nc.scalar.copy(mt[:, 0:NPAIR], bank[0][0:E1, :])
                nc.scalar.copy(mt[:, NPAIR:], bank[1][0:E1, 0:FW - NPAIR]).then_inc(s_mt, 1)
                features(h, 0)
                for p in range(NT):
                    if p % CH == 0 and p < NT - CH:
                        squares(h, NCH + p // CH + 1)
                    if p == NT - CH and not last:
                        squares(h + 1, 0)
                    if p + 1 < NT:
                        features(h, p + 1)
                    sums(h, p)

            heads(act, run)

        @block.vector
        def _(dve):
            v = nc.vector
            dve.wait_ge(s_c, 2)

            def products(h, n):
                s = n % 2
                dve.wait_ge(s_dbl, h * 2 * NCH + n + 1)
                one, two = dbl[s][:, :, :], feat[s][:, :, 0:NPAIR].rearrange("p t (s d) -> p t s d", d=HC)
                part = list(one.ap[0])
                fixed = bass.AP(tensor=one.tensor, offset=one.offset, ap=[part, [2 * HC, CH], [0, HC // 2], [1, HC]])
                moved = bass.AP(tensor=one.tensor, offset=one.offset + 1,
                                ap=[part, [2 * HC, CH], [1, HC // 2], [1, HC]])
                v.tensor_tensor(two, fixed, moved, ALU.mult).then_inc(s_feat, 1)

            def outputs(h, n):
                g = h * NCH + n
                dve.wait_ge(s_y, (g + 1) * CH)
                y3 = bank[6 + n % 2][0:NP_, 0:CH * E1].rearrange("p (t e) -> p t e", t=CH)
                v.reciprocal(rden[:, n, :], y3[:, :, 0]).then_inc(s_den, 1)
                dve.wait_ge(s_den, g + 1)
                v.tensor_tensor(qk[:, n * CH:n * CH + CH, bass.ds(h * HC, HC)], y3[:, :, 1:],
                                bcast(rden[:, n, :].unsqueeze(2), [NP_, CH, HC]), ALU.mult).then_inc(s_out, 1)

            def run(h, first, last):
                for n in range(NCH + 1):
                    products(h, n)
                    if n == 0 and not first:
                        outputs(h - 1, NCH - 1)
                dve.wait_ge(s_m, h + 1)
                m3 = bank[1][:, P:P + NC * E1].rearrange("p (c e) -> p c e", c=NC)
                w3 = bcast(wts[:, :].unsqueeze(2), [P, NC, E1])
                for r, k in ((slice(0, P), slice(0, NC - 1)), (slice(0, LAST), slice(NC - 1, NC))):
                    weighed = v.tensor_tensor(m[r, k, :], m3[r, k, :], w3[r, k, :], ALU.mult)
                weighed.then_inc(s_mc, 1)
                for n in range(1, NCH):
                    products(h, NCH + n)
                    outputs(h, n - 1)
                if last:
                    outputs(h, NCH - 1)

            heads(dve, run)

        @block.tensor
        def _(pe):
            mm = nc.tensor.matmul

            def keys(h, n):
                i = h * 2 * NCH + n
                pe.wait_ge(s_feat, i + 1)
                pe.wait_ge(s_sqr, i + 1)
                if n == 0:
                    wait(pe, s_mc, h)
                for k in range(CH):
                    for b, f in ((0, slice(0, NPAIR)), (1, slice(NPAIR, FW))):
                        r = mm(bank[b][0:E1, 0:f.stop - f.start], vals[n % 2][:, k, :], feat[n % 2][:, k, f],
                               start=n == 0 and k == 0, stop=n == NCH - 1 and k == CH - 1)
                r.then_inc(s_used, 1)

            def turn(h, p):
                q = h * NT + p
                if p % CH == 0:
                    i = h * 2 * NCH + NCH + p // CH
                    pe.wait_ge(s_feat, i + 1)
                    pe.wait_ge(s_sqr, i + 1)
                wait(pe, s_ftc, q - 1 if p else q)
                f = feat[(NCH + p // CH) % 2][:, p % CH, :]
                for j in range(NC - 1):
                    nc.tensor.transpose(bank[2 + p % 2][:, j * NP_:(j + 1) * NP_], f[:, cols(j)], c.ident[0:NP_, 0:NP_])
                wait(pe, s_ytc, q - 1 if p else q)
                pe.sem_inc(s_go, 1)
                nc.tensor.transpose(bank[4 + p % 2][0:LAST, 0:NP_], f[:, cols(NC - 1)],
                                    c.ident[0:NP_, 0:NP_]).then_inc(s_ft, 1)

            def query(h, p):
                q = h * NT + p
                pe.wait_ge(s_ftc, q + 1)
                y = bank[4 + p % 2][0:E1, P:P + NP_]
                from_ = ft[:, p % 2, :]
                for j in range(NC - 1):
                    mm(y, m[:, j, :], from_[:, j * NP_:(j + 1) * NP_], start=j == 0, stop=False)
                mm(y, m[0:LAST, NC - 1, :], from_[0:LAST, (NC - 1) * NP_:], start=False, stop=True).then_inc(s_yt, 1)

            def back(h, p):
                g = h * NCH + p // CH
                pe.wait_ge(s_ytc, h * NT + p + 1)
                if p % CH == 0:
                    wait(pe, s_out, g - 1)
                pe.sem_inc(s_go, 1)
                k = p % CH
                nc.tensor.transpose(bank[6 + p // CH % 2][0:NP_, k * E1:(k + 1) * E1], yt[:, p % 2, :],
                                    c.ident[0:E1, 0:E1]).then_inc(s_y, 1)

            def run(h, first, last):
                for n in range(NCH):
                    keys(h, n)
                turn(h, 0)
                pe.wait_ge(s_mt, h + 1)
                pe.sem_inc(s_go, 1)
                for j in range(NC):
                    r = nc.tensor.transpose(bank[1][0:cols(j).stop - cols(j).start, P + j * E1:P + (j + 1) * E1],
                                            mt[:, cols(j)], c.ident[0:E1, 0:E1])
                r.then_inc(s_m, 1)
                for p in range(NT):
                    if p + 1 < NT:
                        turn(h, p + 1)
                    if p == 0:
                        pe.wait_ge(s_mc, h + 1)
                    query(h, p)
                    if p:
                        back(h, p - 1)
                back(h, NT - 1)

            heads(pe, run)


def mix_out(c, qk):
    nc, a, bank = c.nc, c.a, c.bank
    with ExitStack() as ctx:
        c.stage = ctx

        def sb(name, shape, dt=F32):
            return c.sb(name, shape, dt, ctx)

        wp = sb("wp", [P, 2, D])
        bp = sb("bp", [NP_, D])
        zr = sb("mo_zr", [NP_, 4, D])
        ztr = sb("mo_ztr", [P, 2, 2 * NP_])
        sum_ = sb("mo_sum", [NP_, 2, D])
        s_w = c.sem("mo_s_w")
        s_in = c.sem("mo_s_in")
        s_tp = c.sem("mo_s_tp")
        s_ztr = c.sem("mo_s_ztr")
        s_mm = c.sem("mo_s_mm")
        s_b = c.sem("mo_s_b")
        block = ctx.enter_context(nc.Block())

        @block.sync
        def _(sp):
            sp.dma_start(wp[:, :, :], a["L1_mix_wprojt"].rearrange("(k p) f -> p k f", p=P)).then_inc(s_w, 16)
            sp.dma_start(bp[:, :], row_to_all(a["L1_mix_bproj"], D, NP_)).then_inc(s_w, 16)
            sp.wait_ge(s_w, 32)

        @block.scalar
        def _(act):
            def load(t, u):
                wait(act, s_tp, t - 3)
                nc.scalar.copy(zr[:, u, :], flat(qk, t)[:, 0:D]).then_inc(s_in, 1)

            each_node_tile(act, load)

        @block.vector
        def _(dve):
            v = nc.vector
            dve.wait_ge(s_w, 32)

            def turn(t, u):
                dve.wait_ge(s_tp, t + 1)
                wait(dve, s_mm, t - 1)
                v.tensor_copy(ztr[:, u % 2, :], bank[u % 2][:, 0:2 * NP_]).then_inc(s_ztr, 1)

            def tile(t, u):
                if not (isinstance(t, int) and t == NT - 1):
                    turn(t + 1, (u + 1) % 4)
                dve.wait_ge(s_mm, t + 1)
                v.tensor_tensor(sum_[:, u % 2, :], bank[2 + u % 2][0:NP_, 0:D], bp[:, :], ALU.add).then_inc(s_b, 1)
                dve.wait_ge(s_b, t + 1)
                v.tensor_tensor(flat(c.x, t), flat(c.x, t), sum_[:, u % 2, :], ALU.add)

            turn(0, 0)
            each_node_tile(dve, tile)

        @block.tensor
        def _(pe):
            def turn(t, u):
                pe.wait_ge(s_in, t + 1)
                wait(pe, s_ztr, t - 1)
                for k in range(2):
                    r = nc.tensor.transpose(bank[u % 2][:, k * NP_:(k + 1) * NP_], zr[:, u, k * P:(k + 1) * P],
                                            c.ident[0:NP_, 0:NP_])
                r.then_inc(s_tp, 1)

            def tile(t, u):
                if not (isinstance(t, int) and t == NT - 1):
                    turn(t + 1, (u + 1) % 4)
                pe.wait_ge(s_ztr, t + 1)
                wait(pe, s_b, t - 1)
                for k in range(2):
                    r = nc.tensor.matmul(bank[2 + u % 2][0:NP_, 0:D], ztr[:, u % 2, k * NP_:(k + 1) * NP_],
                                         wp[:, k, :], start=k == 0, stop=k == 1)
                r.then_inc(s_mm, 1)

            pe.wait_ge(s_w, 32)
            turn(0, 0)
            each_node_tile(pe, tile)



GM = 4
NG = ST // GM
GR = UN // GM


def second_edges(c, acc):
    nc, a, bank = c.nc, c.a, c.bank
    NB = 8
    PRODS = AG + 2 * MUL
    with ExitStack() as ctx:
        c.stage = ctx

        def sb(name, shape, dt=F32):
            return c.sb(name, shape, dt, ctx)

        rec = c.rec
        idx_ring = [sb(f"e1_idx{h}", [P, UN // 2], I32) for h in range(2)]
        g = sb("e1_g", [P, UN, D + 3 * MUL])
        w1 = sb("e1_w1", [GM * NB, 2, P])
        w2 = sb("e1_w2", [P, P])
        w3 = sb("e1_w3", [P, 4 * MUL])
        attr = sb("e1_attr", [P, GR, GM * NB])
        attr_t = sb("e1_attr_t", [GM * NB, GR, P])
        h1 = sb("e1_h1", [P, GR, 2 * P])
        h2 = sb("e1_h2", [P, GR, 2 * P])
        oh = sb("e1_oh", [P, 4, NP_])
        ws = sb("e1_ws", [P, 4, 6 * MUL])
        prod = sb("e1_prod", [P, 4, PRODS])
        s_zero = c.sem("e1_s_zero")
        s_w = c.sem("e1_s_w")
        s_w3 = c.sem("e1_s_w3")
        s_rec = c.sem("e1_s_rec")
        s_ring = c.sem("e1_s_ring")
        s_got = c.s_got
        s_at = c.sem("e1_s_at")
        s_tp = c.sem("e1_s_tp")
        s_att = c.sem("e1_s_att")
        s_l1 = c.sem("e1_s_l1")
        s_h1 = c.sem("e1_s_h1")
        s_l2 = c.sem("e1_s_l2")
        s_h2 = c.sem("e1_s_h2")
        s_wt = c.sem("e1_s_wt")
        s_oh = c.sem("e1_s_oh")
        s_ws = c.sem("e1_s_ws")
        s_dot = c.sem("e1_s_dot")
        s_prod = c.sem("e1_s_prod")
        s_agg = c.sem("e1_s_agg")
        s_acc = c.sem("e1_s_acc")
        block = ctx.enter_context(nc.Block())

        def rounds(engine, body):
            for u in range(UN):
                body(0, u, False)
            with engine.Fori(1, ST // UN - 1) as i:
                for u in range(UN):
                    body(i, u, False)
            for u in range(UN):
                body(ST // UN - 1, u, True)

        @block.sync
        def _(sp):
            sp.dma_start(rec[:, :, :], c.rec_dram.rearrange("(p j) f -> p j f", p=P)).then_inc(s_rec, 16)
            for h in range(2):
                sp.dma_start(w3[h * MUL:h * MUL + MUL, :], a["L1_gnn_fc_w3"]).then_inc(s_w, 16)
            sp.wait_ge(s_zero, 2)
            for q in range(2):
                sp.dma_start(w2[q * MUL:q * MUL + MUL, q * MUL:q * MUL + MUL], a["L1_gnn_fc_w2"]).then_inc(s_w, 16)
            for j in range(GM):
                lo = j % 2 * MUL
                sp.dma_start(w1[j * NB:j * NB + NB, j // 2, lo:lo + MUL], a["L1_gnn_fc_w1"]).then_inc(s_w, 16)
            sp.wait_ge(s_w, 8 * 16)

        @block.gpsimd
        def _(pool):
            nc.gpsimd.memset(w1[:, :, :], 0.0).then_inc(s_zero, 1)
            nc.gpsimd.memset(w2[:, :], 0.0).then_inc(s_zero, 1)
            pool.wait_ge(s_rec, 16)
            gather_rows(c, pool, c.y_dram, idx_ring, [g[:, u, 0:D] for u in range(UN)], s_ring, s_prod, s_got, rec)

        @block.scalar
        def _(act):
            def attributes(g_, k):
                nc.scalar.copy(attr[:, k % GR, :].rearrange("p (j b) -> p j b", j=GM),
                               rec[:, bass.ds(g_ * GM, GM), R_ATTR:R_ATTR + NB]).then_inc(s_at, 1)

            def turned(g_, k):
                act.wait_ge(s_tp, g_ + 1)
                nc.scalar.copy(attr_t[:, k % GR, :], bank[0][0:GM * NB, 0:P]).then_inc(s_att, 1)

            def layer1(g_, k):
                act.wait_ge(s_l1, g_ + 1)
                nc.scalar.activation(h1[:, k % GR, :], bank[0][:, P:3 * P], ACT.Silu,
                                     scale=float(NB) ** -0.5).then_inc(s_h1, 1)

            def layer2(g_, k):
                act.wait_ge(s_l2, g_ + 1)
                nc.scalar.activation(h2[:, k % GR, :], bank[1][:, 0:2 * P], ACT.Silu,
                                     scale=float(MUL) ** -0.5).then_inc(s_h2, 1)

            def scaled(j, u):
                act.wait_ge(s_wt, j + 1)
                wait(act, s_prod, j - 3)
                w, to, sh = bank[2 + u % 2], ws[:, u % 4, :], flat(rec, j)[:, R_SH:R_SH + 4]
                nc.scalar.activation(to[:, 0:4 * MUL + MUL].rearrange("p (b f) -> p b f", f=MUL)[:, 0:5:4, :],
                                     w[:, 0:3 * MUL].rearrange("p (b f) -> p b f", f=MUL)[:, 0:3:2, :],
                                     ACT.Copy, scale=sh[:, 0:1])
                for d in range(1, 4):
                    nc.scalar.activation(to[:, d * MUL:(d + 1) * MUL], w[:, MUL:2 * MUL], ACT.Copy,
                                         scale=sh[:, d:d + 1])
                nc.scalar.copy(to[:, 5 * MUL:], w[:, 3 * MUL:4 * MUL]).then_inc(s_ws, 1)

            def tile(i, u, last):
                j, g_, k, at = i * UN + u, i * GR + u // GM, u // GM, u % GM
                left = NG - 1 - g_ if last else GR
                if at == 0 and left >= 1:
                    layer2(g_ + 1, k + 1)
                if at == 1 and left >= 2:
                    attributes(g_ + 2, k + 2)
                if at == 2 and left >= 2:
                    turned(g_ + 2, k + 2)
                if at == 3 and left >= 2:
                    layer1(g_ + 2, k + 2)
                if not (last and u >= UN - 3):
                    scaled(j + 3, u + 3)

            act.wait_ge(s_rec, 16)
            attributes(0, 0)
            attributes(1, 1)
            turned(0, 0)
            layer1(0, 0)
            layer2(0, 0)
            turned(1, 1)
            layer1(1, 1)
            for u in range(3):
                scaled(u, u)
            rounds(act, tile)

        @block.vector
        def _(dve):
            v = nc.vector
            v.memset(acc[:, :, :], 0.0).then_inc(s_acc, 1)
            dve.wait_ge(s_w, 8 * 16)
            v.tensor_scalar(w3[:, 0:3 * MUL], w3[:, 0:3 * MUL], MUL ** -0.5, None, ALU.mult)
            v.tensor_scalar(w3[:, 3 * MUL:], w3[:, 3 * MUL:], MUL ** -0.5 * 0.5773502691896258, None,
                            ALU.mult).then_inc(s_w3, 1)
            dve.wait_ge(s_rec, 16)

            def one_hot(j, u):
                v.tensor_scalar(oh[:, u % 4, :], c.iota[:, :], flat(rec, j)[:, R_LOCAL:R_LOCAL + 1], None,
                                ALU.is_equal).then_inc(s_oh, 1)

            def dots(i, j, u):
                dve.wait_ge(s_got[u % UN], (i + ST // UN0) * 16 + 16)
                y = g[:, u % UN, :]
                v.tensor_tensor(y[:, D:].rearrange("p (d f) -> p d f", d=3),
                                y[:, MUL:D].rearrange("p (d f) -> p d f", d=3),
                                bcast(flat(rec, j)[:, R_SH + 1:R_SH + 4].unsqueeze(2), [P, 3, MUL]),
                                ALU.mult).then_inc(s_dot, 1)

            def products(j, u):
                dve.wait_ge(s_ws, j + 1)
                dve.wait_ge(s_dot, j + 1)
                w, y, to = ws[:, u % 4, :], g[:, u % UN, :], prod[:, u % 4, :]
                v.tensor_tensor(to[:, 0:4 * MUL].rearrange("p (b f) -> p b f", b=4),
                                w[:, 0:4 * MUL].rearrange("p (b f) -> p b f", b=4),
                                bcast(y[:, 0:MUL].unsqueeze(1), [P, 4, MUL]), ALU.mult)
                v.tensor_tensor(to[:, 4 * MUL:].rearrange("p (b d f) -> p b d f", b=2, d=3),
                                bcast(w[:, 4 * MUL:].rearrange("p (b f) -> p b f", b=2).unsqueeze(2), [P, 2, 3, MUL]),
                                y[:, MUL:].rearrange("p (b d f) -> p b d f", b=2, d=3), ALU.mult).then_inc(s_prod, 1)

            def tile(i, u, last):
                j = i * UN + u
                if u == 0:
                    indices(c, idx_ring, rec, i, 1, s_ring)
                if u == UN // 2 and not last:
                    indices(c, idx_ring, rec, i + 1, 0, s_ring)
                if not (last and u >= UN - 2):
                    one_hot(j + 2, u + 2)
                if not (last and u >= UN - 3):
                    dots(i + (u + 3) // UN, j + 3, u + 3)
                if not (last and u >= UN - 2):
                    products(j + 2, u + 2)
                b = dve.value_load(c.bucket_of[0:1, bass.ds(j, 1)], min_val=0, max_val=NT)
                dve.wait_ge(s_agg, j + 1)
                dve.wait_ge(s_acc, j + 1)
                v.tensor_tensor(flat(acc, b), flat(acc, b), bank[4 + u % 4][0:NP_, :], ALU.add).then_inc(s_acc, 1)

            one_hot(0, 0)
            one_hot(1, 1)
            indices(c, idx_ring, rec, 0, 0, s_ring)
            for u in range(3):
                dots(0, u, u)
            products(0, 0)
            products(1, 1)
            rounds(dve, tile)

        @block.tensor
        def _(pe):
            mm = nc.tensor.matmul

            def turn(g_, k):
                pe.wait_ge(s_at, g_ + 1)
                wait(pe, s_h1, g_)
                nc.tensor.transpose(bank[0][0:GM * NB, 0:P], attr[:, k % GR, :], c.ident[:, :]).then_inc(s_tp, 1)

            def layer1(g_, k):
                pe.wait_ge(s_att, g_ + 1)
                for q in range(2):
                    r = mm(bank[0][:, (1 + q) * P:(2 + q) * P], w1[:, q, :], attr_t[:, k % GR, :],
                           start=True, stop=True)
                r.then_inc(s_l1, 1)

            def layer2(g_, k):
                pe.wait_ge(s_h1, g_ + 1)
                wait(pe, s_h2, g_)
                mm(bank[1][:, 0:2 * P], w2[:, :], h1[:, k % GR, :], start=True, stop=True).then_inc(s_l2, 1)

            def weights(g_, j, u):
                pe.wait_ge(s_h2, g_ + 1)
                wait(pe, s_ws, j - 1)
                half, pair = slice(u % 2 * MUL, u % 2 * MUL + MUL), u % GM // 2
                mm(bank[2 + u % 2][:, 0:4 * MUL], h2[half, u // GM % GR, pair * P:pair * P + P], w3[half, :],
                   start=True, stop=True).then_inc(s_wt, 1)

            def sums(j, u):
                pe.wait_ge(s_prod, j + 1)
                pe.wait_ge(s_oh, j + 1)
                wait(pe, s_acc, j - 2)
                p4 = prod[:, u % 4, :]
                to = bank[4 + u % 4][0:NP_, :]
                mm(to, oh[:, u % 4, :], p4[:, 0:AG], start=True, stop=False)
                for d in range(2):
                    r = mm(to[:, AG - MUL:], oh[:, u % 4, :], p4[:, AG + d * MUL:AG + (d + 1) * MUL],
                           start=False, stop=d == 1)
                r.then_inc(s_agg, 1)

            def tile(i, u, last):
                j, g_, k, at = i * UN + u, i * GR + u // GM, u // GM, u % GM
                left = NG - 1 - g_ if last else GR
                if at == 0 and left >= 1:
                    layer2(g_ + 1, k + 1)
                if at == 2 and left >= 2:
                    turn(g_ + 2, k + 2)
                if at == 3 and left >= 2:
                    layer1(g_ + 2, k + 2)
                if not (last and u >= UN - 3):
                    weights(i * GR + (u + 3) // GM, j + 3, u + 3)
                sums(j, u)

            pe.wait_ge(s_w3, 1)
            turn(0, 0)
            layer1(0, 0)
            layer2(0, 0)
            turn(1, 1)
            layer1(1, 1)
            for u in range(3):
                weights(0, u, u)
            rounds(pe, tile)


def second_nodes(c, acc):
    nc, a, bank = c.nc, c.a, c.bank
    with ExitStack() as ctx:
        c.stage = ctx

        def sb(name, shape, dt=F32):
            return c.sb(name, shape, dt, ctx)

        w2 = sb("sn_w2", [P, 2, MUL])
        gain = sb("sn_gain", [NP_, D])
        dn = sb("sn_dn", [NP_, NT])
        root = sb("sn_root", [NP_, NT])
        rows_in = sb("sn_rows", [NP_, 4, AG])
        cols_in = sb("sn_cols", [P, 2, 4 * NP_])
        junk = sb("sn_junk", [NP_, D])
        ss = sb("sn_ss", [NP_, NT, 2])
        rms = sb("sn_rms", [NP_, NT, 2])
        norm = Norm(c, "n4", ctx)
        s_w = c.sem("sn_s_w")
        s_dn = c.sem("sn_s_dn")
        s_root = c.sem("sn_s_root")
        s_in = c.sem("sn_s_in")
        s_tp = c.sem("sn_s_tp")
        s_cols = c.sem("sn_s_cols")
        s_mm = c.sem("sn_s_mm")
        s_add = c.sem("sn_s_add")
        s_ss = c.sem("sn_s_ss")
        s_ms = c.sem("sn_s_ms")
        s_rms = c.sem("sn_s_rms")
        s_dve = c.sem("sn_s_dve")
        block = ctx.enter_context(nc.Block())

        @block.sync
        def _(sp):
            sp.dma_start(w2[:, 0, :], a["L1_gnn_w2_s"]).then_inc(s_w, 16)
            sp.dma_start(w2[:, 1, :], a["L1_gnn_w2_v"]).then_inc(s_w, 16)
            sp.dma_start(gain[:, 0:MUL], row_to_all(a["L1_gnn_g_s"], MUL, NP_)).then_inc(s_w, 16)
            for d in range(3):
                sp.dma_start(gain[:, (1 + d) * MUL:(2 + d) * MUL], row_to_all(a["L1_gnn_g_v"], MUL, NP_)).then_inc(s_w, 16)
            sp.wait_ge(s_w, 6 * 16)

        @block.scalar
        def _(act):
            act.wait_ge(s_dn, 1)
            nc.scalar.activation(root[:, :], root[:, :], ACT.Sqrt).then_inc(s_root, 1)
            act.wait_ge(s_dn, 2)

            def load(t, u):
                wait(act, s_tp, t - 3)
                src, to = flat(acc, t), rows_in[:, u, :]
                to3 = to[:, P:].rearrange("p (d f) -> p d f", d=3)
                by = column(dn, t)
                nc.scalar.activation(to[:, 0:P].rearrange("p (b f) -> p b f", b=2),
                                     src.rearrange("p (b f) -> p b f", b=8)[:, 0:8:7, :], ACT.Copy, scale=by)
                nc.scalar.activation(to3[:, :, 0:MUL], src[:, MUL:4 * MUL].rearrange("p (d f) -> p d f", d=3),
                                     ACT.Copy, scale=by)
                nc.scalar.activation(to3[:, :, MUL:], src[:, 4 * MUL:7 * MUL].rearrange("p (d f) -> p d f", d=3),
                                     ACT.Copy, scale=by).then_inc(s_in, 1)

            def tile(t, u):
                if not (isinstance(t, int) and t >= NT - 2):
                    load(t + 2, (u + 2) % 4)
                act.wait_ge(s_add, t + 1)
                for k, lo, hi in ((0, 0, MUL), (1, MUL, D)):
                    if k == 0:
                        wait(act, s_ss, t)
                    r = nc.scalar.activation(junk[:, lo:hi], flat(c.z, t)[:, lo:hi], ACT.Square,
                                             accum_out=flat(ss, t)[:, k:k + 1])
                r.then_inc(s_ss, 1)

            load(0, 0)
            load(1, 1)
            each_node_tile(act, tile)
            act.wait_ge(s_ms, 1)
            nc.scalar.activation(rms[:, :, :], rms[:, :, :], ACT.Sqrt).then_inc(s_rms, 1)
            norm.root(act)

        @block.vector
        def _(dve):
            v = nc.vector
            link = Chain(dve, s_dve)
            v.tensor_scalar(root[:, :], c.deg[:, :], 1.0, None, ALU.max).then_inc(s_dn, 1)
            dve.wait_ge(s_w, 6 * 16)
            link(v.tensor_scalar(w2[:, :, :], w2[:, :, :], (2.0 * MUL) ** -0.5, None, ALU.mult))
            dve.wait_ge(s_root, 1)
            v.reciprocal(dn[:, :], root[:, :]).then_inc(s_dn, 1)

            def turn(t, u):
                dve.wait_ge(s_tp, t + 1)
                wait(dve, s_mm, t - 1)
                v.tensor_copy(cols_in[:, u % 2, :], bank[u % 2][:, 0:4 * NP_]).then_inc(s_cols, 1)

            def tile(t, u):
                if not (isinstance(t, int) and t == NT - 1):
                    turn(t + 1, (u + 1) % 4)
                dve.wait_ge(s_mm, t + 1)
                v.tensor_tensor(flat(c.z, t), flat(c.z, t), bank[2 + u % 2][0:NP_, 0:D], ALU.add).then_inc(s_add, 1)

            turn(0, 0)
            each_node_tile(dve, tile)
            dve.wait_ge(s_ss, NT)
            link(v.tensor_scalar(rms[:, :, 0], ss[:, :, 0], 1.0 / MUL, EPS, ALU.mult, ALU.add))
            v.tensor_scalar(rms[:, :, 1], ss[:, :, 1], 1.0 / (3 * MUL), EPS, ALU.mult, ALU.add).then_inc(s_ms, 1)
            dve.wait_ge(s_rms, 1)
            link(v.reciprocal(rms[:, :, :], rms[:, :, :]))
            for k, lo, hi in ((0, 0, MUL), (1, MUL, D)):
                z3 = c.z[:, :, lo:hi]
                link(v.tensor_tensor(z3, z3, bcast(rms[:, :, k:k + 1], [NP_, NT, hi - lo]), ALU.mult))
            link(v.tensor_tensor(c.z[:, :, :], c.z[:, :, :], bcast(gain[:, :].unsqueeze(1), [NP_, NT, D]), ALU.mult))
            v.tensor_tensor(c.x[:, :, 0:MUL], c.x[:, :, 0:MUL], c.z[:, :, 0:MUL], ALU.add)
            x4 = c.x[:, :, MUL:].rearrange("p t (m d) -> p t d m", d=3)
            link(v.tensor_tensor(x4, x4, c.z[:, :, MUL:].rearrange("p t (d m) -> p t d m", d=3), ALU.add))
            each_node_tile(dve, lambda t, u: norm.tile(t))
            norm.finish(dve, link)

        @block.tensor
        def _(pe):
            def turn(t, u):
                pe.wait_ge(s_in, t + 1)
                wait(pe, s_cols, t - 1)
                for k in range(4):
                    r = nc.tensor.transpose(bank[u % 2][:, k * NP_:(k + 1) * NP_],
                                            rows_in[:, u, k * P:(k + 1) * P], c.ident[0:NP_, 0:NP_])
                r.then_inc(s_tp, 1)

            def tile(t, u):
                if not (isinstance(t, int) and t == NT - 1):
                    turn(t + 1, (u + 1) % 4)
                pe.wait_ge(s_cols, t + 1)
                wait(pe, s_add, t - 1)
                for k in range(4):
                    r = nc.tensor.matmul(bank[2 + u % 2][0:NP_, k * MUL:(k + 1) * MUL],
                                         cols_in[:, u % 2, k * NP_:(k + 1) * NP_], w2[:, min(k, 1), :],
                                         start=True, stop=True)
                r.then_inc(s_mm, 1)

            pe.wait_ge(s_dn, 2)
            turn(0, 0)
            each_node_tile(pe, tile)


NE, FH = 8, 512
MG = 4
GROUPS = [(t, min(MG, NT - t)) for t in range(0, NT, MG)]


def route(c, z4t, wfull):
    nc, a, bank = c.nc, c.a, c.bank
    with ExitStack() as ctx:
        c.stage = ctx

        def sb(name, shape, dt=F32):
            return c.sb(name, shape, dt, ctx)

        gamma = sb("gamma", [P, 2])
        beta = sb("beta", [P, 2])
        wr = sb("wr", [P, 2, NE])
        br = sb("br", [NE, 1])
        b2 = sb("b2", [NE, D])
        zr = sb("ro_zr", [NP_, 4, D])
        lgt = sb("ro_lgt", [NE, N])
        lg = sb("ro_lg", [NP_, NT, NE])
        gt = sb("ro_gt", [NP_, NT, NE, NE])
        eq = sb("ro_eq", [NP_, NT, NE, NE])
        earlier = sb("ro_earlier", [P, NE, NE])
        mx = sb("ro_mx", [NP_, NT])
        rank = sb("ro_rank", [NP_, NT, NE])
        ex = sb("ro_ex", [NP_, NT, NE])
        tot = sb("ro_tot", [NP_, NT])
        inv = sb("ro_inv", [NP_, NT])
        wt = sb("ro_wt", [NE, N])
        s_w = c.sem("ro_s_w")
        s_one = c.sem("ro_s_one")
        s_in = c.sem("ro_s_in")
        s_tp = c.sem("ro_s_tp")
        s_z = c.sem("ro_s_z")
        s_lg = c.sem("ro_s_lg")
        s_lgt = c.sem("ro_s_lgt")
        s_back = c.sem("ro_s_back")
        s_sub = c.sem("ro_s_sub")
        s_exp = c.sem("ro_s_exp")
        s_wf = c.sem("ro_s_wf")
        s_wtp = c.sem("ro_s_wtp")
        s_wt = c.sem("ro_s_wt")
        s_b2 = c.sem("ro_s_b2")
        s_add = c.sem("ro_s_add")
        s_dve = c.sem("ro_s_dve")
        block = ctx.enter_context(nc.Block())
        SIX = [(n, min(4 * NP_, N - n)) for n in range(0, N, 4 * NP_)]

        @block.gpsimd
        def _(pool):
            nc.gpsimd.memset(earlier[:, :, :], 1.0).then_inc(s_one, 1)
            pool.wait_ge(s_one, 1)
            nc.gpsimd.affine_select(out=earlier[:, :, :], in_=earlier[:, :, :], compare_op=ALU.is_gt, fill=0.0,
                                    base=0, pattern=[[1, NE], [-1, NE]], channel_multiplier=0).then_inc(s_one, 1)

        @block.sync
        def _(sp):
            with nc.allow_non_contiguous_dma("one column per chunk"):
                for k in range(2):
                    sp.dma_start(gamma[:, k:k + 1], a["L1_ffn_gamma"][k * P:k * P + P].unsqueeze(1)).then_inc(s_w, 16)
                    sp.dma_start(beta[:, k:k + 1], a["L1_ffn_beta"][k * P:k * P + P].unsqueeze(1)).then_inc(s_w, 16)
                sp.dma_start(br[:, :], a["L1_ffn_br"].unsqueeze(1)).then_inc(s_w, 16)
            sp.dma_start(wr[:, :, :], a["L1_ffn_Wr"].rearrange("(k p) e -> p k e", p=P)).then_inc(s_w, 16)
            sp.dma_start(b2[:, :], a["L1_ffn_b2"]).then_inc(s_w, 16)
            sp.wait_ge(s_w, 7 * 16)

        @block.scalar
        def _(act):
            def load(t, u):
                wait(act, s_tp, t - 3)
                nc.scalar.activation(zr[:, u, :], flat(c.x, t), ACT.Identity, bias=column(c.shift, t),
                                     scale=column(c.rstd, t)).then_inc(s_in, 1)

            each_node_tile(act, load)
            act.wait_ge(s_sub, 1)
            nc.scalar.activation(ex[:, :, :], lg[:, :, :], ACT.Exp).then_inc(s_exp, 1)

        @block.vector
        def _(dve):
            v = nc.vector
            link = Chain(dve, s_dve)
            dve.wait_ge(s_w, 7 * 16)
            dve.wait_ge(s_one, 2)

            def tile(t, u):
                dve.wait_ge(s_tp, t + 1)
                for k in range(2):
                    r = v.tensor_scalar(z4t[:, k, bass.ds(t * NP_, NP_)], bank[u % 2][:, k * NP_:(k + 1) * NP_],
                                        gamma[:, k:k + 1], beta[:, k:k + 1], ALU.mult, ALU.add)
                r.then_inc(s_z, 1)

            each_node_tile(dve, tile)
            for i, (n, w) in enumerate(SIX):
                dve.wait_ge(s_lg, i + 1)
                v.tensor_scalar(lgt[:, n:n + w], bank[2 + i % 2][0:NE, 0:w], br[:, 0:1], None, ALU.add).then_inc(s_lgt, 1)
            dve.wait_ge(s_back, 1)
            link(v.tensor_copy(lg[:, :, :].rearrange("p t e -> p (t e)"), bank[4][0:NP_, 0:NT * NE]))
            full = [NP_, NT, NE, NE]
            mine, other = bcast(lg[:, :, :].unsqueeze(3), full), bcast(lg[:, :, :].unsqueeze(2), full)
            v.tensor_tensor(gt[:, :, :, :], other, mine, ALU.is_gt)
            link(v.tensor_tensor(eq[:, :, :, :], other, mine, ALU.is_equal))
            e3 = eq[:, :, :, :].rearrange("p t a b -> p t (a b)")
            link(v.tensor_tensor(e3, e3, bcast(earlier[0:NP_, :, :].rearrange("p a b -> p (a b)").unsqueeze(1),
                                               [NP_, NT, NE * NE]), ALU.mult))
            link(v.tensor_tensor(gt[:, :, :, :], gt[:, :, :, :], eq[:, :, :, :], ALU.add))
            v.tensor_reduce(mx[:, :], lg[:, :, :], X, ALU.max)
            link(v.reduce_sum(rank[:, :, :], gt[:, :, :, :], X))
            v.tensor_tensor(lg[:, :, :], lg[:, :, :], bcast(mx[:, :].unsqueeze(2), [NP_, NT, NE]),
                            ALU.subtract).then_inc(s_sub, 1)
            dve.wait_ge(s_exp, 1)
            link(v.tensor_scalar(rank[:, :, :], rank[:, :, :], 2.0, None, ALU.is_lt))
            link(v.tensor_tensor(ex[:, :, :], ex[:, :, :], rank[:, :, :], ALU.mult))
            link(v.reduce_sum(tot[:, :], ex[:, :, :], X))
            link(v.reciprocal(inv[:, :], tot[:, :]))
            v.tensor_tensor(wfull[:, :, :], ex[:, :, :], bcast(inv[:, :].unsqueeze(2), [NP_, NT, NE]),
                            ALU.mult).then_inc(s_wf, 1)
            for i, (n, w) in enumerate(SIX):
                dve.wait_ge(s_wtp, i + 1)
                v.tensor_copy(wt[:, n:n + w], bank[5 + i % 2][0:NE, 0:w]).then_inc(s_wt, 1)
            for t in range(NT):
                dve.wait_ge(s_b2, t + 1)
                v.tensor_tensor(c.x[:, t, :], c.x[:, t, :], bank[t % 4][0:NP_, 0:D], ALU.add).then_inc(s_add, 1)

        @block.tensor
        def _(pe):
            def turn(t, u):
                pe.wait_ge(s_in, t + 1)
                wait(pe, s_z, t - 1)
                for k in range(2):
                    r = nc.tensor.transpose(bank[u % 2][:, k * NP_:(k + 1) * NP_], zr[:, u, k * P:(k + 1) * P],
                                            c.ident[0:NP_, 0:NP_])
                r.then_inc(s_tp, 1)

            each_node_tile(pe, turn)
            pe.wait_ge(s_z, NT)
            pe.wait_ge(s_w, 7 * 16)
            for i, (n, w) in enumerate(SIX):
                wait(pe, s_lgt, i - 1)
                for k in range(2):
                    r = nc.tensor.matmul(bank[2 + i % 2][0:NE, 0:w], wr[:, k, :], z4t[:, k, n:n + w],
                                         start=k == 0, stop=k == 1)
                r.then_inc(s_lg, 1)
            pe.wait_ge(s_lgt, len(SIX))
            for t in range(NT):
                r = nc.tensor.transpose(bank[4][0:NP_, t * NE:(t + 1) * NE], lgt[:, t * NP_:(t + 1) * NP_],
                                        c.ident[0:NE, 0:NE])
            r.then_inc(s_back, 1)
            pe.wait_ge(s_wf, 1)
            for i, (n, w) in enumerate(SIX):
                wait(pe, s_wt, i - 1)
                for t in range(n // NP_, (n + w) // NP_):
                    r = nc.tensor.transpose(bank[5 + i % 2][0:NE, t * NP_ - n:(t + 1) * NP_ - n], wfull[:, t, :],
                                            c.ident[0:NP_, 0:NP_])
                r.then_inc(s_wtp, 1)
            pe.wait_ge(s_wt, len(SIX))
            for t in range(NT):
                wait(pe, s_add, t - 3)
                nc.tensor.matmul(bank[t % 4][0:NP_, 0:D], wt[:, t * NP_:(t + 1) * NP_], b2[:, :],
                                 start=True, stop=True).then_inc(s_b2, 1)


def experts(c, z4t, wfull):
    nc, a, bank = c.nc, c.a, c.bank
    KD, KH = D // P, FH // P
    with ExitStack() as ctx:
        c.stage = ctx

        def sb(name, shape, dt=F32):
            return c.sb(name, shape, dt, ctx)

        w1 = sb("ex_w1", [P, 2, KD, FH])
        w2 = sb("ex_w2", [P, 2, KH, D])
        b1 = sb("ex_b1", [P, 2, KH])
        h = sb("ex_h", [P, 2, KH, MG * NP_])
        s_w = [c.sem(f"ex_s_w{s}") for s in range(2)]
        s_h = c.sem("ex_s_h")
        s_gelu = c.sem("ex_s_gelu")
        s_y = c.sem("ex_s_y")
        s_add = c.sem("ex_s_add")
        s_out = c.sem("ex_s_out")
        block = ctx.enter_context(nc.Block())
        n_groups = len(GROUPS)

        def each_expert(engine, body):
            body(0, 0)
            body(1, 1)
            with engine.Fori(1, NE // 2) as i:
                body(i * 2, 0)
                body(i * 2 + 1, 1)

        @block.sync
        def _(sp):
            def load(e, s):
                wait(sp, s_y, (e - 1) * NT)
                sp.dma_start(b1[:, s, :], a["L1_ffn_b1t"][:, bass.ds(e * KH, KH)]).then_inc(s_w[s], 16)
                sp.dma_start(w1[:, s, :, :], a["L1_ffn_W1"][bass.ds(e * D, D), :].rearrange("(k p) f -> p k f", p=P))\
                  .then_inc(s_w[s], 16)
                sp.dma_start(w2[:, s, :, :], a["L1_ffn_W2"][bass.ds(e * FH, FH), :].rearrange("(k p) f -> p k f", p=P))\
                  .then_inc(s_w[s], 16)

            each_expert(sp, load)
            sp.wait_ge(s_add, NE * NT)
            sp.dma_start(rows(c.out), c.x[:, :, :]).then_inc(s_out, 16)
            sp.wait_ge(s_out, 16)

        @block.scalar
        def _(act):
            def expert(e, s):
                act.wait_ge(s_w[s], e * 24 + 48 - s * 24)
                for i, (t, n) in enumerate(GROUPS):
                    g_ = e * n_groups + i
                    wait(act, s_y, e * NT + (t - MG if i else -1))
                    for k in range(KH):
                        q = g_ * KH + k
                        act.wait_ge(s_h, q + 1)
                        nc.scalar.activation(h[:, (i + s) % 2, k, 0:n * NP_], bank[k][:, 0:n * NP_], ACT.Gelu,
                                             bias=b1[:, s, k:k + 1])\
                          .then_inc(s_gelu, 1)

            each_expert(act, expert)

        @block.vector
        def _(dve):
            def expert(e, s):
                for t in range(NT):
                    dve.wait_ge(s_y, e * NT + t + 1)
                    wait(dve, s_add, e * NT + t - NT + 1)
                    nc.vector.scalar_tensor_tensor(
                        out=c.x[:, t, :], in0=bank[4 + t % 4][0:NP_, 0:D],
                        scalar=wfull[:, t, bass.ds(e, 1)], in1=c.x[:, t, :], op0=ALU.mult, op1=ALU.add)\
                      .then_inc(s_add, 1)

            each_expert(dve, expert)

        @block.tensor
        def _(pe):
            mm = nc.tensor.matmul

            def hidden(e, s, i):
                t, n = GROUPS[i]
                for k in range(KH):
                    wait(pe, s_gelu, (e * n_groups + i - 1) * KH + k + 1)
                    for j in range(KD):
                        r = mm(bank[k][:, 0:n * NP_], w1[:, s, j, k * P:k * P + P], z4t[:, j, t * NP_:(t + n) * NP_],
                               start=j == 0, stop=j == KD - 1)
                    r.then_inc(s_h, 1)

            def output(e, s, i):
                t0, n = GROUPS[i]
                pe.wait_ge(s_gelu, (e * n_groups + i + 1) * KH)
                for t in range(t0, t0 + n):
                    back = 4 if t >= 4 else (1 if t == 0 else 4)
                    wait(pe, s_add, e * NT + t - back + 1)
                    for k in range(KH):
                        r = mm(bank[4 + t % 4][0:NP_, 0:D], h[:, (i + s) % 2, k, (t - t0) * NP_:(t - t0 + 1) * NP_],
                               w2[:, s, k, :], start=k == 0, stop=k == KH - 1)
                    r.then_inc(s_y, 1)

            def expert(e, s):
                pe.wait_ge(s_w[s], e * 24 + 48 - s * 24)
                hidden(e, s, 0)
                for i in range(n_groups):
                    if i + 1 < n_groups:
                        hidden(e, s, i + 1)
                    output(e, s, i)

            each_expert(pe, expert)


def build(nc, args, out):
    with ExitStack() as ctx:
        c = Core(nc, ctx, args, out)
        sort_and_first_norm(c)
        c.deg = c.sb("deg", [NP_, NT])
        with ExitStack() as graph:
            c.rec = c.sb("rec", [P, ST, RF], F32, graph)
            acc = c.sb("acc0", [NP_, NT + 1, D + 1], F32, graph)
            first_edges(c, acc)
            combine_first(c, acc)
        with ExitStack() as slices:
            swt = c.sb("swt", [P, 4, N], F32, slices)
            tokens = c.sb("tokens", [P, 4, D + 1], F32, slices)
            pw = c.sb("pw", [P, 4, D], F32, slices)
            slice_weights(c, swt, tokens)
            slice_attention(c, tokens, pw)
            slices_back(c, swt, pw)
        c.clear_stages()
        with ExitStack() as mix:
            qk = c.sb("qk", [NP_, NT, 2 * D], F32, mix)
            v1 = c.sb("v1", [NP_, NT, H0, HC + 1], F32, mix)
            second_inputs(c, qk, v1)
            second_mix(c, qk, v1)
            mix_out(c, qk)
        with ExitStack() as graph:
            c.rec = c.sb("rec2", [P, ST, RF], F32, graph)
            acc = c.sb("acc1", [NP_, NT + 1, AG], F32, graph)
            second_edges(c, acc)
            second_nodes(c, acc)
        with ExitStack() as ffn:
            z4t = c.sb("z4t", [P, 2, N], F32, ffn)
            wfull = c.sb("wfull", [NP_, NT, NE], F32, ffn)
            route(c, z4t, wfull)
            experts(c, z4t, wfull)


def kernel(**inputs):
    import concourse.bacc as bacc
    from concourse.bass_utils import run_bass_kernel_spmd

    def cols(v):
        n = (ET - 1) * P
        return (np.ascontiguousarray(np.swapaxes(v[:n].reshape((ET - 1, P) + v.shape[1:]), 0, 1)),
                np.ascontiguousarray(v[n:]))

    given = {k: np.asarray(v) for k, v in inputs.items()}
    rec = np.concatenate([given["edge_weight"][:, None], given["edge_attr_4"],
                          np.zeros((E, 2), np.float32), np.ones((E, 1), np.float32), given["edge_attr_8"]], axis=1)
    arrays = {"x": given["x"]}
    arrays["L0_ffn_wxt"] = np.concatenate([given["L0_ffn_W_x"].T, given["L0_ffn_b_x"][:, None]], axis=1)
    arrays["L1_ffn_W1"] = given["L1_ffn_W1"].reshape(NE * D, FH)
    arrays["L1_ffn_W2"] = given["L1_ffn_W2"].reshape(NE * FH, D)
    arrays["L1_ffn_b1t"] = np.ascontiguousarray(given["L1_ffn_b1"].reshape(NE, FH // P, P).transpose(2, 0, 1)).reshape(P, -1)
    arrays["L1_mix_wqkvt"] = np.ascontiguousarray(given["L1_mix_Wqkv"].T)
    arrays["L1_mix_wprojt"] = np.ascontiguousarray(given["L1_mix_Wproj"].T)
    arrays["L1_mix_temperature"] = given["L1_mix_temperature"].reshape(H0)
    arrays["L0_ffn_temperature"] = given["L0_ffn_temperature"].reshape(H0)
    for name in ("L0_gnn_filters", "L0_ffn_W_slice", "L0_ffn_b_slice", "L0_ffn_W_fx", "L0_ffn_b_fx", "L0_ffn_W_q",
                 "L0_ffn_W_k", "L0_ffn_W_v", "L0_ffn_W_out", "L0_ffn_b_out", "L1_gnn_w1_s", "L1_gnn_w1_v",
                 "L1_gnn_fc_w1", "L1_gnn_fc_w2", "L1_gnn_fc_w3", "L1_gnn_w2_s", "L1_gnn_w2_v", "L1_gnn_g_s",
                 "L1_gnn_g_v", "L1_ffn_gamma", "L1_ffn_beta", "L1_ffn_Wr", "L1_ffn_br", "L1_ffn_b2", "L1_gnn_wsc_s", "L1_gnn_wsc_v", "L1_mix_bqkv", "L1_mix_bproj"):
        arrays[name] = given[name]
    for name in ("kln_weight", "kln_bias", "vln_weight", "vln_bias"):
        arrays["L0_mix_" + name] = given["L0_mix_" + name].reshape(D)
    arrays["rec_cols"], arrays["rec_rest"] = cols(rec)
    arrays["src_cols"], arrays["src_rest"] = cols(given["src"])
    arrays["dst_cols"], arrays["dst_rest"] = cols(given["dst"])
    arrays["src_rest"] = arrays["src_rest"][:, None]
    arrays["dst_rest"] = arrays["dst_rest"][:, None]
    nc = bacc.Bacc("TRN2", target_bir_lowering=False, num_devices=1)
    args = {k: nc.dram_tensor("in_" + k, v.shape, mybir.dt.from_np(v.dtype), kind="ExternalInput").ap()
            for k, v in arrays.items()}
    out = nc.dram_tensor("out", (N, D), F32, kind="ExternalOutput").ap()
    build(nc, args, out)
    r = run_bass_kernel_spmd(nc, [{"in_" + k: v for k, v in arrays.items()}], core_ids=[0])
    return r.results[0]["out"]
```
